# Optimizing a Trainium2 kernel written in Bass

```python
import numpy as np
import jax
import jax.numpy as jnp

def _softmax(x, axis=-1):
    return jax.nn.softmax(x, axis=axis)

def _gelu(x):
    return jax.nn.gelu(x, approximate=True)

def _silu(x):
    return jax.nn.silu(x)

def _sigmoid(x):
    return jax.nn.sigmoid(x)

def _layernorm(x, axis=-1, eps=1e-05):
    m = jnp.mean(x, axis=axis, keepdims=True)
    v = jnp.var(x, axis=axis, keepdims=True)
    return (x - m) / jnp.sqrt(v + eps)

def _scatter_add(tgt, idx, src, axis=0):
    return tgt.at[idx].add(src)

def _segment_sum(src, seg, n):
    return jax.ops.segment_sum(src, seg, n)
kernel_name = 'mk_cond_resid_d4_seqx_r4_29b3b1'

def setup_inputs(seed: int=0):
    np.random.seed(seed)
    _w = jnp.asarray

    def _rec_inputs():
        import jax
        import jax.numpy as jnp
        _rk = jax.random.key(seed)
        x = 7.22e-05 + 1 * jax.random.normal(jax.random.fold_in(_rk, 1), (4, 512, 256), jnp.float32)
        _lenS = 512 - jax.random.randint(jax.random.fold_in(_rk, 7), (4,), 0, max(1, 512 // 4) + 1, jnp.int32)
        _lenS2 = 512 - jax.random.randint(jax.random.fold_in(_rk, 8), (4,), 0, max(1, 512 // 4) + 1, jnp.int32)
        cond_64 = -0.104238 + 1.01173 * jax.random.normal(jax.random.fold_in(_rk, 11), (4, 64), jnp.float32)
        fside_16xSxS_0 = -5.72187e-05 + 0.999849 * jax.random.normal(jax.random.fold_in(_rk, 12), (16, 512, 512), jnp.float32)
        _validS = jnp.arange(512)[None, :] < _lenS[:, None]
        _validS2 = jnp.arange(512)[None, :] < _lenS2[:, None]
        _causal = jnp.tril(jnp.ones((512, 512), dtype=bool))
        mask_BxS_bk0 = jnp.logical_not(jnp.broadcast_to(_validS[:, :], (4, 512)))
        mask_BxS_bf1 = jnp.ones((4, 512), dtype=bool)
        return (x, cond_64, fside_16xSxS_0, mask_BxS_bk0, mask_BxS_bf1)
    x, cond_64, fside_16xSxS_0, mask_BxS_bk0, mask_BxS_bf1 = _rec_inputs()

    def _L0_cond_setup():
        import jax, jax.numpy as jnp
        import numpy as np
        B, S, H = (4, 512, 256)
        E = 8
        M = 128
        K = 2
        N_SHARED = 2
        SM = M * N_SHARED
        G = 64
        GE_TEMP = 1.0
        ALPHA = 0.001
        SEQ_AUX = True
        NORM_TOPK = True
        COS_TEMP = 0.78
        CONS_ALPHA = 0.01
        LEAKY_SLOPE = 0.01
        EPS_COS = 1e-08

        def _leaky(x):
            return jnp.where(x >= 0, x, LEAKY_SLOPE * x)

        def _moe_forward(hidden_states, g, wt, wg, w_gate, w_up, w_down, sw_gate, sw_up, sw_down):
            b, s, h = hidden_states.shape
            x = hidden_states.reshape(-1, h)
            T = x.shape[0]
            logits_h = x @ wt.T
            logits_g = g @ wg.T
            logits_g = jnp.repeat(logits_g, s, axis=0)
            logits = (logits_h + logits_g / GE_TEMP) / (1.0 + 1.0 / GE_TEMP)
            scores = jax.nn.softmax(logits, axis=-1)
            topk_w, topk_idx = jax.lax.top_k(scores, K)
            if K > 1 and NORM_TOPK:
                topk_w = topk_w / (topk_w.sum(-1, keepdims=True) + 1e-20)
            onehot = jax.nn.one_hot(topk_idx.reshape(b, s * K), E, dtype=jnp.float32)
            ce = onehot.sum(1) / (s * K / E)
            aux_loss = (ce * scores.reshape(b, s, E).mean(1)).sum(1).mean() * ALPHA
            gp = _leaky(jnp.einsum('th,ehm->etm', x, w_gate))
            up = jnp.einsum('th,ehm->etm', x, w_up)
            y_all = jnp.einsum('etm,emh->eth', gp * up, w_down)
            y_sel = y_all[topk_idx, jnp.arange(T)[:, None], :]
            y = (y_sel * topk_w[..., None]).sum(1).reshape(b, s, h)
            p = _leaky(hidden_states @ sw_gate) * (hidden_states @ sw_up) @ sw_down
            y = y + p
            num = jnp.sum(y * p, -1)
            den = jnp.maximum(jnp.linalg.norm(y, axis=-1), EPS_COS) * jnp.maximum(jnp.linalg.norm(p, axis=-1), EPS_COS)
            closs = CONS_ALPHA * jnp.mean(num / den / (1.0 + COS_TEMP))
            return (y, aux_loss + closs)
        key = jax.random.key(seed)
        ks = jax.random.split(key, 12)
        sh = 1.0 / np.sqrt(H)
        sm = 1.0 / np.sqrt(M)
        ssm = 1.0 / np.sqrt(SM)
        sg = 1.0 / np.sqrt(G)
        return {'hidden_states': jax.random.normal(ks[0], (B, S, H), jnp.float32), 'g': jax.random.normal(ks[1], (B, G), jnp.float32), 'wt': jax.random.uniform(ks[2], (E, H), jnp.float32, -sh, sh), 'wg': jax.random.uniform(ks[3], (E, G), jnp.float32, -sg, sg), 'w_gate': jax.random.uniform(ks[4], (E, H, M), jnp.float32, -sh, sh), 'w_up': jax.random.uniform(ks[5], (E, H, M), jnp.float32, -sh, sh), 'w_down': jax.random.uniform(ks[6], (E, M, H), jnp.float32, -sm, sm), 'sw_gate': jax.random.uniform(ks[7], (H, SM), jnp.float32, -sh, sh), 'sw_up': jax.random.uniform(ks[8], (H, SM), jnp.float32, -sh, sh), 'sw_down': jax.random.uniform(ks[9], (SM, H), jnp.float32, -ssm, ssm)}
    _L0_cond_all = _L0_cond_setup()
    _L0_cond_in = {k: v for k, v in _L0_cond_all.items() if k in ('wt', 'wg', 'w_gate', 'w_up', 'w_down', 'sw_gate', 'sw_up', 'sw_down')}
    del _L0_cond_all

    def _L1_cond_setup():
        import jax, jax.numpy as jnp
        import numpy as np
        B, N, DIM, H, DH = (2, 512, 256, 16, 64)
        INNER = H * DH
        EPS = 1e-05

        def layernorm(x, g):
            mean = jnp.mean(x, axis=-1, keepdims=True)
            var = jnp.var(x, axis=-1, keepdims=True)
            return (x - mean) * jax.lax.rsqrt(var + EPS) * g
        key = jax.random.key(seed)
        ks = jax.random.split(key, 10)
        x = jax.random.normal(ks[0], (B, N, DIM), dtype=jnp.float32)
        attn_bias = jax.random.normal(ks[1], (H, N, N), dtype=jnp.float32)
        mask = jax.random.randint(ks[2], (B, N), 0, 2).astype(bool)
        g_in = jnp.ones((DIM,), dtype=jnp.float32)
        null_attn_bias = jax.random.normal(ks[3], (H,), dtype=jnp.float32)
        null_kv = jax.random.normal(ks[4], (2, DH), dtype=jnp.float32)
        Wq = jax.random.normal(ks[5], (DIM, INNER), dtype=jnp.float32) * 0.02
        Wkv = jax.random.normal(ks[6], (DIM, 2 * DH), dtype=jnp.float32) * 0.02
        Wo = jax.random.normal(ks[7], (INNER, DIM), dtype=jnp.float32) * 0.02
        g_out = jnp.ones((DIM,), dtype=jnp.float32)
        return {'x': x, 'attn_bias': attn_bias, 'mask': mask, 'g_in': g_in, 'null_attn_bias': null_attn_bias, 'null_kv': null_kv, 'Wq': Wq, 'Wkv': Wkv, 'Wo': Wo, 'g_out': g_out}
    _L1_cond_all = _L1_cond_setup()
    _L1_cond_in = {k: v for k, v in _L1_cond_all.items() if k in ('g_in', 'null_attn_bias', 'Wq', 'Wkv', 'Wo', 'g_out')}
    del _L1_cond_all

    def _L2_cond_setup():
        import jax, jax.numpy as jnp
        import numpy as np
        DIM = 256
        HEADS = 16
        DIM_HEAD = 64
        SCALE = 8.0

        def ln(x, g, eps=1e-05):
            mean = x.mean(axis=-1, keepdims=True)
            var = ((x - mean) ** 2).mean(axis=-1, keepdims=True)
            return (x - mean) * jax.lax.rsqrt(var + eps) * g

        def l2norm(t):
            n = jnp.maximum(jnp.linalg.norm(t, axis=-1, keepdims=True), 1e-12)
            return t / n

        def rel_pos_bias(n, w0, b0, g0, w1, b1, g1, w2, b2, dtype):
            pos = jnp.arange(-n + 1, n, dtype=dtype)[:, None]
            h = jax.nn.silu(ln(pos @ w0 + b0, g0))
            h = jax.nn.silu(ln(h @ w1 + b1, g1))
            h = h @ w2 + b2
            i = jnp.arange(n)
            idx = i[:, None] - i[None, :] + n - 1
            bias = h[idx]
            return jnp.transpose(bias, (2, 0, 1))
        key = jax.random.key(seed)
        ks = jax.random.split(key, 16)
        b, n = (2, 512)
        inner = HEADS * DIM_HEAD
        s = 0.02
        return {'x': jax.random.normal(ks[0], (b, n, DIM), jnp.float32), 'mask': jnp.ones((b, n), dtype=bool), 'g_norm': jnp.ones((DIM,), jnp.float32), 'Wq': jax.random.normal(ks[1], (DIM, inner), jnp.float32) * s, 'Wkv': jax.random.normal(ks[2], (DIM, 2 * DIM_HEAD), jnp.float32) * s, 'q_scale': jnp.ones((DIM_HEAD,), jnp.float32), 'k_scale': jnp.ones((DIM_HEAD,), jnp.float32), 'null_kv': jax.random.normal(ks[3], (2, DIM_HEAD), jnp.float32), 'null_attn_bias': jax.random.normal(ks[4], (HEADS,), jnp.float32), 'w0': jax.random.normal(ks[5], (1, DIM), jnp.float32) * s, 'b0': jnp.zeros((DIM,), jnp.float32), 'g0': jnp.ones((DIM,), jnp.float32), 'w1': jax.random.normal(ks[6], (DIM, DIM), jnp.float32) * s, 'b1': jnp.zeros((DIM,), jnp.float32), 'g1': jnp.ones((DIM,), jnp.float32), 'w2': jax.random.normal(ks[7], (DIM, HEADS), jnp.float32) * s, 'b2': jnp.zeros((HEADS,), jnp.float32), 'Wout': jax.random.normal(ks[8], (inner, DIM), jnp.float32) * s, 'g_out': jnp.ones((DIM,), jnp.float32)}
    _L2_cond_all = _L2_cond_setup()
    _L2_cond_in = {k: v for k, v in _L2_cond_all.items() if k in ('g_norm', 'Wq', 'Wkv', 'q_scale', 'k_scale', 'null_attn_bias', 'w0', 'b0', 'g0', 'w1', 'b1', 'g1', 'w2', 'b2', 'Wout', 'g_out')}
    del _L2_cond_all

    def _L3_cond_setup():
        import jax, jax.numpy as jnp
        import numpy as np
        DIM = 256
        HEADS = 16
        DIM_HEAD = 64
        SCALE = 8.0

        def ln(x, g, eps=1e-05):
            mean = x.mean(axis=-1, keepdims=True)
            var = ((x - mean) ** 2).mean(axis=-1, keepdims=True)
            return (x - mean) * jax.lax.rsqrt(var + eps) * g

        def l2norm(t):
            n = jnp.maximum(jnp.linalg.norm(t, axis=-1, keepdims=True), 1e-12)
            return t / n

        def rel_pos_bias(n, w0, b0, g0, w1, b1, g1, w2, b2, dtype):
            pos = jnp.arange(-n + 1, n, dtype=dtype)[:, None]
            h = jax.nn.silu(ln(pos @ w0 + b0, g0))
            h = jax.nn.silu(ln(h @ w1 + b1, g1))
            h = h @ w2 + b2
            i = jnp.arange(n)
            idx = i[:, None] - i[None, :] + n - 1
            bias = h[idx]
            return jnp.transpose(bias, (2, 0, 1))
        key = jax.random.key(seed)
        ks = jax.random.split(key, 16)
        b, n = (2, 512)
        inner = HEADS * DIM_HEAD
        s = 0.02
        return {'x': jax.random.normal(ks[0], (b, n, DIM), jnp.float32), 'mask': jnp.ones((b, n), dtype=bool), 'g_norm': jnp.ones((DIM,), jnp.float32), 'Wq': jax.random.normal(ks[1], (DIM, inner), jnp.float32) * s, 'Wkv': jax.random.normal(ks[2], (DIM, 2 * DIM_HEAD), jnp.float32) * s, 'q_scale': jnp.ones((DIM_HEAD,), jnp.float32), 'k_scale': jnp.ones((DIM_HEAD,), jnp.float32), 'null_kv': jax.random.normal(ks[3], (2, DIM_HEAD), jnp.float32), 'null_attn_bias': jax.random.normal(ks[4], (HEADS,), jnp.float32), 'w0': jax.random.normal(ks[5], (1, DIM), jnp.float32) * s, 'b0': jnp.zeros((DIM,), jnp.float32), 'g0': jnp.ones((DIM,), jnp.float32), 'w1': jax.random.normal(ks[6], (DIM, DIM), jnp.float32) * s, 'b1': jnp.zeros((DIM,), jnp.float32), 'g1': jnp.ones((DIM,), jnp.float32), 'w2': jax.random.normal(ks[7], (DIM, HEADS), jnp.float32) * s, 'b2': jnp.zeros((HEADS,), jnp.float32), 'Wout': jax.random.normal(ks[8], (inner, DIM), jnp.float32) * s, 'g_out': jnp.ones((DIM,), jnp.float32)}
    _L3_cond_all = _L3_cond_setup()
    _L3_cond_in = {k: v for k, v in _L3_cond_all.items() if k in ('g_norm', 'Wq', 'Wkv', 'q_scale', 'k_scale', 'null_attn_bias', 'w0', 'b0', 'g0', 'w1', 'b1', 'g1', 'w2', 'b2', 'Wout', 'g_out')}
    del _L3_cond_all
    return {'x': x, 'cond_64': cond_64, 'fside_16xSxS_0': fside_16xSxS_0, 'mask_BxS_bk0': mask_BxS_bk0, 'mask_BxS_bf1': mask_BxS_bf1, 'L0_cond_wt': _L0_cond_in['wt'], 'L0_cond_wg': _L0_cond_in['wg'], 'L0_cond_w_gate': _L0_cond_in['w_gate'], 'L0_cond_w_up': _L0_cond_in['w_up'], 'L0_cond_w_down': _L0_cond_in['w_down'], 'L0_cond_sw_gate': _L0_cond_in['sw_gate'], 'L0_cond_sw_up': _L0_cond_in['sw_up'], 'L0_cond_sw_down': _L0_cond_in['sw_down'], 'L1_cond_g_in': _L1_cond_in['g_in'], 'L1_cond_null_attn_bias': _L1_cond_in['null_attn_bias'], 'L1_cond_Wq': _L1_cond_in['Wq'], 'L1_cond_Wkv': _L1_cond_in['Wkv'], 'L1_cond_Wo': _L1_cond_in['Wo'], 'L1_cond_g_out': _L1_cond_in['g_out'], 'L2_cond_g_norm': _L2_cond_in['g_norm'], 'L2_cond_Wq': _L2_cond_in['Wq'], 'L2_cond_Wkv': _L2_cond_in['Wkv'], 'L2_cond_q_scale': _L2_cond_in['q_scale'], 'L2_cond_k_scale': _L2_cond_in['k_scale'], 'L2_cond_null_attn_bias': _L2_cond_in['null_attn_bias'], 'L2_cond_w0': _L2_cond_in['w0'], 'L2_cond_b0': _L2_cond_in['b0'], 'L2_cond_g0': _L2_cond_in['g0'], 'L2_cond_w1': _L2_cond_in['w1'], 'L2_cond_b1': _L2_cond_in['b1'], 'L2_cond_g1': _L2_cond_in['g1'], 'L2_cond_w2': _L2_cond_in['w2'], 'L2_cond_b2': _L2_cond_in['b2'], 'L2_cond_Wout': _L2_cond_in['Wout'], 'L2_cond_g_out': _L2_cond_in['g_out'], 'L3_cond_g_norm': _L3_cond_in['g_norm'], 'L3_cond_Wq': _L3_cond_in['Wq'], 'L3_cond_Wkv': _L3_cond_in['Wkv'], 'L3_cond_q_scale': _L3_cond_in['q_scale'], 'L3_cond_k_scale': _L3_cond_in['k_scale'], 'L3_cond_null_attn_bias': _L3_cond_in['null_attn_bias'], 'L3_cond_w0': _L3_cond_in['w0'], 'L3_cond_b0': _L3_cond_in['b0'], 'L3_cond_g0': _L3_cond_in['g0'], 'L3_cond_w1': _L3_cond_in['w1'], 'L3_cond_b1': _L3_cond_in['b1'], 'L3_cond_g1': _L3_cond_in['g1'], 'L3_cond_w2': _L3_cond_in['w2'], 'L3_cond_b2': _L3_cond_in['b2'], 'L3_cond_Wout': _L3_cond_in['Wout'], 'L3_cond_g_out': _L3_cond_in['g_out']}

def reference(x, cond_64, fside_16xSxS_0, mask_BxS_bk0, mask_BxS_bf1, L0_cond_wt, L0_cond_wg, L0_cond_w_gate, L0_cond_w_up, L0_cond_w_down, L0_cond_sw_gate, L0_cond_sw_up, L0_cond_sw_down, L1_cond_g_in, L1_cond_null_attn_bias, L1_cond_Wq, L1_cond_Wkv, L1_cond_Wo, L1_cond_g_out, L2_cond_g_norm, L2_cond_Wq, L2_cond_Wkv, L2_cond_q_scale, L2_cond_k_scale, L2_cond_null_attn_bias, L2_cond_w0, L2_cond_b0, L2_cond_g0, L2_cond_w1, L2_cond_b1, L2_cond_g1, L2_cond_w2, L2_cond_b2, L2_cond_Wout, L2_cond_g_out, L3_cond_g_norm, L3_cond_Wq, L3_cond_Wkv, L3_cond_q_scale, L3_cond_k_scale, L3_cond_null_attn_bias, L3_cond_w0, L3_cond_b0, L3_cond_g0, L3_cond_w1, L3_cond_b1, L3_cond_g1, L3_cond_w2, L3_cond_b2, L3_cond_Wout, L3_cond_g_out):
    import jax
    import jax.numpy as jnp

    def _L0_cond_ref(hidden_states, g, wt, wg, w_gate, w_up, w_down, sw_gate, sw_up, sw_down):
        import jax, jax.numpy as jnp
        import numpy as np
        B, S, H = (4, 512, 256)
        E = 8
        M = 128
        K = 2
        N_SHARED = 2
        SM = M * N_SHARED
        G = 64
        GE_TEMP = 1.0
        ALPHA = 0.001
        SEQ_AUX = True
        NORM_TOPK = True
        COS_TEMP = 0.78
        CONS_ALPHA = 0.01
        LEAKY_SLOPE = 0.01
        EPS_COS = 1e-08

        def _leaky(x):
            return jnp.where(x >= 0, x, LEAKY_SLOPE * x)

        def _moe_forward(hidden_states, g, wt, wg, w_gate, w_up, w_down, sw_gate, sw_up, sw_down):
            b, s, h = hidden_states.shape
            x = hidden_states.reshape(-1, h)
            T = x.shape[0]
            logits_h = x @ wt.T
            logits_g = g @ wg.T
            logits_g = jnp.repeat(logits_g, s, axis=0)
            logits = (logits_h + logits_g / GE_TEMP) / (1.0 + 1.0 / GE_TEMP)
            scores = jax.nn.softmax(logits, axis=-1)
            topk_w, topk_idx = jax.lax.top_k(scores, K)
            if K > 1 and NORM_TOPK:
                topk_w = topk_w / (topk_w.sum(-1, keepdims=True) + 1e-20)
            onehot = jax.nn.one_hot(topk_idx.reshape(b, s * K), E, dtype=jnp.float32)
            ce = onehot.sum(1) / (s * K / E)
            aux_loss = (ce * scores.reshape(b, s, E).mean(1)).sum(1).mean() * ALPHA
            gp = _leaky(jnp.einsum('th,ehm->etm', x, w_gate))
            up = jnp.einsum('th,ehm->etm', x, w_up)
            y_all = jnp.einsum('etm,emh->eth', gp * up, w_down)
            y_sel = y_all[topk_idx, jnp.arange(T)[:, None], :]
            y = (y_sel * topk_w[..., None]).sum(1).reshape(b, s, h)
            p = _leaky(hidden_states @ sw_gate) * (hidden_states @ sw_up) @ sw_down
            y = y + p
            num = jnp.sum(y * p, -1)
            den = jnp.maximum(jnp.linalg.norm(y, axis=-1), EPS_COS) * jnp.maximum(jnp.linalg.norm(p, axis=-1), EPS_COS)
            closs = CONS_ALPHA * jnp.mean(num / den / (1.0 + COS_TEMP))
            return (y, aux_loss + closs)
        y, _ = _moe_forward(hidden_states, g, wt, wg, w_gate, w_up, w_down, sw_gate, sw_up, sw_down)
        return y

    def _L1_cond_ref(x, attn_bias, mask, g_in, null_attn_bias, null_kv, Wq, Wkv, Wo, g_out):
        import jax, jax.numpy as jnp
        import numpy as np
        B, N, DIM, H, DH = (2, 512, 256, 16, 64)
        INNER = H * DH
        EPS = 1e-05

        def layernorm(x, g):
            mean = jnp.mean(x, axis=-1, keepdims=True)
            var = jnp.var(x, axis=-1, keepdims=True)
            return (x - mean) * jax.lax.rsqrt(var + EPS) * g
        b, n, _ = x.shape
        scale = DH ** (-0.5)
        xn = layernorm(x, g_in)
        q = (xn @ Wq).reshape(b, n, H, DH).transpose(0, 2, 1, 3) * scale
        kv = xn @ Wkv
        k, v = (kv[..., :DH], kv[..., DH:])
        nk = jnp.broadcast_to(null_kv[0], (b, 1, DH))
        nv = jnp.broadcast_to(null_kv[1], (b, 1, DH))
        k = jnp.concatenate([nk, k], axis=1)
        v = jnp.concatenate([nv, v], axis=1)
        sim = jnp.einsum('bhid,bjd->bhij', q, k)
        null_col = jnp.broadcast_to(null_attn_bias[:, None, None], (H, n, 1))
        bias = jnp.concatenate([null_col, attn_bias], axis=-1)
        sim = sim + bias
        neg = -jnp.finfo(sim.dtype).max
        j = n + 1
        causal_mask = jnp.triu(jnp.ones((n, j), dtype=bool), k=j - n + 1)
        sim = jnp.where(causal_mask, neg, sim)
        mask_p = jnp.pad(mask, ((0, 0), (1, 0)), constant_values=True)
        sim = jnp.where(mask_p[:, None, None, :], sim, neg)
        attn = jax.nn.softmax(sim, axis=-1)
        out = jnp.einsum('bhij,bjd->bhid', attn, v)
        out = out.transpose(0, 2, 1, 3).reshape(b, n, INNER)
        out = out @ Wo
        return layernorm(out, g_out)

    def _L2_cond_ref(x, mask, g_norm, Wq, Wkv, q_scale, k_scale, null_kv, null_attn_bias, w0, b0, g0, w1, b1, g1, w2, b2, Wout, g_out):
        import jax, jax.numpy as jnp
        import numpy as np
        DIM = 256
        HEADS = 16
        DIM_HEAD = 64
        SCALE = 8.0

        def ln(x, g, eps=1e-05):
            mean = x.mean(axis=-1, keepdims=True)
            var = ((x - mean) ** 2).mean(axis=-1, keepdims=True)
            return (x - mean) * jax.lax.rsqrt(var + eps) * g

        def l2norm(t):
            n = jnp.maximum(jnp.linalg.norm(t, axis=-1, keepdims=True), 1e-12)
            return t / n

        def rel_pos_bias(n, w0, b0, g0, w1, b1, g1, w2, b2, dtype):
            pos = jnp.arange(-n + 1, n, dtype=dtype)[:, None]
            h = jax.nn.silu(ln(pos @ w0 + b0, g0))
            h = jax.nn.silu(ln(h @ w1 + b1, g1))
            h = h @ w2 + b2
            i = jnp.arange(n)
            idx = i[:, None] - i[None, :] + n - 1
            bias = h[idx]
            return jnp.transpose(bias, (2, 0, 1))
        b, n, _ = x.shape
        xn = ln(x, g_norm)
        q = (xn @ Wq).reshape(b, n, HEADS, DIM_HEAD).transpose(0, 2, 1, 3)
        kv = xn @ Wkv
        k, v = (kv[..., :DIM_HEAD], kv[..., DIM_HEAD:])
        nk = jnp.broadcast_to(null_kv[0], (b, 1, DIM_HEAD))
        nv = jnp.broadcast_to(null_kv[1], (b, 1, DIM_HEAD))
        k = jnp.concatenate([nk, k], axis=1)
        v = jnp.concatenate([nv, v], axis=1)
        q = l2norm(q) * q_scale
        k = l2norm(k) * k_scale
        sim = jnp.einsum('bhid,bjd->bhij', q, k) * SCALE
        bias = rel_pos_bias(n, w0, b0, g0, w1, b1, g1, w2, b2, q.dtype)
        null_bias = jnp.broadcast_to(null_attn_bias[:, None, None], (HEADS, n, 1))
        attn_bias = jnp.concatenate([null_bias, bias], axis=-1)
        sim = sim + attn_bias
        neg = -jnp.finfo(sim.dtype).max
        causal = jnp.triu(jnp.ones((n, n + 1), dtype=bool), k=2)
        sim = jnp.where(causal, neg, sim)
        m = jnp.pad(mask, ((0, 0), (1, 0)), constant_values=True)[:, None, None, :]
        sim = jnp.where(m, sim, neg)
        attn = jax.nn.softmax(sim, axis=-1)
        out = jnp.einsum('bhij,bjd->bhid', attn, v)
        out = out.transpose(0, 2, 1, 3).reshape(b, n, HEADS * DIM_HEAD)
        return ln(out @ Wout, g_out)

    def _L3_cond_ref(x, mask, g_norm, Wq, Wkv, q_scale, k_scale, null_kv, null_attn_bias, w0, b0, g0, w1, b1, g1, w2, b2, Wout, g_out):
        import jax, jax.numpy as jnp
        import numpy as np
        DIM = 256
        HEADS = 16
        DIM_HEAD = 64
        SCALE = 8.0

        def ln(x, g, eps=1e-05):
            mean = x.mean(axis=-1, keepdims=True)
            var = ((x - mean) ** 2).mean(axis=-1, keepdims=True)
            return (x - mean) * jax.lax.rsqrt(var + eps) * g

        def l2norm(t):
            n = jnp.maximum(jnp.linalg.norm(t, axis=-1, keepdims=True), 1e-12)
            return t / n

        def rel_pos_bias(n, w0, b0, g0, w1, b1, g1, w2, b2, dtype):
            pos = jnp.arange(-n + 1, n, dtype=dtype)[:, None]
            h = jax.nn.silu(ln(pos @ w0 + b0, g0))
            h = jax.nn.silu(ln(h @ w1 + b1, g1))
            h = h @ w2 + b2
            i = jnp.arange(n)
            idx = i[:, None] - i[None, :] + n - 1
            bias = h[idx]
            return jnp.transpose(bias, (2, 0, 1))
        b, n, _ = x.shape
        xn = ln(x, g_norm)
        q = (xn @ Wq).reshape(b, n, HEADS, DIM_HEAD).transpose(0, 2, 1, 3)
        kv = xn @ Wkv
        k, v = (kv[..., :DIM_HEAD], kv[..., DIM_HEAD:])
        nk = jnp.broadcast_to(null_kv[0], (b, 1, DIM_HEAD))
        nv = jnp.broadcast_to(null_kv[1], (b, 1, DIM_HEAD))
        k = jnp.concatenate([nk, k], axis=1)
        v = jnp.concatenate([nv, v], axis=1)
        q = l2norm(q) * q_scale
        k = l2norm(k) * k_scale
        sim = jnp.einsum('bhid,bjd->bhij', q, k) * SCALE
        bias = rel_pos_bias(n, w0, b0, g0, w1, b1, g1, w2, b2, q.dtype)
        null_bias = jnp.broadcast_to(null_attn_bias[:, None, None], (HEADS, n, 1))
        attn_bias = jnp.concatenate([null_bias, bias], axis=-1)
        sim = sim + attn_bias
        neg = -jnp.finfo(sim.dtype).max
        causal = jnp.triu(jnp.ones((n, n + 1), dtype=bool), k=2)
        sim = jnp.where(causal, neg, sim)
        m = jnp.pad(mask, ((0, 0), (1, 0)), constant_values=True)[:, None, None, :]
        sim = jnp.where(m, sim, neg)
        attn = jax.nn.softmax(sim, axis=-1)
        out = jnp.einsum('bhij,bjd->bhid', attn, v)
        out = out.transpose(0, 2, 1, 3).reshape(b, n, HEADS * DIM_HEAD)
        return ln(out @ Wout, g_out)
    x = x + _L0_cond_ref(x, cond_64, L0_cond_wt, L0_cond_wg, L0_cond_w_gate, L0_cond_w_up, L0_cond_w_down, L0_cond_sw_gate, L0_cond_sw_up, L0_cond_sw_down)
    x = x + _L1_cond_ref(x, fside_16xSxS_0, mask_BxS_bk0, L1_cond_g_in, L1_cond_null_attn_bias, cond_64, L1_cond_Wq, L1_cond_Wkv, L1_cond_Wo, L1_cond_g_out)
    x = x + _L2_cond_ref(x, mask_BxS_bf1, L2_cond_g_norm, L2_cond_Wq, L2_cond_Wkv, L2_cond_q_scale, L2_cond_k_scale, cond_64, L2_cond_null_attn_bias, L2_cond_w0, L2_cond_b0, L2_cond_g0, L2_cond_w1, L2_cond_b1, L2_cond_g1, L2_cond_w2, L2_cond_b2, L2_cond_Wout, L2_cond_g_out)
    x = x + _L3_cond_ref(x, mask_BxS_bf1, L3_cond_g_norm, L3_cond_Wq, L3_cond_Wkv, L3_cond_q_scale, L3_cond_k_scale, cond_64, L3_cond_null_attn_bias, L3_cond_w0, L3_cond_b0, L3_cond_g0, L3_cond_w1, L3_cond_b1, L3_cond_g1, L3_cond_w2, L3_cond_b2, L3_cond_Wout, L3_cond_g_out)
    return x

_drawn_inputs = setup_inputs


def setup_inputs(seed=0):
    import zlib

    import numpy as np

    out = dict(_drawn_inputs(seed))
    spreads = {'L1_cond_g_in': (1.0, 0.582),
     'L1_cond_g_out': (1.0, 0.2),
     'L2_cond_g_norm': (1.0, 0.2),
     'L2_cond_q_scale': (1.0, 0.2),
     'L2_cond_k_scale': (1.0, 0.6),
     'L2_cond_b0': (0.0, 0.8),
     'L2_cond_g0': (1.0, 0.6),
     'L2_cond_b1': (0.0, 0.8),
     'L2_cond_g1': (1.0, 0.6),
     'L2_cond_b2': (0.0, 0.8),
     'L2_cond_g_out': (1.0, 0.2),
     'L3_cond_g_norm': (1.0, 0.2),
     'L3_cond_q_scale': (1.0, 0.6),
     'L3_cond_k_scale': (1.0, 0.6),
     'L3_cond_b0': (0.0, 0.8),
     'L3_cond_g0': (1.0, 0.6),
     'L3_cond_b1': (0.0, 0.619),
     'L3_cond_g1': (1.0, 0.6),
     'L3_cond_b2': (0.0, 0.8),
     'L3_cond_g_out': (1.0, 0.2)}
    factors = {'L2_cond_w0': 6.468,
     'L2_cond_w1': 3.988,
     'L2_cond_w2': 3.144,
     'L3_cond_w0': 5.723,
     'L3_cond_w1': 5.776,
     'L3_cond_w2': 3.893}
    for name, (base, spread) in spreads.items():
        noise = np.random.default_rng([zlib.crc32(name.encode()), seed]).standard_normal(out[name].shape)
        drawn = base * np.exp(spread * noise) if base else spread * noise
        out[name] = jnp.asarray(drawn.astype(out[name].dtype))
    for name, factor in factors.items():
        out[name] = (out[name] * factor).astype(out[name].dtype)
    return out
```

```python
from contextlib import ExitStack

import concourse.bass as bass
from concourse import mybir

F32 = mybir.dt.float32
F16 = mybir.dt.float16
U32 = mybir.dt.uint32
U8 = mybir.dt.uint8
ALU = mybir.AluOpType
ACT = mybir.ActivationFunctionType
AX_X = mybir.AxisListType.X

P = 128
B, S, D = 4, 512, 256
T = B * S // P
TB = S // P
KC = D // P
H, DH = 16, 64
PAIRS = H // 2
ITEMS = PAIRS * B
E = 8
NE = 10
M = 128
G = 64
LN_EPS = 1e-5
NEG = -1e30
MASK = 65504.0
LEAKY = 0.01

WIDTH = [(t + 1) * P for t in range(TB)]
OFF = [sum(WIDTH[:t]) for t in range(TB)]
CAUSAL = sum(WIDTH)
BLOCKS = [(t, k) for t in range(TB) for k in range(t + 1)]
GROUPS = [BLOCKS[0:4], BLOCKS[4:8], BLOCKS[8:10]]

RAW_SCALE = 8.0
NORM_SCALE = 32.0


class Item:

    def __init__(self, layer, i, par, b, last=False):
        self.layer, self.i, self.par, self.b, self.last = layer, i, par, b, last

    def count(self, per_item, more=0, layer0=0):
        fixed = per_item * (ITEMS * (self.layer - layer0) + 4 * self.par + self.b) + more
        return self.i * (8 * per_item) + fixed

    def pair(self):
        return self.i * 2 + self.par

    def next(self):
        if self.b < 3:
            return Item(self.layer, self.i, self.par, self.b + 1, self.last)
        if self.par == 0:
            return Item(self.layer, self.i, 1, 0, self.last)
        return None if self.last else Item(self.layer, self.i + 1, 0, 0)


def await_(eng, sem, value):
    if isinstance(value, int) and value <= 0:
        return
    eng.wait_ge(sem, value)


def build(nc, a, out):
    bias_dram = nc.dram_tensor("bias_rows", (2, H, P, 640), F32, kind="Internal").ap()

    def bcast_rows(ap1d, n, offset=0):
        return bass.AP(tensor=ap1d.tensor, offset=ap1d.offset + offset, ap=[[0, P], [1, n]])

    with ExitStack() as ctx:
        def sb(name, shape, dt=F32):
            return ctx.enter_context(nc.sbuf_tensor(name, shape, dt))

        def sem(name):
            return ctx.enter_context(nc.semaphore(name))

        x = sb("x", [P, T, D])
        xT = sb("xT", [P, KC, T * P])
        outT = sb("outT", [P, PAIRS, T * P])
        ident = sb("ident", [P, P])
        ident16 = sb("ident16", [P, P], F16)
        consts = sb("consts", [P, 4])
        wq = [sb(f"wq{n}", [P, KC, H * DH]) for n in range(1)]
        wkv = [sb(f"wkv{n}", [P, KC, 2 * DH]) for n in range(1)]
        wo = [sb(f"wo{n}", [P, PAIRS, D]) for n in range(1)]
        gin = sb("gin", [P, 3, KC])
        gout = sb("gout", [P, D])
        kscale = sb("kscale", [P, 3, DH])
        qscale = sb("qscale", [P, 2, DH])
        nullb = sb("nullb", [P, 3, H])
        nullb_flat = nullb[:, :, :].rearrange("p a b -> p (a b)")
        nk = sb("nk", [P, DH])
        nv = sb("nv", [P, DH])
        nvT = sb("nvT", [P, 1])
        mask8 = sb("mask8", [P, 2, T], U8)
        maskv = sb("maskv", [P, 2, T])
        stats = sb("stats", [P, T, 6])
        mv = sb("mv", [P, T, 2])
        rstd = sb("rstd", [P, T])
        rtmp = sb("rtmp", [P, T])
        kh = sb("kh", [P, T * P], F16)
        kl = sb("kl", [DH + 1, T * P], F16)
        v = sb("v", [P, T, DH])
        nkT = sb("nkT", [P, 2], F16)
        bias = [sb(f"bias{n}", [P, 2, CAUSAL]) for n in range(2)]
        pr = [sb(f"pr{n}", [P, CAUSAL]) for n in range(2)]
        prT = [sb(f"prT{n}", [P, CAUSAL]) for n in range(2)]
        qsq = sb("qsq", [P, TB, 2, DH])
        qn = sb("qn", [P, TB, 2, DH])
        qs = sb("qs", [P, TB, 2, 2, DH], F16)
        qT = [sb(f"qT{n}", [P, 2, S], F16) for n in range(2)]
        qB = [sb(f"qB{n}", [DH + 1, 2, S], F16) for n in range(2)]
        qss = sb("qss", [P, 3, TB, 2])
        sn0 = sb("nullsc", [P, 2, TB, 2])
        sn = [sb(f"sn{n}", [P, TB, 2]) for n in range(2)]
        nmax = [sb(f"nmax{n}", [P, TB, 2]) for n in range(2)]
        rsum = [sb(f"rsum{n}", [P, TB, 2]) for n in range(2)]
        pn = sb("pn", [P, 4, TB, 2])
        orow = sb("orow", [P, TB, 2, DH])
        ytmp = sb("ytmp", [P, 2, D])
        over = outT[:, :, :].rearrange("p a b -> p (a b)")
        xn = over[:, 0:4096].rearrange("p (t d) -> p t d", t=T)
        ks = over[:, 4096:5120].bitcast(F16).rearrange("p (t c d) -> p t c d", t=T, c=2)
        kls = over[:, 5120:6144].bitcast(F16).rearrange("p (t c d) -> p t c d", t=T, c=2)
        ksq = over[:, 6144:6400].rearrange("p (t d) -> p t d", t=TB)
        kn = over[:, 6400:7424].rearrange("p (t d) -> p t d", t=T)
        kn2 = over[:, 7424:8448].rearrange("p (t d) -> p t d", t=T)
        kss = over[:, 8448:8496].rearrange("p (c t) -> p c t", c=3)
        nks = over[:, 8512:8640].bitcast(F16).rearrange("p (c d) -> p c d", c=2)
        nkn = over[:, 8640:8704]
        nkn2 = over[:, 8704:8768]
        nss = over[:, 8768:8772]
        wgu = [over[:, 512 * n:512 * n + 512].rearrange("p (w k m) -> p w k m", w=2, k=KC) for n in range(2)]
        wd = [over[:, 1024 + 256 * n:1280 + 256 * n] for n in range(2)]
        gcopy = [over[:, 1536 + 512 * n:2048 + 512 * n] for n in range(2)]
        gleaky = [over[:, 2560 + 512 * n:3072 + 512 * n] for n in range(2)]
        hT = [over[:, 3584 + 512 * n:4096 + 512 * n] for n in range(2)]
        wtT = over[:, 4608:4624].rearrange("p (k e) -> p k e", k=KC)
        wgT = over[0:G, 4624:4632]
        condT = over[0:G, 4640:4644]
        condb = over[0:G, 4656:5168].rearrange("p (b n) -> p b n", b=B)
        lg = over[:, 5168:5296].rearrange("p (t e) -> p t e", t=T)
        sc = over[:, 5296:5424].rearrange("p (t e) -> p t e", t=T)
        top = over[:, 5424:5552].rearrange("p (t e) -> p t e", t=T)
        topi = over[:, 5552:5680].bitcast(U32).rearrange("p (t e) -> p t e", t=T)
        eq = over[:, 5680:5808].rearrange("p (t e) -> p t e", t=T)
        r1 = over[:, 5808:5936].rearrange("p (c t) -> p c t", c=8)
        idx = over[:, 5936:5968].rearrange("p (t c) -> p t c", c=2)
        cw = over[:, 5968:6128].rearrange("p (e t) -> p e t", e=NE)
        iota8 = over[:, 6128:6136]
        ce = [over[:, 6144 + 16 * n:6160 + 16 * n] for n in range(2)]
        h0 = over[:, 6400:7424].rearrange("p (t d) -> p t d", t=TB)
        h1 = over[:, 7424:8448].rearrange("p (t d) -> p t d", t=TB)
        hTT = over[:, 8448:9472].rearrange("p (k n) -> p k n", k=KC)
        rows = over[:, 9472:10752].rearrange("p (c d) -> p c d", c=5)
        w1s = over[:, 10752:11264].rearrange("p (k d) -> p k d", k=KC)
        w2s = over[:, 11264:11296].rearrange("p (k d) -> p k d", k=KC)
        b2s = over[0:H, 11296:11297]
        pos = over[:, 11304:11308]
        brow = over[0:H, 11392:12032]

        bank = [ctx.enter_context(nc.psum_tensor(f"bank{n}", [P, 512], F32)) for n in range(8)]
        psS, psT, psO, psQ, psX = bank[0:3], bank[3:5], bank[5], bank[6], bank[7]
        psX16 = psX[:].bitcast(F16)

        x_loaded = sem("x_loaded")
        gate_loaded = sem("gate_loaded")
        small_loaded = sem("small_loaded")
        mlp_loaded = sem("mlp_loaded")
        layer_loaded = sem("layer_loaded")
        bias_scaled = sem("bias_scaled")
        bias_ready = sem("bias_ready")
        bias_rows_stored = sem("bias_rows_stored")
        stored = sem("stored")
        consts_ready = sem("consts_ready")
        dve_step = sem("dve_step")
        act_step = sem("act_step")
        pool_step = sem("pool_step")
        rsq_in = sem("rsq_in")
        rsq_out = sem("rsq_out")
        stats_ready = sem("stats_ready")
        mlp_h = sem("mlp_h")
        mlp_hT = sem("mlp_hT")
        mlp_done = sem("mlp_done")
        xn_ready = sem("xn_ready")
        xT_done = sem("xT_done")
        xT_by_act = sem("xT_by_act")
        xT_by_dve = sem("xT_by_dve")
        gate_done = sem("gate_done")
        gate_max = sem("gate_max")
        gate_exp = sem("gate_exp")
        kv_done = sem("kv_done")
        kv_squared = sem("kv_squared")
        ks_ready = sem("ks_ready")
        kT_done = sem("kT_done")
        kT_by_act = sem("kT_by_act")
        kT_by_dve = sem("kT_by_dve")
        proj_done = sem("proj_done")
        proj_added = sem("proj_added")
        gu_done = sem("gu_done")
        g_copied = sem("g_copied")
        g_leaky = sem("g_leaky")
        h_ready = sem("h_ready")
        y_done = sem("y_done")
        y_added = sem("y_added")
        ce_ready = sem("ce_ready")
        q_done = sem("q_done")
        q_squared = sem("q_squared")
        q_summed = sem("q_summed")
        q_rsqrt = sem("q_rsqrt")
        q_normed = sem("q_normed")
        q_high = sem("q_high")
        q_low = sem("q_low")
        qT_done = sem("qT_done")
        qT_copied = sem("qT_copied")
        null_done = sem("null_done")
        null_scaled = sem("null_scaled")
        null_ready = sem("null_ready")
        score_done = sem("score_done")
        score_seen = sem("score_seen")
        masked = sem("masked")
        exp_done = sem("exp_done")
        prT_done = sem("prT_done")
        prT_by_act = sem("prT_by_act")
        prT_by_dve = sem("prT_by_dve")
        av_done = sem("av_done")
        null_gap = sem("null_gap")
        null_exp = sem("null_exp")
        den_step = sem("den_step")
        o_ready = sem("o_ready")
        oT_done = sem("oT_done")
        oT_seen = sem("oT_seen")
        oT_copied = sem("oT_copied")
        pool_seen = sem("pool_seen")
        expert_loaded = [sem(f"expert_loaded{n}") for n in range(2)]
        bias_loaded = [sem(f"bias_loaded{n}") for n in range(2)]

        block = ctx.enter_context(nc.Block())

        def items(eng, layer, body):
            with eng.Fori(0, PAIRS // 2 - 1) as i:
                for par in range(2):
                    for b in range(B):
                        body(Item(layer, i, par, b))
            for par in range(2):
                for b in range(B):
                    body(Item(layer, PAIRS // 2 - 1, par, b, last=True))

        LAYERS = (
            dict(n="L1_cond", norm=False, descale=1.0 / (8 * RAW_SCALE * RAW_SCALE),
                 gin="g_in", wo="Wo"),
            dict(n="L2_cond", norm=True, descale=8 / (NORM_SCALE * NORM_SCALE),
                 gin="g_norm", wo="Wout"),
            dict(n="L3_cond", norm=True, descale=8 / (NORM_SCALE * NORM_SCALE),
                 gin="g_norm", wo="Wout"),
        )

        def arg(layer, name):
            return a[f"{LAYERS[layer]['n']}_{name}"]

        N_SMALL = 16 * (3 * 2 + 2 * 2 + 6)
        N_MLP_LOADS = 16 * 8
        N_LAYER_LOADS = 16 * 4

        def rsq(kind, layer=0, j=0):
            if kind == "mlp":
                return 2 * layer + j
            base = (4, 4 + 17, 4 + 17 + 22)[layer]
            before_out = 6 if layer else 1
            return base + {"ln": 0, "nk": 1, "k": 2 + j, "out": before_out + j}[kind]

        def mlp_loads(sp, n):
            for j, name in enumerate(("w0", "b0", "g0", "b1", "g1")):
                sp.dma_start(rows[:, j, :], bcast_rows(arg(n + 1, name), D)).then_inc(mlp_loaded, 16)
            sp.dma_start(w1s, arg(n + 1, "w1").rearrange("(k p) d -> p k d", p=P)).then_inc(mlp_loaded, 16)
            sp.dma_start(w2s, arg(n + 1, "w2").rearrange("(k p) d -> p k d", p=P)).then_inc(mlp_loaded, 16)
            sp.dma_start(b2s, arg(n + 1, "b2").rearrange("(p a) -> p a", a=1)).then_inc(mlp_loaded, 16)

        def load_expert(sp, e, par):
            for w, name in enumerate(("gate", "up")):
                sp.dma_start(wgu[par][:, w], a[name].rearrange("e d m -> (e d) m")[bass.ds(e * D, D)]
                             .rearrange("(k p) m -> p k m", k=KC)).then_inc(expert_loaded[par], 16)
            sp.dma_start(wd[par], a["down"].rearrange("e m d -> (e m) d")[bass.ds(e * M, M)]
                         ).then_inc(expert_loaded[par], 16)

        def load_layer(sp, layer):
            sp.dma_start(wq[0][:], arg(layer, "Wq").rearrange("(k p) n -> p k n", p=P)).then_inc(layer_loaded, 16)
            sp.dma_start(wkv[0][:], arg(layer, "Wkv").rearrange("(k p) n -> p k n", p=P)).then_inc(layer_loaded, 16)
            sp.dma_start(wo[0][:], arg(layer, LAYERS[layer]["wo"]).rearrange("(k p) n -> p k n", p=P)).then_inc(layer_loaded, 16)
            sp.dma_start(gout[:], bcast_rows(arg(layer, "g_out"), D)).then_inc(layer_loaded, 16)

        def load_bias(sp, layer, pair, par):
            if layer == 0:
                f = a["fside_16xSxS_0"].rearrange("h s n -> (h s) n")
                for h in range(2):
                    for t in range(TB):
                        sp.dma_start(bias[par][:, h, OFF[t]:OFF[t] + WIDTH[t]],
                                     f[bass.ds((pair * 2 + h) * S + t * P, P), 0:WIDTH[t]]).then_inc(bias_loaded[par], 16)
            else:
                if isinstance(pair, int) and pair == 0:
                    sp.wait_ge(bias_rows_stored, 16 * layer)
                for h in range(2):
                    src = bias_dram[layer - 1].rearrange("h p n -> (h p n)")[bass.ds((pair * 2 + h) * (P * 640) + P - 1, P * 639)]
                    sp.dma_start(bias[par][:, h, 0:S], src.rearrange("(p n) -> p n", p=P)[:, 0:S]).then_inc(bias_loaded[par], 16)

        def bias_count(layer, i):
            if layer == 0:
                return i * 128 + 128
            return i * 32 + 32 + 512 + 128 * (layer - 1)

        @block.sync
        def _(sp):
            xd = a["x"].rearrange("b (t p) d -> p (b t) d", p=P)
            for n in range(4):
                sp.dma_start(x[:, 4 * n:4 * n + 4, :], xd[:, 4 * n:4 * n + 4, :]).then_inc(x_loaded, 16)
            mlp_loads(sp, 0)
            c = a["cond_64"]
            for k in range(KC):
                sp.dma_start(wtT[:, k, :], a["L0_cond_wt"].rearrange("e (k p) -> k p e", p=P)[k],
                             allow_slow_non_contiguous=True).then_inc(gate_loaded, 16)
            sp.dma_start(wgT, a["L0_cond_wg"].rearrange("e p -> p e"),
                         allow_slow_non_contiguous=True).then_inc(gate_loaded, 16)
            sp.dma_start(condT, c.rearrange("b p -> p b"),
                         allow_slow_non_contiguous=True).then_inc(gate_loaded, 16)
            for n in range(2):
                load_expert(sp, n, n)
            n = 0
            for layer in range(3):
                sp.dma_start(gin[:, layer, :], arg(layer, LAYERS[layer]["gin"]).rearrange("(k p) -> p k", p=P),
                             allow_slow_non_contiguous=True).then_inc(small_loaded, 16)
                sp.dma_start(nullb[:, layer, :], bcast_rows(arg(layer, "null_attn_bias"), H)).then_inc(small_loaded, 16)
                n += 2
                if layer:
                    sp.dma_start(kscale[:, layer, :], bcast_rows(arg(layer, "k_scale"), DH)).then_inc(small_loaded, 16)
                    sp.dma_start(qscale[:, layer - 1, :], bcast_rows(arg(layer, "q_scale"), DH)).then_inc(small_loaded, 16)
                    n += 2
            sp.dma_start(nk[:], bcast_rows(c, G)).then_inc(small_loaded, 16)
            sp.dma_start(nv[:], bcast_rows(c, G, G)).then_inc(small_loaded, 16)
            for half in range(2):
                sp.dma_start(nvT[half * DH:half * DH + DH, :], c[1:2, :].rearrange("a p -> p a"),
                             allow_slow_non_contiguous=True).then_inc(small_loaded, 16)
            for j, name in enumerate(("mask_BxS_bk0", "mask_BxS_bf1")):
                sp.dma_start(mask8[:, j, :], a[name].rearrange("b (t p) -> p (b t)", p=P),
                             allow_slow_non_contiguous=True).then_inc(small_loaded, 16)
            assert 16 * (n + 6) == N_SMALL
            load_layer(sp, 0)
            for par in range(2):
                load_bias(sp, 0, par, par)
            sp.wait_ge(bias_rows_stored, 16)
            mlp_loads(sp, 1)
            with sp.Fori(1, NE // 2) as i:
                for par in range(2):
                    sp.wait_ge(y_done, i * 8 + 4 * par - 4)
                    load_expert(sp, i * 2 + par, par)
            for layer in range(3):
                if layer:
                    sp.wait_ge(proj_added, T * layer)
                    load_layer(sp, layer)
                    for par in range(2):
                        load_bias(sp, layer, par, par)
                def bias_ahead(i):
                    for par in range(2):
                        sp.wait_ge(masked, i * 64 + 8 * (ITEMS * layer + 4 * par - 4))
                        load_bias(sp, layer, i * 2 + par, par)

                with sp.Fori(1, PAIRS // 2) as i:
                    bias_ahead(i)
            od = out.rearrange("b (t p) d -> p (b t) d", p=P)
            for n in range(4):
                sp.wait_ge(proj_added, 2 * T + 4 * n + 4)
                sp.dma_start(od[:, 4 * n:4 * n + 4, :], x[:, 4 * n:4 * n + 4, :]).then_inc(stored, 16)
            sp.wait_ge(stored, 64)

        @block.gpsimd
        def _(pool):
            nc.gpsimd.memset(ident[:], 0.0).then_inc(pool_step, 1)
            nc.gpsimd.memset(consts[:, 0:1], -0.5).then_inc(pool_step, 1)
            nc.gpsimd.memset(consts[:, 1:2], 1.0 / LAYERS[0]["descale"]).then_inc(pool_step, 1)
            nc.gpsimd.iota(iota8, pattern=[[1, E]], base=0, channel_multiplier=0,
                           allow_small_or_imprecise_dtypes=True).then_inc(pool_step, 1)
            nc.gpsimd.iota(pos, pattern=[[-P, TB]], base=S - 1, channel_multiplier=-1,
                           allow_small_or_imprecise_dtypes=True).then_inc(pool_step, 1)
            nc.gpsimd.memset(kscale[:, 0, :], RAW_SCALE).then_inc(pool_step, 1)
            nc.gpsimd.memset(brow[:, S:640], NEG / LAYERS[1]["descale"]).then_inc(pool_step, 1)
            for n in range(2):
                pool.wait_ge(pool_step, 7 + n)
                nc.gpsimd.memset(qB[n][DH:DH + 1, :, :], MASK).then_inc(pool_step, 1)
            pool.wait_ge(pool_step, 9)
            nc.gpsimd.affine_select(out=ident[:], in_=ident[:], compare_op=ALU.not_equal, fill=1.0, base=0,
                                    pattern=[[-1, P]], channel_multiplier=1).then_inc(pool_step, 1)
            pool.wait_ge(pool_step, 10)
            nc.gpsimd.tensor_copy(ident16[:], ident[:]).then_inc(consts_ready, 1)
            steps = [10]

            def rsqrt(number, src, tmp, dst, mult=None, least=None):
                pool.wait_ge(rsq_in, number + 1)
                if mult is None:
                    nc.gpsimd.tensor_scalar(tmp, src, LN_EPS, None, ALU.add).then_inc(pool_step, 1)
                else:
                    nc.gpsimd.tensor_scalar(tmp, src, mult, least, ALU.mult, ALU.max).then_inc(pool_step, 1)
                steps[0] += 1
                pool.wait_ge(pool_step, steps[0])
                nc.gpsimd.tensor_tensor(dst, tmp, consts[:, 0:1].to_broadcast(list(tmp.shape)), ALU.pow
                                        ).then_inc(rsq_out, 1)

            for n in range(2):
                for j in range(2):
                    rsqrt(rsq("mlp", n, j), mv[:, 0:TB, 1], rtmp[:, 0:TB], rstd[:, 0:TB])
            for layer in range(3):
                norm = LAYERS[layer]["norm"]
                rsqrt(rsq("ln", layer), mv[:, :, 1], rtmp[:], rstd[:])
                if norm:
                    rsqrt(rsq("nk", layer), nss[:, 0:1], nss[:, 1:2], nss[:, 2:3], 1.0, 1e-24)
                    for b in range(B):
                        w = slice(TB * b, TB * b + TB)
                        rsqrt(rsq("k", layer, b), kss[:, 0, w], kss[:, 1, w], kss[:, 2, w], 1.0, 1e-24)

                def bias_part(i, par, b):
                    h, tiles = b // 2, ((0, 1, 2), (3,))[b % 2]
                    if b == 0:
                        pool.wait_ge(bias_loaded[par], bias_count(0, i))
                        nc.gpsimd.sem_inc(pool_seen, 1)
                    w = bias[par][:, h, OFF[tiles[0]]:OFF[tiles[-1]] + WIDTH[tiles[-1]]]
                    nc.gpsimd.tensor_tensor(w, w, consts[:, 1:2].to_broadcast(list(w.shape)), ALU.mult
                                            ).then_inc(bias_scaled, 1)
                    pool.wait_ge(bias_scaled, i * 8 + 4 * par + b + 1)
                    nc.gpsimd.sem_inc(pool_seen, 1)
                    for t in tiles:
                        d = bias[par][:, h, OFF[t] + t * P:OFF[t] + t * P + P]
                        nc.gpsimd.affine_select(out=d, in_=d, compare_op=ALU.is_ge, fill=NEG, base=0,
                                                pattern=[[-1, P]], channel_multiplier=1).then_inc(bias_ready, 1)

                def q_halves(it):
                    if norm:
                        pool.wait_ge(q_summed, it.count(1, 1, 1))
                        nc.gpsimd.sem_inc(pool_seen, 1)
                        nc.gpsimd.tensor_scalar(qss[:, 1], qss[:, 0], NORM_SCALE ** -2, 1e-24 * NORM_SCALE ** -2,
                                                ALU.mult, ALU.max).then_inc(q_rsqrt, 1)
                        pool.wait_ge(q_rsqrt, it.count(2, 1, 1))
                        nc.gpsimd.tensor_tensor(qss[:, 2], qss[:, 1], consts[:, 0:1].unsqueeze(2).to_broadcast([P, TB, 2]),
                                                ALU.pow).then_inc(q_rsqrt, 1)
                    pool.wait_ge(q_high, it.count(1, 1))
                    nc.gpsimd.tensor_tensor(qs[:, :, :, 1, :], qn[:], qs[:, :, :, 0, :], ALU.subtract).then_inc(q_low, 1)

                if layer == 0:
                    for b in range(4):
                        bias_part(0, 0, b)
                first = Item(layer, 0, 0, 0)
                q_halves(first)
                q_halves(first.next())

                def body(it):
                    if layer == 0 and not (it.last and it.par == 1):
                        bias_part(it.i + it.par, 1 - it.par, it.b)
                    ahead = it.next() and it.next().next()
                    if ahead:
                        q_halves(ahead)

                items(pool, layer, body)
                for t in range(T):
                    rsqrt(rsq("out", layer, t), mv[:, t, 1:2], rtmp[:, t:t + 1], rstd[:, t:t + 1])

        @block.tensor
        def _(pe):
            pe.wait_ge(consts_ready, 1)

            def transposes(n):
                for g in range(8):
                    done = 8 * n + g
                    if n == 0:
                        if g % 2 == 0:
                            pe.wait_ge(x_loaded, 16 * 4)
                    else:
                        pe.wait_ge(xn_ready, 8 * (n - 1) + g + 1)
                    await_(pe, xT_by_act, done - 1 if g >= 2 else 8 * n)
                    await_(pe, xT_by_dve, done - 1 if g >= 2 else 8 * n)
                    src = x if n == 0 else xn
                    for c in range(KC):
                        for j in range(2):
                            ins = pe.transpose(bank[2 * (g % 2) + c][:, j * P:(j + 1) * P],
                                               src[:, 2 * g + j, c * P:(c + 1) * P], ident[:])
                    ins.then_inc(xT_done, 1)

            for n in range(2):
                for stage in range(2):
                    pe.wait_ge(mlp_h, 2 * n + stage + 1)
                    for c in range(KC):
                        for t in range(TB):
                            ins = pe.transpose(bank[c][:, t * P:(t + 1) * P], h1[:, t, c * P:(c + 1) * P], ident[:])
                    ins.then_inc(mlp_done, 1)
                    pe.wait_ge(mlp_hT, 2 * n + stage + 1)
                    if stage == 0:
                        for t in range(TB):
                            for c in range(KC):
                                ins = pe.matmul(bank[2 + t // 2][:, (t % 2) * D:(t % 2 + 1) * D], hTT[:, c, t * P:(t + 1) * P],
                                                w1s[:, c, :], start=(c == 0), stop=(c == KC - 1))
                    else:
                        for c in range(KC):
                            ins = pe.matmul(bank[4][0:H, :], w2s[:, c, :], hTT[:, c, :], start=(c == 0), stop=(c == KC - 1))
                    ins.then_inc(mlp_done, 1)

            transposes(0)
            pe.wait_ge(xT_by_act, 8)
            pe.wait_ge(xT_by_dve, 8)
            pe.wait_ge(gate_loaded, 16 * 4)
            pe.wait_ge(gate_max, 1)
            for t in range(T):
                o = bank[5][:, t * E:(t + 1) * E]
                for c in range(KC):
                    pe.matmul(o, xT[:, c, t * P:(t + 1) * P], wtT[:, c, :], start=(c == 0), stop=False)
                ins = pe.matmul(o, condb[:, t // TB, :], wgT, start=False, stop=True)
            ins.then_inc(gate_done, 1)

            def gate_up(i, par, n):
                s = 4 * par + n
                if n == 0:
                    pe.wait_ge(expert_loaded[par], i * 48 + 48)
                for w in range(2):
                    for c in range(KC):
                        ins = pe.matmul(bank[2 * w + s % 2][:], wgu[par][:, w, c, :], xT[:, c, n * S:(n + 1) * S],
                                        start=(c == 0), stop=(c == KC - 1))
                ins.then_inc(gu_done, 1)

            def down(i, par, n):
                s = 4 * par + n
                pe.wait_ge(h_ready, i * 8 + s + 1)
                for t in range(TB):
                    ins = pe.matmul(bank[4 + 2 * (s % 2) + t // 2][:, (t % 2) * D:(t % 2 + 1) * D],
                                    hT[s % 2][:, t * P:(t + 1) * P], wd[par], start=True, stop=True)
                ins.then_inc(y_done, 1)

            pe.wait_ge(ce_ready, 1)
            gate_up(0, 0, 0)

            def expert_pair(i, last):
                for s in range(8):
                    if s < 7:
                        gate_up(i, (s + 1) // 4, (s + 1) % 4)
                    elif not last:
                        gate_up(i + 1, 0, 0)
                    down(i, s // 4, s % 4)

            with pe.Fori(0, NE // 2 - 1) as i:
                expert_pair(i, False)
            expert_pair(NE // 2 - 1, True)

            for layer in range(3):
                pe.wait_ge(y_added, T * NE)
                await_(pe, proj_added, T * layer)
                pe.wait_ge(layer_loaded, N_LAYER_LOADS * (layer + 1))
                transposes(layer + 1)
                for b in range(B):
                    pe.wait_ge(xT_by_act, 8 * (layer + 1) + 2 * b + 2)
                    pe.wait_ge(xT_by_dve, 8 * (layer + 1) + 2 * b + 2)
                    for t in range(TB):
                        for c in range(KC):
                            ins = pe.matmul(bank[4 + b][:, t * P:(t + 1) * P], xT[:, c, (TB * b + t) * P:(TB * b + t + 1) * P],
                                            wkv[0][:, c, :], start=(c == 0), stop=(c == KC - 1))
                    ins.then_inc(kv_done, 1)
                for half, src in enumerate((ks, kls)):
                    for g in range(2):
                        pe.wait_ge(ks_ready, 5 * layer + 2 * g + 2)
                        o16 = bank[2 * half + g][:].bitcast(F16)
                        rows_ = P if half == 0 else DH + 1
                        for j in range(8):
                            t = 8 * g + j
                            ins = pe.transpose(o16[0:rows_, j * P:(j + 1) * P],
                                               src[:, t, :, :].rearrange("p c d -> p (c d)")[:, 0:rows_], ident16[:])
                        ins.then_inc(kT_done, 1)
                pe.wait_ge(ks_ready, 5 * layer + 5)
                for j in range(2):
                    ins = pe.transpose(bank[4][:].bitcast(F16)[:, j * P:(j + 1) * P], nks[:, j, :], ident16[:])
                ins.then_inc(kT_done, 1)
                pe.wait_ge(kT_by_act, 2 * (layer + 1))
                pe.wait_ge(kT_by_dve, 3 * (layer + 1))

                def q_rows(it):
                    await_(pe, null_ready, it.count(1, -1) if False else it.count(1, 0))
                    for t in range(TB):
                        for c in range(KC):
                            ins = pe.matmul(psQ[:, t * P:(t + 1) * P], xT[:, c, (TB * it.b + t) * P:(TB * it.b + t + 1) * P],
                                            wq[0][:, c, bass.ds(it.pair() * P, P)], start=(c == 0), stop=(c == KC - 1))
                    ins.then_inc(q_done, 1)

                def q_turn(it):
                    pe.wait_ge(q_low, it.count(1, 1))
                    await_(pe, oT_copied, it.count(1, -1))
                    for h in range(2):
                        for t in range(TB):
                            ins = pe.transpose(psX16[:, (TB * h + t) * P:(TB * h + t + 1) * P],
                                               qs[:, t, h, :, :].rearrange("p c d -> p (c d)"), ident16[:])
                    ins.then_inc(qT_done, 1)

                def null_scores(it):
                    pe.wait_ge(qT_copied, it.count(2, 2))
                    for t in range(TB):
                        for h in range(2):
                            o = 2 * (2 * t + h)
                            ins = pe.matmul(psQ[:, o:o + 2], qT[it.b % 2][:, h, t * P:(t + 1) * P], nkT[:],
                                            start=True, stop=True)
                    ins.then_inc(null_done, 1)

                def score(it, h, t):
                    s = TB * h + t
                    await_(pe, masked, it.count(8, s - 2 if s >= 3 else (-1, 0, -2)[s]))
                    o, keys = psS[s % 3][:, 0:WIDTH[t]], slice(S * it.b, S * it.b + WIDTH[t])
                    pe.matmul(o, qT[it.b % 2][:, h, t * P:(t + 1) * P], kh[:, keys], start=True, stop=False)
                    pe.matmul(o, qB[it.b % 2][:, h, t * P:(t + 1) * P], kl[:, keys], start=False, stop=True
                              ).then_inc(score_done, 1)

                def turn(it, h, g):
                    q = 3 * h + g
                    pe.wait_ge(exp_done, it.count(8, TB * h + GROUPS[g][-1][0] + 1))
                    if q == 3:
                        pe.wait_ge(prT_by_dve, it.count(2, 1))
                    elif q >= 2:
                        pe.wait_ge(prT_by_act, it.count(4, {2: 1, 4: 2, 5: 3}[q]))
                    for j, (t, k) in enumerate(GROUPS[g]):
                        ins = pe.transpose(psT[q % 2][:, j * P:(j + 1) * P], pr[h][:, OFF[t] + k * P:OFF[t] + (k + 1) * P],
                                           ident[:])
                    ins.then_inc(prT_done, 1)

                def av(it, h):
                    pe.wait_ge(prT_by_act, it.count(4, 2 * h + 2))
                    pe.wait_ge(prT_by_dve, it.count(2, h + 1))
                    for t in range(TB):
                        o = (2 * t + h) * DH
                        for k in range(t + 1):
                            j = BLOCKS.index((t, k))
                            ins = pe.matmul(psO[:, o:o + DH], prT[h][:, j * P:(j + 1) * P], v[:, TB * it.b + k, :],
                                            start=(k == 0), stop=(k == t))
                    ins.then_inc(av_done, 1)

                def o_turn(it):
                    pe.wait_ge(o_ready, it.count(1, 1))
                    for t in range(TB):
                        ins = pe.transpose(psX[:, t * P:(t + 1) * P], orow[:, t, :, :].rearrange("p h d -> p (h d)"), ident[:])
                    ins.then_inc(oT_done, 1)

                first = Item(layer, 0, 0, 0)
                q_rows(first)
                q_turn(first)
                null_scores(first)
                for t in range(TB):
                    score(first, 0, t)
                q_rows(first.next())

                def body(it):
                    nxt = it.next()
                    ahead = nxt and nxt.next()
                    score(it, 1, 0)
                    turn(it, 0, 0)
                    score(it, 1, 1)
                    turn(it, 0, 1)
                    score(it, 1, 2)
                    turn(it, 0, 2)
                    score(it, 1, 3)
                    av(it, 0)
                    if nxt:
                        q_turn(nxt)
                        turn(it, 1, 0)
                        null_scores(nxt)
                        score(nxt, 0, 0)
                    else:
                        turn(it, 1, 0)
                    turn(it, 1, 1)
                    if nxt:
                        score(nxt, 0, 1)
                    turn(it, 1, 2)
                    if nxt:
                        score(nxt, 0, 2)
                    av(it, 1)
                    if nxt:
                        score(nxt, 0, 3)
                    if ahead:
                        q_rows(ahead)
                    o_turn(it)

                items(pe, layer, body)
                pe.wait_ge(oT_copied, ITEMS * (layer + 1))
                pe.wait_ge(prT_by_dve, 2 * ITEMS * (layer + 1))
                for t in range(T):
                    await_(pe, proj_added, T * layer + t - 3)
                    for k in range(PAIRS):
                        ins = pe.matmul(bank[t % 4][:, 0:D], outT[:, k, t * P:(t + 1) * P], wo[0][:, k, :],
                                        start=(k == 0), stop=(k == PAIRS - 1))
                    ins.then_inc(proj_done, 1)

        @block.scalar
        def _(act):
            act.wait_ge(consts_ready, 1)
            steps = [0]
            for n in range(2):
                for stage in range(2):
                    act.wait_ge(stats_ready, 2 * n + stage + 1)
                    nc.scalar.activation(h1[:, :, :], h0[:, :, :], ACT.Silu).then_inc(mlp_h, 1)
                act.wait_ge(mlp_done, 4 * n + 4)
                await_(act, bias_rows_stored, 16 * n)
                nc.scalar.activation(brow[:, 0:S], bank[4][0:H, :], ACT.Identity, bias=b2s,
                                     scale=1 / LAYERS[1]["descale"]).then_inc(act_step, 1)
                steps[0] += 1
                act.wait_ge(act_step, steps[0])
                act.dma_start(bias_dram[n], brow.unsqueeze(1).to_broadcast([H, P, 640])).then_inc(bias_rows_stored, 16)

            def xT_copies(n):
                for g in range(8):
                    act.wait_ge(xT_done, 8 * n + g + 1)
                    o, src = xT[:, 0, 2 * g * P:(2 * g + 2) * P], bank[2 * (g % 2)][:, 0:2 * P]
                    if n == 0:
                        nc.scalar.copy(o, src).then_inc(xT_by_act, 1)
                    else:
                        nc.scalar.activation(o, src, ACT.Copy, scale=gin[:, n - 1, 0:1]).then_inc(xT_by_act, 1)

            xT_copies(0)
            act.wait_ge(gate_max, 2)
            nc.scalar.activation(sc, lg, ACT.Exp, scale=0.5).then_inc(gate_exp, 1)

            def g_copy(i, s):
                act.wait_ge(gu_done, i * 8 + s + 1)
                await_(act, h_ready, i * 8 + s - 1)
                nc.scalar.copy(gcopy[s % 2], bank[s % 2][:]).then_inc(g_copied, 1)

            for s in range(8):
                g_copy(0, s)
            with act.Fori(1, NE // 2) as i:
                for s in range(8):
                    g_copy(i, s)

            for layer in range(3):
                norm, negd = LAYERS[layer]["norm"], -LAYERS[layer]["descale"]
                act.wait_ge(small_loaded, N_SMALL)
                act.wait_ge(bias_rows_stored, 32)
                xT_copies(layer + 1)
                if norm:
                    for b in range(B):
                        act.wait_ge(kv_done, B * layer + b + 1)
                        await_(act, rsq_in, rsq("k", layer, b - 1) + 1)
                        nc.scalar.activation(ksq, bank[4 + b][:].rearrange("p (t n) -> p t n", t=TB)[:, :, 0:DH],
                                             ACT.Square).then_inc(kv_squared, 1)
                for g in range(2):
                    act.wait_ge(kT_done, 5 * layer + g + 1)
                    nc.scalar.copy(kh[:, g * 8 * P:(g + 1) * 8 * P], bank[g][:].bitcast(F16)).then_inc(kT_by_act, 1)

                def q_square(it):
                    act.wait_ge(q_done, it.count(1, 1))
                    if norm:
                        nc.scalar.activation(qsq[:], psQ[:].rearrange("p (t h d) -> p t h d", t=TB, h=2), ACT.Square
                                             ).then_inc(q_squared, 1)
                    else:
                        await_(act, q_low, it.count(1, 0))
                        nc.scalar.activation(qn[:], psQ[:].rearrange("p (t h d) -> p t h d", t=TB, h=2), ACT.Copy,
                                             scale=RAW_SCALE).then_inc(q_normed, 1)

                def q_take_high(it):
                    if norm:
                        act.wait_ge(q_normed, it.count(1, 1))
                    else:
                        act.wait_ge(q_normed, it.count(1, 1))
                    await_(act, qT_done, it.count(1, 0))
                    nc.scalar.copy(qs[:, :, :, 0, :], qn[:]).then_inc(q_high, 1)

                def exp(it, h, t):
                    act.wait_ge(masked, it.count(8, TB * h + t + 1))
                    w = pr[h][:, OFF[t]:OFF[t] + WIDTH[t]]
                    nc.scalar.activation(w, w, ACT.Exp, bias=nmax[it.b % 2][:, t, h:h + 1], scale=-1.0,
                                         accum_out=rsum[it.b % 2][:, t, h:h + 1]).then_inc(exp_done, 1)

                def prT_copy(it, h, g):
                    act.wait_ge(prT_done, it.count(6, 3 * h + g + 1))
                    n = len(GROUPS[g]) * P
                    nc.scalar.copy(prT[h][:, 4 * g * P:4 * g * P + n], psT[(3 * h + g) % 2][:, 0:n]).then_inc(prT_by_act, 1)

                def null_weight(it):
                    act.wait_ge(null_gap, it.count(1, 1))
                    nc.scalar.activation(pn[:, 1], pn[:, 0], ACT.Exp).then_inc(null_exp, 1)

                def oT_copy(it):
                    act.wait_ge(oT_done, it.count(1, 1))
                    act.sem_inc(oT_seen, 1)
                    nc.scalar.activation(over[:, bass.ds(it.pair() * (T * P) + it.b * S, S)], psX[:], ACT.Identity,
                                         bias=nvT[:]).then_inc(oT_copied, 1)

                first = Item(layer, 0, 0, 0)
                q_square(first)
                q_take_high(first)
                for t in range(TB):
                    exp(first, 0, t)
                q_square(first.next())
                q_take_high(first.next())

                def body(it):
                    nxt = it.next()
                    ahead = nxt and nxt.next()
                    exp(it, 1, 0)
                    prT_copy(it, 0, 0)
                    exp(it, 1, 1)
                    exp(it, 1, 2)
                    prT_copy(it, 0, 2)
                    exp(it, 1, 3)
                    if nxt:
                        pass
                    prT_copy(it, 1, 0)
                    if nxt:
                        exp(nxt, 0, 0)
                    null_weight(it)
                    if nxt:
                        exp(nxt, 0, 1)
                    prT_copy(it, 1, 2)
                    if nxt:
                        exp(nxt, 0, 2)
                        exp(nxt, 0, 3)
                    if ahead:
                        q_square(ahead)
                    oT_copy(it)
                    if ahead:
                        q_take_high(ahead)

                items(act, layer, body)

        @block.vector
        def _(dve):
            vec = nc.vector
            steps = [0]

            def link(ins):
                steps[0] += 1
                ins.then_inc(dve_step, 1)
                dve.wait_ge(dve_step, steps[0])

            def layer_stats(src, n, number):
                for t in range(n):
                    link(vec.bn_stats(stats[:, t, :], src(t)))
                for t in range(n):
                    ins = vec.bn_aggr(mv[:, t, :], stats[:, t, :])
                    if t < n - 1:
                        steps[0] += 1
                        ins.then_inc(dve_step, 1)
                ins.then_inc(rsq_in, 1)
                dve.wait_ge(rsq_out, number + 1)

            for n in range(2):
                dve.wait_ge(consts_ready, 1)
                dve.wait_ge(mlp_loaded, N_MLP_LOADS * (n + 1))
                link(vec.tensor_scalar(b2s, b2s, 1 / LAYERS[1]["descale"], None, ALU.mult))
                for t in range(TB):
                    link(vec.scalar_tensor_tensor(h0[:, t, :], rows[:, 0, :], pos[:, t:t + 1], rows[:, 1, :],
                                                  ALU.mult, ALU.add))
                for stage in range(2):
                    if stage:
                        for t in range(TB):
                            link(vec.tensor_tensor(h0[:, t, :], bank[2 + t // 2][:, (t % 2) * D:(t % 2 + 1) * D],
                                                   rows[:, 3, :], ALU.add))
                    layer_stats(lambda t: h0[:, t, :], TB, rsq("mlp", n, stage))
                    for t in range(TB):
                        link(vec.tensor_scalar(h0[:, t, :], h0[:, t, :], mv[:, t, 0:1], rstd[:, t:t + 1],
                                               ALU.subtract, ALU.mult))
                    for t in range(TB):
                        ins = vec.tensor_tensor(h0[:, t, :], h0[:, t, :], rows[:, 2 + 2 * stage, :], ALU.mult)
                        if t < TB - 1:
                            steps[0] += 1
                            ins.then_inc(dve_step, 1)
                    ins.then_inc(stats_ready, 1)
                    dve.wait_ge(mlp_done, 4 * n + 2 * stage + 1)
                    for c in range(KC):
                        ins = vec.tensor_copy(hTT[:, c, :], bank[c][:])
                        if c < KC - 1:
                            steps[0] += 1
                            ins.then_inc(dve_step, 1)
                    ins.then_inc(mlp_hT, 1)
                    dve.wait_ge(mlp_done, 4 * n + 2 * stage + 2)

            def xT_copies(n):
                for g in range(8):
                    dve.wait_ge(xT_done, 8 * n + g + 1)
                    o, src = xT[:, 1, 2 * g * P:(2 * g + 2) * P], bank[2 * (g % 2) + 1][:, 0:2 * P]
                    if n == 0:
                        vec.tensor_copy(o, src).then_inc(xT_by_dve, 1)
                    else:
                        vec.tensor_scalar(o, src, gin[:, n - 1, 1:2], None, ALU.mult).then_inc(xT_by_dve, 1)

            dve.wait_ge(gate_loaded, 16 * 4)
            vec.tensor_copy(condb, condT.unsqueeze(2).to_broadcast([G, B, P])).then_inc(gate_max, 1)
            xT_copies(0)
            dve.wait_ge(gate_done, 1)
            logits = bank[5][:, 0:T * E].rearrange("p (t e) -> p t e", t=T)
            link(vec.tensor_reduce(r1[:, 0, :], logits, AX_X, ALU.max))
            vec.tensor_tensor(lg, logits, r1[:, 0, :].unsqueeze(2).to_broadcast([P, T, E]), ALU.subtract).then_inc(gate_max, 1)
            dve.wait_ge(gate_exp, 1)
            link(vec.tensor_reduce(r1[:, 1, :], sc, AX_X, ALU.add))
            link(vec.reciprocal(r1[:, 2, :], r1[:, 1, :]))
            link(vec.tensor_tensor(sc, sc, r1[:, 2, :].unsqueeze(2).to_broadcast([P, T, E]), ALU.mult))
            for t in range(T):
                link(vec.max(top[:, t, :], sc[:, t, :]))
                link(vec.max_index(topi[:, t, :], top[:, t, :], sc[:, t, :]))
            link(vec.tensor_copy(idx, topi[:, :, 0:2]))
            link(vec.tensor_tensor(r1[:, 3, :], top[:, :, 0], top[:, :, 1], ALU.add))
            link(vec.tensor_scalar(r1[:, 4, :], r1[:, 3, :], 1e-20, None, ALU.add))
            link(vec.reciprocal(r1[:, 5, :], r1[:, 4, :]))
            cwt = cw[:, 0:E, :].rearrange("p e t -> p t e")
            for j in range(2):
                link(vec.tensor_tensor(r1[:, 6 + j, :], top[:, :, j], r1[:, 5, :], ALU.mult))
                link(vec.tensor_tensor(eq, iota8.unsqueeze(1).to_broadcast([P, T, E]),
                                       idx[:, :, j].unsqueeze(2).to_broadcast([P, T, E]), ALU.is_equal))
                w = r1[:, 6 + j, :].unsqueeze(2).to_broadcast([P, T, E])
                if j == 0:
                    link(vec.tensor_tensor(cwt, eq, w, ALU.mult))
                else:
                    link(vec.tensor_tensor(eq, eq, w, ALU.mult))
                    link(vec.tensor_tensor(cwt, cwt, eq, ALU.add))
            link(vec.memset(cw[:, E:NE, :], 1.0))
            vec.tensor_copy(ce[0], cw[:, 0, :]).then_inc(ce_ready, 1)

            def hidden(i, s):
                dve.wait_ge(g_copied, i * 8 + s + 1)
                vec.scalar_tensor_tensor(gleaky[s % 2], gcopy[s % 2], LEAKY, gcopy[s % 2], ALU.mult, ALU.max
                                         ).then_inc(g_leaky, 1)
                dve.wait_ge(g_leaky, i * 8 + s + 1)
                vec.tensor_tensor(hT[s % 2], gleaky[s % 2], bank[2 + s % 2][:], ALU.mult).then_inc(h_ready, 1)

            def add_out(i, s):
                dve.wait_ge(y_done, i * 8 + s + 1)
                for t in range(TB):
                    tile = TB * (s % 4) + t
                    vec.scalar_tensor_tensor(x[:, tile, :], bank[4 + 2 * (s % 2) + t // 2][:, (t % 2) * D:(t % 2 + 1) * D],
                                             ce[s // 4][:, tile:tile + 1], x[:, tile, :], ALU.mult, ALU.add
                                             ).then_inc(y_added, 1)

            def expert_pair(i, last):
                for s in range(8):
                    if s < 7:
                        hidden(i, s + 1)
                    elif not last:
                        hidden(i + 1, 0)
                    if s == 0:
                        vec.tensor_copy(ce[1], cw_flat[:, bass.ds(i * 2 * T + T, T)]).then_inc(ce_ready, 1)
                    if s == 4:
                        dve.wait_ge(ce_ready, i * 2 + 2)
                    if s == 0:
                        dve.wait_ge(ce_ready, i * 2 + 1)
                    if s == 4:
                        dve.wait_ge(y_added, i * 32 + 16)
                        if not last:
                            vec.tensor_copy(ce[0], cw_flat[:, bass.ds(i * 2 * T + 2 * T, T)]).then_inc(ce_ready, 1)
                    add_out(i, s)
                dve.wait_ge(y_added, i * 32 + 32)

            cw_flat = over[:, 5968:6128]
            hidden(0, 0)
            with dve.Fori(0, NE // 2 - 1) as i:
                expert_pair(i, False)
            expert_pair(NE // 2 - 1, True)

            for layer in range(3):
                norm, negd = LAYERS[layer]["norm"], -LAYERS[layer]["descale"]
                dve.wait_ge(y_added, T * NE)
                dve.wait_ge(small_loaded, N_SMALL)
                await_(dve, proj_added, T * layer)
                if layer == 0:
                    for j in range(2):
                        link(vec.tensor_copy(maskv[:, j, :], mask8[:, j, :]))
                        link(vec.tensor_scalar(maskv[:, j, :], maskv[:, j, :], 1.0, MASK, ALU.subtract, ALU.mult))
                    for j in range(2):
                        link(vec.tensor_tensor(kscale[:, j + 1, :], kscale[:, j + 1, :], qscale[:, j, :], ALU.mult))
                        link(vec.tensor_scalar(kscale[:, j + 1, :], kscale[:, j + 1, :], NORM_SCALE, None, ALU.mult))
                        link(vec.tensor_scalar(nullb[:, j + 1, :], nullb[:, j + 1, :], 1.0, None, ALU.mult))
                layer_stats(lambda t: x[:, t, :], T, rsq("ln", layer))
                for t in range(T):
                    ins = vec.tensor_scalar(xn[:, t, :], x[:, t, :], mv[:, t, 0:1], rstd[:, t:t + 1], ALU.subtract, ALU.mult)
                    if t % 2:
                        ins.then_inc(xn_ready, 1)
                    else:
                        steps[0] += 1
                        ins.then_inc(dve_step, 1)
                xT_copies(layer + 1)

                def halves(hi, lo, src, dup):
                    link(vec.tensor_copy(hi, dup))
                    return vec.tensor_tensor(lo, src, hi[:, :, 0, :] if len(hi.shape) == 4 else hi[:, 0:DH], ALU.subtract)

                if norm:
                    link(vec.tensor_tensor(nkn, nk[:], nk[:], ALU.mult))
                    vec.tensor_reduce(nss[:, 0:1], nkn, AX_X, ALU.add).then_inc(rsq_in, 1)
                    dve.wait_ge(rsq_out, rsq("nk", layer) + 1)
                    link(vec.tensor_scalar(nkn, nk[:], nss[:, 2:3], None, ALU.mult))
                else:
                    link(vec.tensor_copy(nkn, nk[:]))
                link(vec.tensor_tensor(nkn2, nkn, kscale[:, layer, :], ALU.mult))
                link(vec.tensor_copy(nks[:, 0, :].rearrange("p (c d) -> p c d", c=2), nkn2.unsqueeze(1).to_broadcast([P, 2, DH])))
                link(vec.tensor_tensor(nks[:, 1, 0:DH], nkn2, nks[:, 0, 0:DH], ALU.subtract))
                link(vec.tensor_copy(nks[:, 1, DH:P], nks[:, 1, 0:DH]))

                for b in range(B):
                    dve.wait_ge(kv_done, B * layer + b + 1)
                    w = slice(TB * b, TB * b + TB)
                    kv = bank[4 + b][:].rearrange("p (t c d) -> p t c d", t=TB, c=2)
                    if norm:
                        dve.wait_ge(kv_squared, B * (layer - 1) + b + 1)
                        vec.tensor_reduce(kss[:, 0, w], ksq, AX_X, ALU.add).then_inc(rsq_in, 1)
                        dve.wait_ge(rsq_out, rsq("k", layer, b) + 1)
                        link(vec.tensor_tensor(kn[:, w, :], kv[:, :, 0, :], kss[:, 2, w].unsqueeze(2).to_broadcast([P, TB, DH]),
                                               ALU.mult))
                        link(vec.tensor_tensor(kn2[:, w, :], kn[:, w, :], kscale[:, layer, :].unsqueeze(1).to_broadcast([P, TB, DH]),
                                               ALU.mult))
                    else:
                        link(vec.tensor_tensor(kn2[:, w, :], kv[:, :, 0, :], kscale[:, layer, :].unsqueeze(1).to_broadcast([P, TB, DH]),
                                               ALU.mult))
                    for c in range(2):
                        link(vec.tensor_copy(ks[:, w, c, :], kn2[:, w, :]))
                    link(vec.tensor_tensor(v[:, w, :], kv[:, :, 1, :], nv[:].unsqueeze(1).to_broadcast([P, TB, DH]), ALU.subtract))
                    link(vec.tensor_copy(kls[:, w, 1, 0:1], maskv[:, 0 if layer == 0 else 1, w].unsqueeze(2)))
                    vec.tensor_tensor(kls[:, w, 0, :], kn2[:, w, :], ks[:, w, 0, :], ALU.subtract).then_inc(ks_ready, 1)
                dve.nop()
                link(vec.tensor_copy(nkn, nkn2))
                vec.tensor_copy(nkn, nkn2).then_inc(ks_ready, 1)
                for g in range(2):
                    dve.wait_ge(kT_done, 5 * layer + 3 + g)
                    vec.tensor_copy(kl[:, g * 8 * P:(g + 1) * 8 * P], bank[2 + g][:].bitcast(F16)[0:DH + 1, :]).then_inc(kT_by_dve, 1)
                dve.wait_ge(kT_done, 5 * layer + 5)
                vec.tensor_copy(nkT[:], bank[4][:].bitcast(F16)[:, 0:2 * P].rearrange("p (c n) -> p c n", c=2)[:, :, 0]
                                ).then_inc(kT_by_dve, 1)

                def q_sum(it):
                    if norm:
                        dve.wait_ge(q_squared, it.count(1, 1, 1))
                        vec.tensor_reduce(qss[:, 0], qsq[:], AX_X, ALU.add).then_inc(q_summed, 1)

                def q_norm(it):
                    if norm:
                        dve.wait_ge(q_rsqrt, it.count(2, 2, 1))
                        vec.tensor_tensor(qn[:], psQ[:].rearrange("p (t h d) -> p t h d", t=TB, h=2),
                                          qss[:, 2].unsqueeze(3).to_broadcast([P, TB, 2, DH]), ALU.mult).then_inc(q_normed, 1)

                def qT_copy(it):
                    dve.wait_ge(qT_done, it.count(1, 1))
                    vec.tensor_copy(qT[it.b % 2][:].rearrange("p h n -> p (h n)"), psX16).then_inc(qT_copied, 1)
                    vec.tensor_copy(qB[it.b % 2][0:DH].rearrange("p h n -> p (h n)"), psX16[0:DH]).then_inc(qT_copied, 1)

                def null_score(it):
                    dve.wait_ge(null_done, it.count(1, 1))
                    vec.tensor_reduce(sn0[:, 0], psQ[:, 0:4 * TB].rearrange("p (t h c) -> p t h c", t=TB, h=2), AX_X, ALU.add
                                      ).then_inc(null_ready, 1)
                    dve.wait_ge(null_ready, it.count(1, 1))
                    vec.tensor_scalar(sn0[:, 1], sn0[:, 0], negd, None, ALU.mult).then_inc(null_scaled, 1)
                    dve.wait_ge(null_scaled, it.count(2, 1))
                    vec.tensor_tensor(sn[it.b % 2][:], sn0[:, 1],
                                      nullb_flat[:, bass.ds(it.pair() * 2 + H * layer, 2)].unsqueeze(1).to_broadcast([P, TB, 2]),
                                      ALU.subtract).then_inc(null_scaled, 1)

                def mask_tile(it, h, t):
                    if it.b == 0 and h == 0 and t == 0:
                        if layer == 0:
                            dve.wait_ge(bias_ready, it.i * 16 + 8 * it.par + 8)
                        else:
                            dve.wait_ge(bias_loaded[it.par], bias_count(layer, it.i))
                        dve.sem_inc(score_seen, 1)
                    if t == 0:
                        v0 = it.count(6, -3)
                        if h == 0 and not (isinstance(v0, int) and v0 <= 0):
                            dve.wait_ge(prT_done, v0)
                            dve.sem_inc(score_seen, 1)
                        dve.wait_ge(null_scaled, it.count(2, 2))
                        dve.sem_inc(score_seen, 1)
                    dve.wait_ge(score_done, it.count(8, TB * h + t + 1))
                    dve.sem_inc(score_seen, 1)
                    n = WIDTH[t]
                    bt = bias[it.par][:, h, OFF[t]:OFF[t] + n] if layer == 0 else bias[it.par][:, h, S - n:S]
                    vec.tensor_tensor_reduce(pr[h][:, OFF[t]:OFF[t] + n], psS[(TB * h + t) % 3][:, 0:n], bt, negd,
                                             sn[it.b % 2][:, t, h:h + 1], ALU.add, ALU.min,
                                             nmax[it.b % 2][:, t, h:h + 1]).then_inc(masked, 1)

                def prT_copy(it, h):
                    dve.wait_ge(prT_done, it.count(6, 3 * h + 2))
                    vec.tensor_copy(prT[h][:, 4 * P:8 * P], psT[(3 * h + 1) % 2][:]).then_inc(prT_by_dve, 1)

                def null_part(it):
                    dve.wait_ge(masked, it.count(8, 8))
                    vec.tensor_tensor(pn[:, 0], nmax[it.b % 2][:], sn[it.b % 2][:], ALU.subtract).then_inc(null_gap, 1)

                def denominators(it):
                    dve.wait_ge(null_exp, it.count(1, 1))
                    vec.tensor_tensor(pn[:, 2], rsum[it.b % 2][:], pn[:, 1], ALU.add).then_inc(den_step, 1)
                    dve.wait_ge(den_step, it.count(2, 1))
                    vec.reciprocal(pn[:, 3], pn[:, 2]).then_inc(den_step, 1)

                def o_rows(it):
                    dve.wait_ge(av_done, it.count(2, 2))
                    dve.wait_ge(den_step, it.count(2, 2))
                    vec.tensor_tensor(orow[:], psO[:].rearrange("p (t h d) -> p t h d", t=TB, h=2),
                                      pn[:, 3].unsqueeze(3).to_broadcast([P, TB, 2, DH]), ALU.mult).then_inc(o_ready, 1)

                first = Item(layer, 0, 0, 0)
                q_sum(first)
                q_norm(first)
                qT_copy(first)
                null_score(first)
                for t in range(TB):
                    mask_tile(first, 0, t)
                q_sum(first.next())

                def body(it):
                    nxt = it.next()
                    ahead = nxt and nxt.next()
                    if nxt:
                        if not (isinstance(it.i, int) and it.i == 0 and it.par == 0 and it.b == 0):
                            pass
                        q_norm(nxt)
                    mask_tile(it, 1, 0)
                    mask_tile(it, 1, 1)
                    prT_copy(it, 0)
                    mask_tile(it, 1, 2)
                    mask_tile(it, 1, 3)
                    null_part(it)
                    if nxt:
                        qT_copy(nxt)
                        null_score(nxt)
                        mask_tile(nxt, 0, 0)
                    prT_copy(it, 1)
                    if nxt:
                        mask_tile(nxt, 0, 1)
                    denominators(it)
                    if nxt:
                        mask_tile(nxt, 0, 2)
                    o_rows(it)
                    if nxt:
                        mask_tile(nxt, 0, 3)
                    if ahead:
                        q_sum(ahead)

                items(dve, layer, body)
                for t in range(T):
                    y = bank[t % 4][:, 0:D]
                    dve.wait_ge(proj_done, T * layer + t + 1)
                    link(vec.bn_stats(stats[:, t, :], y))
                    vec.bn_aggr(mv[:, t, :], stats[:, t, :]).then_inc(rsq_in, 1)
                    dve.wait_ge(rsq_in, rsq("out", layer, t) + 1)
                    link(vec.scalar_tensor_tensor(ytmp[:, t % 2, :], y, mv[:, t, 0:1], gout[:], ALU.subtract, ALU.mult))
                    dve.wait_ge(rsq_out, rsq("out", layer, t) + 1)
                    vec.scalar_tensor_tensor(x[:, t, :], ytmp[:, t % 2, :], rstd[:, t:t + 1], x[:, t, :], ALU.mult, ALU.add
                                             ).then_inc(proj_added, 1)


_ATTN = ("null_attn_bias", "Wq", "Wkv", "g_out")
_NORMED = ("g_norm", "q_scale", "k_scale", "w0", "b0", "g0", "w1", "b1", "g1", "w2", "b2", "Wout")
_INS = (["x", "cond_64", "fside_16xSxS_0", "mask_BxS_bk0", "mask_BxS_bf1", "L0_cond_wt", "L0_cond_wg"]
        + [f"L1_cond_{n}" for n in (*_ATTN, "g_in", "Wo")]
        + [f"L{k}_cond_{n}" for k in (2, 3) for n in (*_ATTN, *_NORMED)])


def kernel(**inputs):
    import numpy as _np
    import concourse.bacc as _bacc
    from concourse import mybir as _mybir
    from concourse.bass_utils import run_bass_kernel_spmd as _run

    nc = _bacc.Bacc("TRN2", target_bir_lowering=False, num_devices=1)
    host = {n: _np.ascontiguousarray(inputs[n]) for n in _INS}

    def experts(own, shared, axis):
        halves = _np.split(_np.asarray(inputs[shared]), 2, axis=axis)
        return _np.concatenate([_np.asarray(inputs[own]), _np.stack(halves)])

    host["gate"] = experts("L0_cond_w_gate", "L0_cond_sw_gate", 1)
    host["up"] = experts("L0_cond_w_up", "L0_cond_sw_up", 1)
    host["down"] = experts("L0_cond_w_down", "L0_cond_sw_down", 0)
    arrays, args = {}, {}
    for name, value in host.items():
        arrays[f"in_{name}_dram"] = value
        args[name] = nc.dram_tensor(f"in_{name}_dram", value.shape, _mybir.dt.from_np(value.dtype), kind="ExternalInput").ap()
    out = nc.dram_tensor("out_0_dram", (4, 512, 256), _mybir.dt.float32, kind="ExternalOutput").ap()
    build(nc, args, out)
    r = _run(nc, [arrays], core_ids=[0])
    return r.results[0]["out_0_dram"]
```

```python
from contextlib import ExitStack

import concourse.bass as bass
from concourse import mybir

F32 = mybir.dt.float32
F16 = mybir.dt.float16
U32 = mybir.dt.uint32
U8 = mybir.dt.uint8
ALU = mybir.AluOpType
ACT = mybir.ActivationFunctionType
AX_X = mybir.AxisListType.X

P = 128
B, S, D = 4, 512, 256
T = B * S // P
TB = S // P
KC = D // P
H, DH = 16, 64
PAIRS = H // 2
ITEMS = PAIRS * B
E = 8
NE = 10
M = 128
G = 64
LN_EPS = 1e-5
NEG = -1e30
MASK = 65504.0
LEAKY = 0.01

WIDTH = [(t + 1) * P for t in range(TB)]
OFF = [sum(WIDTH[:t]) for t in range(TB)]
CAUSAL = sum(WIDTH)
BLOCKS = [(t, k) for t in range(TB) for k in range(t + 1)]
GROUPS = [BLOCKS[0:4], BLOCKS[4:8], BLOCKS[8:10]]

RAW_SCALE = 8.0
PROB_SCALE = 1024.0
VALUE_SCALE = 16.0
WEIGHT_SCALE = 64.0
NORM_SCALE = 32.0


class Item:

    def __init__(self, layer, i, par, b):
        self.layer, self.i, self.par, self.b = layer, i, par, b

    def count(self, per_item, more=0, layer0=0):
        fixed = per_item * (ITEMS * (self.layer - layer0) + 4 * self.par + self.b) + more
        return self.i * (8 * per_item) + fixed

    def pair(self):
        return self.i * 2 + self.par

    def ahead(self, n):
        turn, left = divmod(4 * self.par + self.b + n, 8)
        i = self.i + turn if turn else self.i
        if isinstance(i, int) and not 0 <= i < ITEMS // 8:
            return None
        return Item(self.layer, i, left // 4, left % 4)


def await_(eng, sem, value):
    if isinstance(value, int) and value <= 0:
        return
    eng.wait_ge(sem, value)


def build(nc, a, out):
    bias_dram = nc.dram_tensor("bias_rows", (2, H, P, 640), F32, kind="Internal").ap()

    def bcast_rows(ap1d, n, offset=0):
        return bass.AP(tensor=ap1d.tensor, offset=ap1d.offset + offset, ap=[[0, P], [1, n]])

    with ExitStack() as ctx:
        def sb(name, shape, dt=F32):
            return ctx.enter_context(nc.sbuf_tensor(name, shape, dt))

        def sem(name):
            return ctx.enter_context(nc.semaphore(name))

        x = sb("x", [P, T, D])
        xT = sb("xT", [P, KC, T * P])
        outT = sb("outT", [P, PAIRS, T * P])
        ident = sb("ident", [P, P])
        ident16 = sb("ident16", [P, P], F16)
        consts = sb("consts", [P, 4])
        wq = [sb(f"wq{n}", [P, KC, H * DH]) for n in range(1)]
        wkv = [sb(f"wkv{n}", [P, KC, 2 * DH]) for n in range(1)]
        wo = [sb(f"wo{n}", [P, PAIRS, D]) for n in range(1)]
        gin = sb("gin", [P, 3, KC])
        gout = sb("gout", [P, D])
        kscale = sb("kscale", [P, 3, DH])
        qscale = sb("qscale", [P, 2, DH])
        nullb = sb("nullb", [P, 3, H])
        nullb_flat = nullb[:, :, :].rearrange("p a b -> p (a b)")
        nk = sb("nk", [P, DH])
        nv = sb("nv", [P, DH])
        nvT = sb("nvT", [P, 1])
        mask8 = sb("mask8", [P, 2, T], U8)
        maskv = sb("maskv", [P, 2, T])
        stats = sb("stats", [P, T, 6])
        mv = sb("mv", [P, T, 2])
        rstd = sb("rstd", [P, T])
        rtmp = sb("rtmp", [P, T])
        kh = sb("kh", [P, T * P], F16)
        kl = sb("kl", [DH + 1, T * P], F16)
        vh = sb("vh", [P, T, DH], F16)
        vl = sb("vl", [P, T, DH], F16)
        nkT = sb("nkT", [P, 2], F16)
        bias = [sb(f"bias{n}", [P, 2, CAUSAL]) for n in range(2)]
        pr = [sb(f"pr{n}", [P, CAUSAL]) for n in range(2)]
        prh = [sb(f"prh{n}", [P, CAUSAL], F16) for n in range(2)]
        prl = [sb(f"prl{n}", [P, CAUSAL], F16) for n in range(2)]
        qsq = sb("qsq", [P, TB, 2, DH])
        qn = sb("qn", [P, TB, 2, DH])
        qs = sb("qs", [P, TB, 2, 2, DH], F16)
        qT = [sb(f"qT{n}", [P, 2, S], F16) for n in range(2)]
        qB = [sb(f"qB{n}", [DH + 1, 2, S], F16) for n in range(2)]
        qss = sb("qss", [P, 3, TB, 2])
        sn0 = sb("nullsc", [P, 2, TB, 2])
        sn = [sb(f"sn{n}", [P, TB, 2]) for n in range(2)]
        nmax = [sb(f"nmax{n}", [P, TB, 2]) for n in range(2)]
        rsum = [sb(f"rsum{n}", [P, TB, 2]) for n in range(2)]
        pn = sb("pn", [P, 4, TB, 2])
        orow = sb("orow", [P, TB, 2, DH])
        ytmp = sb("ytmp", [P, 2, D])
        over = outT[:, :, :].rearrange("p a b -> p (a b)")
        xn = over[:, 0:4096].rearrange("p (t d) -> p t d", t=T)
        ks = over[:, 4096:5120].bitcast(F16).rearrange("p (t c d) -> p t c d", t=T, c=2)
        kls = over[:, 5120:6144].bitcast(F16).rearrange("p (t c d) -> p t c d", t=T, c=2)
        ksq = over[:, 6144:6400].rearrange("p (t d) -> p t d", t=TB)
        kn = over[:, 6400:7424].rearrange("p (t d) -> p t d", t=T)
        kn2 = over[:, 7424:8448].rearrange("p (t d) -> p t d", t=T)
        kss = over[:, 8448:8496].rearrange("p (c t) -> p c t", c=3)
        vd = over[:, 8800:9824].rearrange("p (t d) -> p t d", t=T)
        nks = over[:, 8512:8640].bitcast(F16).rearrange("p (c d) -> p c d", c=2)
        nkn = over[:, 8640:8704]
        nkn2 = over[:, 8704:8768]
        nss = over[:, 8768:8772]
        wgu = [over[:, 512 * n:512 * n + 512].rearrange("p (w k m) -> p w k m", w=2, k=KC) for n in range(2)]
        wd = [over[:, 1024 + 256 * n:1280 + 256 * n] for n in range(2)]
        gcopy = [over[:, 1536 + 512 * n:2048 + 512 * n] for n in range(2)]
        gleaky = [over[:, 2560 + 512 * n:3072 + 512 * n] for n in range(2)]
        hT = [over[:, 3584 + 512 * n:4096 + 512 * n] for n in range(2)]
        wtT = over[:, 4608:4624].rearrange("p (k e) -> p k e", k=KC)
        wgT = over[0:G, 4624:4632]
        condT = over[0:G, 4640:4644]
        condb = over[0:G, 4656:5168].rearrange("p (b n) -> p b n", b=B)
        lg = over[:, 5168:5296].rearrange("p (t e) -> p t e", t=T)
        sc = over[:, 5296:5424].rearrange("p (t e) -> p t e", t=T)
        top = over[:, 5424:5552].rearrange("p (t e) -> p t e", t=T)
        topi = over[:, 5552:5680].bitcast(U32).rearrange("p (t e) -> p t e", t=T)
        eq = over[:, 5680:5808].rearrange("p (t e) -> p t e", t=T)
        r1 = over[:, 5808:5936].rearrange("p (c t) -> p c t", c=8)
        idx = over[:, 5936:5968].rearrange("p (t c) -> p t c", c=2)
        cw = over[:, 5968:6128].rearrange("p (e t) -> p e t", e=NE)
        iota8 = over[:, 6128:6136]
        ce = [over[:, 6144 + 16 * n:6160 + 16 * n] for n in range(2)]
        h0 = over[:, 6400:7424].rearrange("p (t d) -> p t d", t=TB)
        h1 = over[:, 7424:8448].rearrange("p (t d) -> p t d", t=TB)
        hTT = over[:, 8448:9472].rearrange("p (k n) -> p k n", k=KC)
        rows = over[:, 9472:10752].rearrange("p (c d) -> p c d", c=5)
        w1s = over[:, 10752:11264].rearrange("p (k d) -> p k d", k=KC)
        w2s = over[:, 11264:11296].rearrange("p (k d) -> p k d", k=KC)
        b2s = over[0:H, 11296:11297]
        pos = over[:, 11304:11308]
        brow = over[0:H, 11392:12032]

        bank = [ctx.enter_context(nc.psum_tensor(f"bank{n}", [P, 512], F32)) for n in range(8)]
        psS, psT, psO, psQ, psX = bank[0:3], bank[3:5], bank[5], bank[6], bank[7]
        psX16 = psX[:].bitcast(F16)

        x_loaded = sem("x_loaded")
        gate_loaded = sem("gate_loaded")
        small_loaded = sem("small_loaded")
        mlp_loaded = sem("mlp_loaded")
        layer_loaded = sem("layer_loaded")
        bias_scaled = sem("bias_scaled")
        bias_ready = sem("bias_ready")
        bias_rows_stored = sem("bias_rows_stored")
        stored = sem("stored")
        consts_ready = sem("consts_ready")
        dve_step = sem("dve_step")
        act_step = sem("act_step")
        pool_step = sem("pool_step")
        rsq_in = sem("rsq_in")
        rsq_out = sem("rsq_out")
        stats_ready = sem("stats_ready")
        mlp_h = sem("mlp_h")
        mlp_hT = sem("mlp_hT")
        mlp_done = sem("mlp_done")
        xn_ready = sem("xn_ready")
        xT_done = sem("xT_done")
        xT_by_act = sem("xT_by_act")
        xT_by_dve = sem("xT_by_dve")
        gate_done = sem("gate_done")
        gate_max = sem("gate_max")
        gate_exp = sem("gate_exp")
        kv_done = sem("kv_done")
        v_halved = sem("v_halved")
        kv_squared = sem("kv_squared")
        ks_ready = sem("ks_ready")
        kT_done = sem("kT_done")
        kT_by_act = sem("kT_by_act")
        kT_by_dve = sem("kT_by_dve")
        proj_done = sem("proj_done")
        proj_added = sem("proj_added")
        gu_done = sem("gu_done")
        g_copied = sem("g_copied")
        g_leaky = sem("g_leaky")
        h_ready = sem("h_ready")
        y_done = sem("y_done")
        y_added = sem("y_added")
        ce_ready = sem("ce_ready")
        q_done = sem("q_done")
        q_squared = sem("q_squared")
        q_summed = sem("q_summed")
        q_rsqrt = sem("q_rsqrt")
        q_normed = sem("q_normed")
        q_high = sem("q_high")
        q_low = sem("q_low")
        qT_done = sem("qT_done")
        qT_copied = sem("qT_copied")
        qB_copied = sem("qB_copied")
        null_done = sem("null_done")
        null_scaled = sem("null_scaled")
        null_ready = sem("null_ready")
        score_done = sem("score_done")
        score_seen = sem("score_seen")
        masked = sem("masked")
        exp_done = sem("exp_done")
        prT_done = sem("prT_done")
        prT_high = sem("prT_high")
        prT_low = sem("prT_low")
        av_done = sem("av_done")
        null_gap = sem("null_gap")
        null_exp = sem("null_exp")
        den_step = sem("den_step")
        o_ready = sem("o_ready")
        oT_done = sem("oT_done")
        oT_seen = sem("oT_seen")
        oT_copied = sem("oT_copied")
        pool_seen = sem("pool_seen")
        expert_loaded = [sem(f"expert_loaded{n}") for n in range(2)]
        bias_loaded = [sem(f"bias_loaded{n}") for n in range(2)]

        block = ctx.enter_context(nc.Block())

        def positions(eng, layer, body):
            def run(item):
                body(*(item.ahead(n) for n in range(-2, 3)))

            def run_number(n):
                body(*(Item(layer, (n + m) // 8, (n + m) % 8 // 4, (n + m) % 4) if 0 <= n + m < ITEMS else None
                       for m in range(-2, 3)))

            for n in range(-2, 4):
                run_number(n)
            with eng.Fori(0, ITEMS // 8 - 1) as i:
                for n in range(4, 12):
                    run(Item(layer, i, 0, 0).ahead(n))
            for n in range(ITEMS - 4, ITEMS + 2):
                run_number(n)

        LAYERS = (
            dict(n="L1_cond", norm=False, descale=1.0 / (8 * RAW_SCALE * RAW_SCALE),
                 gin="g_in", wo="Wo"),
            dict(n="L2_cond", norm=True, descale=8 / (NORM_SCALE * NORM_SCALE),
                 gin="g_norm", wo="Wout"),
            dict(n="L3_cond", norm=True, descale=8 / (NORM_SCALE * NORM_SCALE),
                 gin="g_norm", wo="Wout"),
        )

        def arg(layer, name):
            return a[f"{LAYERS[layer]['n']}_{name}"]

        N_SMALL = 16 * (3 * 2 + 2 * 2 + 6)
        N_MLP_LOADS = 16 * 8
        N_LAYER_LOADS = 16 * 4

        def rsq(kind, layer=0, j=0):
            if kind == "mlp":
                return 2 * layer + j
            base = (4, 4 + 17, 4 + 17 + 22)[layer]
            before_out = 6 if layer else 1
            return base + {"ln": 0, "nk": 1, "k": 2 + j, "out": before_out + j}[kind]

        def mlp_loads(sp, n):
            for j, name in enumerate(("w0", "b0", "g0", "b1", "g1")):
                sp.dma_start(rows[:, j, :], bcast_rows(arg(n + 1, name), D)).then_inc(mlp_loaded, 16)
            sp.dma_start(w1s, arg(n + 1, "w1").rearrange("(k p) d -> p k d", p=P)).then_inc(mlp_loaded, 16)
            sp.dma_start(w2s, arg(n + 1, "w2").rearrange("(k p) d -> p k d", p=P)).then_inc(mlp_loaded, 16)
            sp.dma_start(b2s, arg(n + 1, "b2").rearrange("(p a) -> p a", a=1)).then_inc(mlp_loaded, 16)

        def load_expert(sp, e, par):
            for w, name in enumerate(("gate", "up")):
                sp.dma_start(wgu[par][:, w], a[name].rearrange("e d m -> (e d) m")[bass.ds(e * D, D)]
                             .rearrange("(k p) m -> p k m", k=KC)).then_inc(expert_loaded[par], 16)
            sp.dma_start(wd[par], a["down"].rearrange("e m d -> (e m) d")[bass.ds(e * M, M)]
                         ).then_inc(expert_loaded[par], 16)

        def load_layer(sp, layer):
            sp.dma_start(wq[0][:], arg(layer, "Wq").rearrange("(k p) n -> p k n", p=P)).then_inc(layer_loaded, 16)
            sp.dma_start(wkv[0][:], arg(layer, "Wkv").rearrange("(k p) n -> p k n", p=P)).then_inc(layer_loaded, 16)
            sp.dma_start(wo[0][:], arg(layer, LAYERS[layer]["wo"]).rearrange("(k p) n -> p k n", p=P)).then_inc(layer_loaded, 16)
            sp.dma_start(gout[:], bcast_rows(arg(layer, "g_out"), D)).then_inc(layer_loaded, 16)

        def load_bias(sp, layer, pair, par):
            if layer == 0:
                f = a["fside_16xSxS_0"].rearrange("h s n -> (h s) n")
                for h in range(2):
                    for t in range(TB):
                        sp.dma_start(bias[par][:, h, OFF[t]:OFF[t] + WIDTH[t]],
                                     f[bass.ds((pair * 2 + h) * S + t * P, P), 0:WIDTH[t]]).then_inc(bias_loaded[par], 16)
            else:
                if isinstance(pair, int) and pair == 0:
                    sp.wait_ge(bias_rows_stored, 16 * layer)
                for h in range(2):
                    src = bias_dram[layer - 1].rearrange("h p n -> (h p n)")[bass.ds((pair * 2 + h) * (P * 640) + P - 1, P * 639)]
                    sp.dma_start(bias[par][:, h, 0:S], src.rearrange("(p n) -> p n", p=P)[:, 0:S]).then_inc(bias_loaded[par], 16)

        def bias_count(layer, i):
            if layer == 0:
                return i * 128 + 128
            return i * 32 + 32 + 512 + 128 * (layer - 1)

        @block.sync
        def _(sp):
            xd = a["x"].rearrange("b (t p) d -> p (b t) d", p=P)
            for n in range(4):
                sp.dma_start(x[:, 4 * n:4 * n + 4, :], xd[:, 4 * n:4 * n + 4, :]).then_inc(x_loaded, 16)
            mlp_loads(sp, 0)
            c = a["cond_64"]
            for k in range(KC):
                sp.dma_start(wtT[:, k, :], a["L0_cond_wt"].rearrange("e (k p) -> k p e", p=P)[k],
                             allow_slow_non_contiguous=True).then_inc(gate_loaded, 16)
            sp.dma_start(wgT, a["L0_cond_wg"].rearrange("e p -> p e"),
                         allow_slow_non_contiguous=True).then_inc(gate_loaded, 16)
            sp.dma_start(condT, c.rearrange("b p -> p b"),
                         allow_slow_non_contiguous=True).then_inc(gate_loaded, 16)
            for n in range(2):
                load_expert(sp, n, n)
            n = 0
            for layer in range(3):
                sp.dma_start(gin[:, layer, :], arg(layer, LAYERS[layer]["gin"]).rearrange("(k p) -> p k", p=P),
                             allow_slow_non_contiguous=True).then_inc(small_loaded, 16)
                sp.dma_start(nullb[:, layer, :], bcast_rows(arg(layer, "null_attn_bias"), H)).then_inc(small_loaded, 16)
                n += 2
                if layer:
                    sp.dma_start(kscale[:, layer, :], bcast_rows(arg(layer, "k_scale"), DH)).then_inc(small_loaded, 16)
                    sp.dma_start(qscale[:, layer - 1, :], bcast_rows(arg(layer, "q_scale"), DH)).then_inc(small_loaded, 16)
                    n += 2
            sp.dma_start(nk[:], bcast_rows(c, G)).then_inc(small_loaded, 16)
            sp.dma_start(nv[:], bcast_rows(c, G, G)).then_inc(small_loaded, 16)
            for half in range(2):
                sp.dma_start(nvT[half * DH:half * DH + DH, :], c[1:2, :].rearrange("a p -> p a"),
                             allow_slow_non_contiguous=True).then_inc(small_loaded, 16)
            for j, name in enumerate(("mask_BxS_bk0", "mask_BxS_bf1")):
                sp.dma_start(mask8[:, j, :], a[name].rearrange("b (t p) -> p (b t)", p=P),
                             allow_slow_non_contiguous=True).then_inc(small_loaded, 16)
            assert 16 * (n + 6) == N_SMALL
            load_layer(sp, 0)
            for par in range(2):
                load_bias(sp, 0, par, par)
            sp.wait_ge(bias_rows_stored, 16)
            mlp_loads(sp, 1)
            with sp.Fori(1, NE // 2) as i:
                for par in range(2):
                    sp.wait_ge(y_done, i * 8 + 4 * par - 4)
                    load_expert(sp, i * 2 + par, par)
            for layer in range(3):
                if layer:
                    sp.wait_ge(proj_added, T * layer)
                    load_layer(sp, layer)
                    for par in range(2):
                        load_bias(sp, layer, par, par)
                def bias_ahead(i):
                    for par in range(2):
                        sp.wait_ge(masked, i * 64 + 8 * (ITEMS * layer + 4 * par - 4))
                        load_bias(sp, layer, i * 2 + par, par)

                with sp.Fori(1, PAIRS // 2) as i:
                    bias_ahead(i)
            od = out.rearrange("b (t p) d -> p (b t) d", p=P)
            for n in range(4):
                sp.wait_ge(proj_added, 2 * T + 4 * n + 4)
                sp.dma_start(od[:, 4 * n:4 * n + 4, :], x[:, 4 * n:4 * n + 4, :]).then_inc(stored, 16)
            sp.wait_ge(stored, 64)

        @block.gpsimd
        def _(pool):
            nc.gpsimd.memset(ident[:], 0.0).then_inc(pool_step, 1)
            nc.gpsimd.memset(consts[:, 0:1], -0.5).then_inc(pool_step, 1)
            nc.gpsimd.memset(consts[:, 1:2], 1.0 / LAYERS[0]["descale"]).then_inc(pool_step, 1)
            nc.gpsimd.iota(iota8, pattern=[[1, E]], base=0, channel_multiplier=0,
                           allow_small_or_imprecise_dtypes=True).then_inc(pool_step, 1)
            nc.gpsimd.iota(pos, pattern=[[-P, TB]], base=S - 1, channel_multiplier=-1,
                           allow_small_or_imprecise_dtypes=True).then_inc(pool_step, 1)
            nc.gpsimd.memset(kscale[:, 0, :], RAW_SCALE).then_inc(pool_step, 1)
            nc.gpsimd.memset(brow[:, S:640], NEG / LAYERS[1]["descale"]).then_inc(pool_step, 1)
            for n in range(2):
                pool.wait_ge(pool_step, 7 + n)
                nc.gpsimd.memset(qB[n][DH:DH + 1, :, :], MASK).then_inc(pool_step, 1)
            pool.wait_ge(pool_step, 9)
            nc.gpsimd.affine_select(out=ident[:], in_=ident[:], compare_op=ALU.not_equal, fill=1.0, base=0,
                                    pattern=[[-1, P]], channel_multiplier=1).then_inc(pool_step, 1)
            pool.wait_ge(pool_step, 10)
            nc.gpsimd.tensor_copy(ident16[:], ident[:]).then_inc(consts_ready, 1)
            steps = [10]

            def rsqrt(number, src, tmp, dst, mult=None, least=None):
                pool.wait_ge(rsq_in, number + 1)
                if mult is None:
                    nc.gpsimd.tensor_scalar(tmp, src, LN_EPS, None, ALU.add).then_inc(pool_step, 1)
                else:
                    nc.gpsimd.tensor_scalar(tmp, src, mult, least, ALU.mult, ALU.max).then_inc(pool_step, 1)
                steps[0] += 1
                pool.wait_ge(pool_step, steps[0])
                nc.gpsimd.tensor_tensor(dst, tmp, consts[:, 0:1].to_broadcast(list(tmp.shape)), ALU.pow
                                        ).then_inc(rsq_out, 1)

            for n in range(2):
                for j in range(2):
                    rsqrt(rsq("mlp", n, j), mv[:, 0:TB, 1], rtmp[:, 0:TB], rstd[:, 0:TB])
            for layer in range(3):
                norm = LAYERS[layer]["norm"]
                rsqrt(rsq("ln", layer), mv[:, :, 1], rtmp[:], rstd[:])
                if norm:
                    rsqrt(rsq("nk", layer), nss[:, 0:1], nss[:, 1:2], nss[:, 2:3], 1.0, 1e-24)
                    for b in range(B):
                        w = slice(TB * b, TB * b + TB)
                        rsqrt(rsq("k", layer, b), kss[:, 0, w], kss[:, 1, w], kss[:, 2, w], 1.0, 1e-24)

                def bias_part(i, par, b):
                    h, tiles = b // 2, ((0, 1, 2), (3,))[b % 2]
                    if b == 0:
                        pool.wait_ge(bias_loaded[par], bias_count(0, i))
                        nc.gpsimd.sem_inc(pool_seen, 1)
                    w = bias[par][:, h, OFF[tiles[0]]:OFF[tiles[-1]] + WIDTH[tiles[-1]]]
                    nc.gpsimd.tensor_tensor(w, w, consts[:, 1:2].to_broadcast(list(w.shape)), ALU.mult
                                            ).then_inc(bias_scaled, 1)
                    pool.wait_ge(bias_scaled, i * 8 + 4 * par + b + 1)
                    nc.gpsimd.sem_inc(pool_seen, 1)
                    for t in tiles:
                        d = bias[par][:, h, OFF[t] + t * P:OFF[t] + t * P + P]
                        nc.gpsimd.affine_select(out=d, in_=d, compare_op=ALU.is_ge, fill=NEG, base=0,
                                                pattern=[[-1, P]], channel_multiplier=1).then_inc(bias_ready, 1)

                def q_rsqrt_norm(it):
                    if not it or not norm:
                        return
                    pool.wait_ge(q_summed, it.count(1, 1, 1))
                    nc.gpsimd.sem_inc(pool_seen, 1)
                    nc.gpsimd.tensor_scalar(qss[:, 1], qss[:, 0], NORM_SCALE ** -2, 1e-24 * NORM_SCALE ** -2,
                                            ALU.mult, ALU.max).then_inc(q_rsqrt, 1)
                    pool.wait_ge(q_rsqrt, it.count(2, 1, 1))
                    nc.gpsimd.tensor_tensor(qss[:, 2], qss[:, 1], consts[:, 0:1].unsqueeze(2).to_broadcast([P, TB, 2]),
                                            ALU.pow).then_inc(q_rsqrt, 1)

                def q_high_half(it):
                    if not it:
                        return
                    pool.wait_ge(q_normed, it.count(1, 1))
                    nc.gpsimd.sem_inc(pool_seen, 1)
                    await_(pool, qT_done, it.count(1, 0))
                    nc.gpsimd.sem_inc(pool_seen, 1)
                    nc.gpsimd.tensor_copy(qs[:, :, :, 0, :], qn[:]).then_inc(q_high, 1)

                def q_low_half(it):
                    if not it:
                        return
                    pool.wait_ge(q_high, it.count(1, 1))
                    nc.gpsimd.tensor_tensor(qs[:, :, :, 1, :], qn[:], qs[:, :, :, 0, :], ALU.subtract).then_inc(q_low, 1)

                def qB_copy(it):
                    if not it:
                        return
                    pool.wait_ge(qT_copied, it.count(1, 1))
                    nc.gpsimd.sem_inc(pool_seen, 1)
                    nc.gpsimd.tensor_copy(qB[it.b % 2][0:DH], qT[it.b % 2][0:DH]).then_inc(qB_copied, 1)

                if layer == 0:
                    for part in range(4):
                        bias_part(0, 0, part)

                def body(before2, before, it, after, after2):
                    q_low_half(after)
                    q_rsqrt_norm(after2)
                    qB_copy(after)
                    q_high_half(after2)
                    last_pair = it and isinstance(it.i, int) and it.pair() == PAIRS - 1
                    if layer == 0 and it and it.b in (1, 2) and not last_pair:
                        for part in (0, 1) if it.b == 1 else (2, 3):
                            bias_part(it.i + it.par, 1 - it.par, part)

                positions(pool, layer, body)
                for t in range(T):
                    rsqrt(rsq("out", layer, t), mv[:, t, 1:2], rtmp[:, t:t + 1], rstd[:, t:t + 1])

        @block.tensor
        def _(pe):
            pe.wait_ge(consts_ready, 1)

            def transposes(n):
                for g in range(8):
                    done = 8 * n + g
                    if n == 0:
                        if g % 2 == 0:
                            pe.wait_ge(x_loaded, 16 * 4)
                    else:
                        pe.wait_ge(xn_ready, 8 * (n - 1) + g + 1)
                    await_(pe, xT_by_act, done - 1 if g >= 2 else 8 * n)
                    await_(pe, xT_by_dve, done - 1 if g >= 2 else 8 * n)
                    src = x if n == 0 else xn
                    for c in range(KC):
                        for j in range(2):
                            ins = pe.transpose(bank[2 * (g % 2) + c][:, j * P:(j + 1) * P],
                                               src[:, 2 * g + j, c * P:(c + 1) * P], ident[:])
                    ins.then_inc(xT_done, 1)

            for n in range(2):
                for stage in range(2):
                    pe.wait_ge(mlp_h, 2 * n + stage + 1)
                    for c in range(KC):
                        for t in range(TB):
                            ins = pe.transpose(bank[c][:, t * P:(t + 1) * P], h1[:, t, c * P:(c + 1) * P], ident[:])
                    ins.then_inc(mlp_done, 1)
                    pe.wait_ge(mlp_hT, 2 * n + stage + 1)
                    if stage == 0:
                        for t in range(TB):
                            for c in range(KC):
                                ins = pe.matmul(bank[2 + t // 2][:, (t % 2) * D:(t % 2 + 1) * D], hTT[:, c, t * P:(t + 1) * P],
                                                w1s[:, c, :], start=(c == 0), stop=(c == KC - 1))
                    else:
                        for c in range(KC):
                            ins = pe.matmul(bank[4][0:H, :], w2s[:, c, :], hTT[:, c, :], start=(c == 0), stop=(c == KC - 1))
                    ins.then_inc(mlp_done, 1)

            transposes(0)
            pe.wait_ge(xT_by_act, 8)
            pe.wait_ge(xT_by_dve, 8)
            pe.wait_ge(gate_loaded, 16 * 4)
            pe.wait_ge(gate_max, 1)
            for t in range(T):
                o = bank[5][:, t * E:(t + 1) * E]
                for c in range(KC):
                    pe.matmul(o, xT[:, c, t * P:(t + 1) * P], wtT[:, c, :], start=(c == 0), stop=False)
                ins = pe.matmul(o, condb[:, t // TB, :], wgT, start=False, stop=True)
            ins.then_inc(gate_done, 1)

            def gate_up(i, par, n):
                s = 4 * par + n
                if n == 0:
                    pe.wait_ge(expert_loaded[par], i * 48 + 48)
                for w in range(2):
                    for c in range(KC):
                        ins = pe.matmul(bank[2 * w + s % 2][:], wgu[par][:, w, c, :], xT[:, c, n * S:(n + 1) * S],
                                        start=(c == 0), stop=(c == KC - 1))
                ins.then_inc(gu_done, 1)

            def down(i, par, n):
                s = 4 * par + n
                pe.wait_ge(h_ready, i * 8 + s + 1)
                for t in range(TB):
                    ins = pe.matmul(bank[4 + 2 * (s % 2) + t // 2][:, (t % 2) * D:(t % 2 + 1) * D],
                                    hT[s % 2][:, t * P:(t + 1) * P], wd[par], start=True, stop=True)
                ins.then_inc(y_done, 1)

            pe.wait_ge(ce_ready, 1)
            gate_up(0, 0, 0)

            def expert_pair(i, last):
                for s in range(8):
                    if s < 7:
                        gate_up(i, (s + 1) // 4, (s + 1) % 4)
                    elif not last:
                        gate_up(i + 1, 0, 0)
                    down(i, s // 4, s % 4)

            with pe.Fori(0, NE // 2 - 1) as i:
                expert_pair(i, False)
            expert_pair(NE // 2 - 1, True)

            for layer in range(3):
                pe.wait_ge(y_added, T * NE)
                await_(pe, proj_added, T * layer)
                pe.wait_ge(layer_loaded, N_LAYER_LOADS * (layer + 1))
                transposes(layer + 1)
                for b in range(B):
                    pe.wait_ge(xT_by_act, 8 * (layer + 1) + 2 * b + 2)
                    pe.wait_ge(xT_by_dve, 8 * (layer + 1) + 2 * b + 2)
                    for t in range(TB):
                        for c in range(KC):
                            ins = pe.matmul(bank[4 + b][:, t * P:(t + 1) * P], xT[:, c, (TB * b + t) * P:(TB * b + t + 1) * P],
                                            wkv[0][:, c, :], start=(c == 0), stop=(c == KC - 1))
                    ins.then_inc(kv_done, 1)
                for half, src in enumerate((ks, kls)):
                    for g in range(2):
                        pe.wait_ge(ks_ready, 5 * layer + 2 * g + 2)
                        o16 = bank[2 * half + g][:].bitcast(F16)
                        rows_ = P if half == 0 else DH + 1
                        for j in range(8):
                            t = 8 * g + j
                            ins = pe.transpose(o16[0:rows_, j * P:(j + 1) * P],
                                               src[:, t, :, :].rearrange("p c d -> p (c d)")[:, 0:rows_], ident16[:])
                        ins.then_inc(kT_done, 1)
                pe.wait_ge(ks_ready, 5 * layer + 5)
                for j in range(2):
                    ins = pe.transpose(bank[4][:].bitcast(F16)[:, j * P:(j + 1) * P], nks[:, j, :], ident16[:])
                ins.then_inc(kT_done, 1)
                pe.wait_ge(v_halved, B * (layer + 1))
                pe.wait_ge(kT_by_act, 2 * (layer + 1))
                pe.wait_ge(kT_by_dve, 3 * (layer + 1))

                def q_rows(it):
                    if not it:
                        return
                    await_(pe, null_ready, it.count(1, -1))
                    if isinstance(it.i, int) and it.ahead(-1) and not it.ahead(-2):
                        pe.wait_ge(q_normed, it.count(1, 0))
                    for t in range(TB):
                        for c in range(KC):
                            ins = pe.matmul(psQ[:, t * P:(t + 1) * P], xT[:, c, (TB * it.b + t) * P:(TB * it.b + t + 1) * P],
                                            wq[0][:, c, bass.ds(it.pair() * P, P)], start=(c == 0), stop=(c == KC - 1))
                    ins.then_inc(q_done, 1)

                def q_turn(it):
                    if not it:
                        return
                    pe.wait_ge(q_low, it.count(1, 1))
                    if it.ahead(-4):
                        pe.wait_ge(oT_copied, it.count(1, -3))
                    for h in range(2):
                        for t in range(TB):
                            ins = pe.transpose(psX16[:, (TB * h + t) * P:(TB * h + t + 1) * P],
                                               qs[:, t, h, :, :].rearrange("p c d -> p (c d)"), ident16[:])
                    ins.then_inc(qT_done, 1)

                def null_scores(it, after):
                    if not it:
                        return
                    if after:
                        pe.wait_ge(q_normed, after.count(1, 1))
                    for t in range(TB):
                        for h in range(2):
                            o = 2 * (2 * t + h)
                            ins = pe.matmul(psQ[:, o:o + 2], qT[it.b % 2][:, h, t * P:(t + 1) * P], nkT[:],
                                            start=True, stop=True)
                    ins.then_inc(null_done, 1)

                def score(it, h, t):
                    if not it:
                        return
                    s = TB * h + t
                    if s == 0:
                        pe.wait_ge(qB_copied, it.count(1, 1))
                    await_(pe, masked, it.count(8, s - 2 if s >= 3 else (-1, 0, -2)[s]))
                    o, keys = psS[s % 3][:, 0:WIDTH[t]], slice(S * it.b, S * it.b + WIDTH[t])
                    pe.matmul(o, qT[it.b % 2][:, h, t * P:(t + 1) * P], kh[:, keys], start=True, stop=False)
                    pe.matmul(o, qB[it.b % 2][:, h, t * P:(t + 1) * P], kl[:, keys], start=False, stop=True
                              ).then_inc(score_done, 1)

                def turn(it, h, g):
                    if not it:
                        return
                    q = 3 * h + g
                    pe.wait_ge(exp_done, it.count(8, TB * h + GROUPS[g][-1][0] + 1))
                    await_(pe, prT_low, it.count(6, q - 1))
                    for j, (t, k) in enumerate(GROUPS[g]):
                        ins = pe.transpose(psT[q % 2][:, j * P:(j + 1) * P], pr[h][:, OFF[t] + k * P:OFF[t] + (k + 1) * P],
                                           ident[:])
                    ins.then_inc(prT_done, 1)

                def av(it, h):
                    if not it:
                        return
                    pe.wait_ge(prT_low, it.count(6, 3 * h + 3))
                    if h == 0:
                        await_(pe, o_ready, it.count(1, 0))
                    for t in range(TB):
                        o = psO[:, (2 * t + h) * DH:(2 * t + h + 1) * DH]
                        for k in range(t + 1):
                            j = BLOCKS.index((t, k))
                            block, values = slice(j * P, (j + 1) * P), TB * it.b + k
                            pe.matmul(o, prh[h][:, block], vh[:, values, :], start=(k == 0), stop=False)
                            pe.matmul(o, prh[h][:, block], vl[:, values, :], start=False, stop=False)
                            ins = pe.matmul(o, prl[h][:, block], vh[:, values, :], start=False, stop=(k == t))
                    ins.then_inc(av_done, 1)

                def o_turn(it):
                    if not it:
                        return
                    pe.wait_ge(o_ready, it.count(1, 1))
                    if it.ahead(3):
                        pe.wait_ge(qT_copied, it.count(1, 4))
                    else:
                        pe.wait_ge(oT_copied, it.count(1, 0))
                    for t in range(TB):
                        ins = pe.transpose(psX[:, t * P:(t + 1) * P], orow[:, t, :, :].rearrange("p h d -> p (h d)"), ident[:])
                    ins.then_inc(oT_done, 1)

                def body(before2, before, it, after, after2):
                    q_rows(after2)
                    q_turn(after)
                    turn(before, 1, 1)
                    turn(before, 1, 2)
                    for t in range(3, TB):
                        score(it, 0, t)
                    score(it, 1, 0)
                    score(it, 1, 1)
                    av(before, 0)
                    o_turn(before2)
                    score(it, 1, 2)
                    score(it, 1, 3)
                    turn(it, 0, 0)
                    turn(it, 0, 1)
                    for t in range(3):
                        score(after, 0, t)
                    av(before, 1)
                    null_scores(after, after2)
                    turn(it, 0, 2)
                    turn(it, 1, 0)

                positions(pe, layer, body)
                pe.wait_ge(oT_copied, ITEMS * (layer + 1))
                pe.wait_ge(prT_low, 6 * ITEMS * (layer + 1))
                for t in range(T):
                    await_(pe, proj_added, T * layer + t - 3)
                    for k in range(PAIRS):
                        ins = pe.matmul(bank[t % 4][:, 0:D], outT[:, k, t * P:(t + 1) * P], wo[0][:, k, :],
                                        start=(k == 0), stop=(k == PAIRS - 1))
                    ins.then_inc(proj_done, 1)

        @block.scalar
        def _(act):
            act.wait_ge(consts_ready, 1)
            steps = [0]
            for n in range(2):
                for stage in range(2):
                    act.wait_ge(stats_ready, 2 * n + stage + 1)
                    nc.scalar.activation(h1[:, :, :], h0[:, :, :], ACT.Silu).then_inc(mlp_h, 1)
                act.wait_ge(mlp_done, 4 * n + 4)
                await_(act, bias_rows_stored, 16 * n)
                nc.scalar.activation(brow[:, 0:S], bank[4][0:H, :], ACT.Identity, bias=b2s,
                                     scale=1 / LAYERS[1]["descale"]).then_inc(act_step, 1)
                steps[0] += 1
                act.wait_ge(act_step, steps[0])
                act.dma_start(bias_dram[n], brow.unsqueeze(1).to_broadcast([H, P, 640])).then_inc(bias_rows_stored, 16)

            def xT_copies(n):
                for g in range(8):
                    act.wait_ge(xT_done, 8 * n + g + 1)
                    o, src = xT[:, 0, 2 * g * P:(2 * g + 2) * P], bank[2 * (g % 2)][:, 0:2 * P]
                    if n == 0:
                        nc.scalar.copy(o, src).then_inc(xT_by_act, 1)
                    else:
                        nc.scalar.activation(o, src, ACT.Copy, scale=gin[:, n - 1, 0:1]).then_inc(xT_by_act, 1)

            xT_copies(0)
            act.wait_ge(gate_max, 2)
            nc.scalar.activation(sc, lg, ACT.Exp, scale=0.5).then_inc(gate_exp, 1)

            def g_copy(i, s):
                act.wait_ge(gu_done, i * 8 + s + 1)
                await_(act, h_ready, i * 8 + s - 1)
                nc.scalar.copy(gcopy[s % 2], bank[s % 2][:]).then_inc(g_copied, 1)

            for s in range(8):
                g_copy(0, s)
            with act.Fori(1, NE // 2) as i:
                for s in range(8):
                    g_copy(i, s)

            for layer in range(3):
                norm, negd = LAYERS[layer]["norm"], -LAYERS[layer]["descale"]
                act.wait_ge(small_loaded, N_SMALL)
                act.wait_ge(bias_rows_stored, 32)
                xT_copies(layer + 1)
                if norm:
                    for b in range(B):
                        act.wait_ge(kv_done, B * layer + b + 1)
                        await_(act, rsq_in, rsq("k", layer, b - 1) + 1)
                        nc.scalar.activation(ksq, bank[4 + b][:].rearrange("p (t n) -> p t n", t=TB)[:, :, 0:DH],
                                             ACT.Square).then_inc(kv_squared, 1)
                for g in range(2):
                    act.wait_ge(kT_done, 5 * layer + g + 1)
                    nc.scalar.copy(kh[:, g * 8 * P:(g + 1) * 8 * P], bank[g][:].bitcast(F16)).then_inc(kT_by_act, 1)

                def q_square(it):
                    if not it:
                        return
                    act.wait_ge(q_done, it.count(1, 1))
                    if norm:
                        nc.scalar.activation(qsq[:], psQ[:].rearrange("p (t h d) -> p t h d", t=TB, h=2), ACT.Square
                                             ).then_inc(q_squared, 1)
                    else:
                        await_(act, q_low, it.count(1, 0))
                        act.sem_inc(oT_seen, 1)
                        nc.scalar.activation(qn[:], psQ[:].rearrange("p (t h d) -> p t h d", t=TB, h=2), ACT.Copy,
                                             scale=RAW_SCALE).then_inc(q_normed, 1)

                def qT_copy(it):
                    if not it:
                        return
                    act.wait_ge(qT_done, it.count(1, 1))
                    nc.scalar.copy(qT[it.b % 2][:].rearrange("p h n -> p (h n)"), psX16).then_inc(qT_copied, 1)

                def exp(it, h, t):
                    if not it:
                        return
                    act.wait_ge(masked, it.count(8, TB * h + t + 1))
                    w = pr[h][:, OFF[t]:OFF[t] + WIDTH[t]]
                    nc.scalar.activation(w, w, ACT.Exp, bias=nmax[it.b % 2][:, t, h:h + 1], scale=-1.0,
                                         accum_out=rsum[it.b % 2][:, t, h:h + 1]).then_inc(exp_done, 1)

                def prT_copy(it, h, g):
                    if not it:
                        return
                    act.wait_ge(prT_done, it.count(6, 3 * h + g + 1))
                    n = len(GROUPS[g]) * P
                    nc.scalar.activation(prh[h][:, 4 * g * P:4 * g * P + n], psT[(3 * h + g) % 2][:, 0:n], ACT.Copy,
                                         scale=PROB_SCALE).then_inc(prT_high, 1)

                def null_weight(it):
                    if not it:
                        return
                    act.wait_ge(null_gap, it.count(1, 1))
                    nc.scalar.activation(pn[:, 1], pn[:, 0], ACT.Exp).then_inc(null_exp, 1)

                def oT_copy(it):
                    if not it:
                        return
                    act.wait_ge(oT_done, it.count(1, 1))
                    act.sem_inc(oT_seen, 1)
                    nc.scalar.activation(over[:, bass.ds(it.pair() * (T * P) + it.b * S, S)], psX[:], ACT.Identity,
                                         bias=nvT[:], scale=1 / (PROB_SCALE * VALUE_SCALE)).then_inc(oT_copied, 1)

                def body(before2, before, it, after, after2):
                    prT_copy(before, 1, 0)
                    exp(it, 0, 0)
                    q_square(after2)
                    exp(it, 0, 1)
                    qT_copy(after)
                    prT_copy(before, 1, 1)
                    prT_copy(before, 1, 2)
                    exp(it, 0, 2)
                    exp(it, 0, 3)
                    exp(it, 1, 0)
                    oT_copy(before2)
                    prT_copy(it, 0, 0)
                    prT_copy(it, 0, 1)
                    exp(it, 1, 1)
                    exp(it, 1, 2)
                    exp(it, 1, 3)
                    prT_copy(it, 0, 2)
                    null_weight(it)

                positions(act, layer, body)

        @block.vector
        def _(dve):
            vec = nc.vector
            steps = [0]

            def link(ins):
                steps[0] += 1
                ins.then_inc(dve_step, 1)
                dve.wait_ge(dve_step, steps[0])

            def layer_stats(src, n, number):
                for t in range(n):
                    link(vec.bn_stats(stats[:, t, :], src(t)))
                for t in range(n):
                    ins = vec.bn_aggr(mv[:, t, :], stats[:, t, :])
                    if t < n - 1:
                        steps[0] += 1
                        ins.then_inc(dve_step, 1)
                ins.then_inc(rsq_in, 1)
                dve.wait_ge(rsq_out, number + 1)

            for n in range(2):
                dve.wait_ge(consts_ready, 1)
                dve.wait_ge(mlp_loaded, N_MLP_LOADS * (n + 1))
                link(vec.tensor_scalar(b2s, b2s, 1 / LAYERS[1]["descale"], None, ALU.mult))
                for t in range(TB):
                    link(vec.scalar_tensor_tensor(h0[:, t, :], rows[:, 0, :], pos[:, t:t + 1], rows[:, 1, :],
                                                  ALU.mult, ALU.add))
                for stage in range(2):
                    if stage:
                        for t in range(TB):
                            link(vec.tensor_tensor(h0[:, t, :], bank[2 + t // 2][:, (t % 2) * D:(t % 2 + 1) * D],
                                                   rows[:, 3, :], ALU.add))
                    layer_stats(lambda t: h0[:, t, :], TB, rsq("mlp", n, stage))
                    for t in range(TB):
                        link(vec.tensor_scalar(h0[:, t, :], h0[:, t, :], mv[:, t, 0:1], rstd[:, t:t + 1],
                                               ALU.subtract, ALU.mult))
                    for t in range(TB):
                        ins = vec.tensor_tensor(h0[:, t, :], h0[:, t, :], rows[:, 2 + 2 * stage, :], ALU.mult)
                        if t < TB - 1:
                            steps[0] += 1
                            ins.then_inc(dve_step, 1)
                    ins.then_inc(stats_ready, 1)
                    dve.wait_ge(mlp_done, 4 * n + 2 * stage + 1)
                    for c in range(KC):
                        ins = vec.tensor_copy(hTT[:, c, :], bank[c][:])
                        if c < KC - 1:
                            steps[0] += 1
                            ins.then_inc(dve_step, 1)
                    ins.then_inc(mlp_hT, 1)
                    dve.wait_ge(mlp_done, 4 * n + 2 * stage + 2)

            def xT_copies(n):
                for g in range(8):
                    dve.wait_ge(xT_done, 8 * n + g + 1)
                    o, src = xT[:, 1, 2 * g * P:(2 * g + 2) * P], bank[2 * (g % 2) + 1][:, 0:2 * P]
                    if n == 0:
                        vec.tensor_copy(o, src).then_inc(xT_by_dve, 1)
                    else:
                        vec.tensor_scalar(o, src, gin[:, n - 1, 1:2], None, ALU.mult).then_inc(xT_by_dve, 1)

            dve.wait_ge(gate_loaded, 16 * 4)
            vec.tensor_copy(condb, condT.unsqueeze(2).to_broadcast([G, B, P])).then_inc(gate_max, 1)
            xT_copies(0)
            dve.wait_ge(gate_done, 1)
            logits = bank[5][:, 0:T * E].rearrange("p (t e) -> p t e", t=T)
            link(vec.tensor_reduce(r1[:, 0, :], logits, AX_X, ALU.max))
            vec.tensor_tensor(lg, logits, r1[:, 0, :].unsqueeze(2).to_broadcast([P, T, E]), ALU.subtract).then_inc(gate_max, 1)
            dve.wait_ge(gate_exp, 1)
            link(vec.tensor_reduce(r1[:, 1, :], sc, AX_X, ALU.add))
            link(vec.reciprocal(r1[:, 2, :], r1[:, 1, :]))
            link(vec.tensor_tensor(sc, sc, r1[:, 2, :].unsqueeze(2).to_broadcast([P, T, E]), ALU.mult))
            for t in range(T):
                link(vec.max(top[:, t, :], sc[:, t, :]))
                link(vec.max_index(topi[:, t, :], top[:, t, :], sc[:, t, :]))
            link(vec.tensor_copy(idx, topi[:, :, 0:2]))
            link(vec.tensor_tensor(r1[:, 3, :], top[:, :, 0], top[:, :, 1], ALU.add))
            link(vec.tensor_scalar(r1[:, 4, :], r1[:, 3, :], 1e-20, None, ALU.add))
            link(vec.reciprocal(r1[:, 5, :], r1[:, 4, :]))
            cwt = cw[:, 0:E, :].rearrange("p e t -> p t e")
            for j in range(2):
                link(vec.tensor_tensor(r1[:, 6 + j, :], top[:, :, j], r1[:, 5, :], ALU.mult))
                link(vec.tensor_tensor(eq, iota8.unsqueeze(1).to_broadcast([P, T, E]),
                                       idx[:, :, j].unsqueeze(2).to_broadcast([P, T, E]), ALU.is_equal))
                w = r1[:, 6 + j, :].unsqueeze(2).to_broadcast([P, T, E])
                if j == 0:
                    link(vec.tensor_tensor(cwt, eq, w, ALU.mult))
                else:
                    link(vec.tensor_tensor(eq, eq, w, ALU.mult))
                    link(vec.tensor_tensor(cwt, cwt, eq, ALU.add))
            link(vec.memset(cw[:, E:NE, :], 1.0))
            vec.tensor_copy(ce[0], cw[:, 0, :]).then_inc(ce_ready, 1)

            def hidden(i, s):
                dve.wait_ge(g_copied, i * 8 + s + 1)
                vec.scalar_tensor_tensor(gleaky[s % 2], gcopy[s % 2], LEAKY, gcopy[s % 2], ALU.mult, ALU.max
                                         ).then_inc(g_leaky, 1)
                dve.wait_ge(g_leaky, i * 8 + s + 1)
                vec.tensor_tensor(hT[s % 2], gleaky[s % 2], bank[2 + s % 2][:], ALU.mult).then_inc(h_ready, 1)

            def add_out(i, s):
                dve.wait_ge(y_done, i * 8 + s + 1)
                for t in range(TB):
                    tile = TB * (s % 4) + t
                    vec.scalar_tensor_tensor(x[:, tile, :], bank[4 + 2 * (s % 2) + t // 2][:, (t % 2) * D:(t % 2 + 1) * D],
                                             ce[s // 4][:, tile:tile + 1], x[:, tile, :], ALU.mult, ALU.add
                                             ).then_inc(y_added, 1)

            def expert_pair(i, last):
                for s in range(8):
                    if s < 7:
                        hidden(i, s + 1)
                    elif not last:
                        hidden(i + 1, 0)
                    if s == 0:
                        vec.tensor_copy(ce[1], cw_flat[:, bass.ds(i * 2 * T + T, T)]).then_inc(ce_ready, 1)
                    if s == 4:
                        dve.wait_ge(ce_ready, i * 2 + 2)
                    if s == 0:
                        dve.wait_ge(ce_ready, i * 2 + 1)
                    if s == 4:
                        dve.wait_ge(y_added, i * 32 + 16)
                        if not last:
                            vec.tensor_copy(ce[0], cw_flat[:, bass.ds(i * 2 * T + 2 * T, T)]).then_inc(ce_ready, 1)
                    add_out(i, s)
                dve.wait_ge(y_added, i * 32 + 32)

            cw_flat = over[:, 5968:6128]
            hidden(0, 0)
            with dve.Fori(0, NE // 2 - 1) as i:
                expert_pair(i, False)
            expert_pair(NE // 2 - 1, True)

            for layer in range(3):
                norm, negd = LAYERS[layer]["norm"], -LAYERS[layer]["descale"]
                dve.wait_ge(y_added, T * NE)
                dve.wait_ge(small_loaded, N_SMALL)
                await_(dve, proj_added, T * layer)
                if layer == 0:
                    for j in range(2):
                        link(vec.tensor_copy(maskv[:, j, :], mask8[:, j, :]))
                        link(vec.tensor_scalar(maskv[:, j, :], maskv[:, j, :], 1.0, MASK, ALU.subtract, ALU.mult))
                    for j in range(2):
                        link(vec.tensor_tensor(kscale[:, j + 1, :], kscale[:, j + 1, :], qscale[:, j, :], ALU.mult))
                        link(vec.tensor_scalar(kscale[:, j + 1, :], kscale[:, j + 1, :], NORM_SCALE, None, ALU.mult))
                        link(vec.tensor_scalar(nullb[:, j + 1, :], nullb[:, j + 1, :], 1.0, None, ALU.mult))
                layer_stats(lambda t: x[:, t, :], T, rsq("ln", layer))
                for t in range(T):
                    ins = vec.tensor_scalar(xn[:, t, :], x[:, t, :], mv[:, t, 0:1], rstd[:, t:t + 1], ALU.subtract, ALU.mult)
                    if t % 2:
                        ins.then_inc(xn_ready, 1)
                    else:
                        steps[0] += 1
                        ins.then_inc(dve_step, 1)
                xT_copies(layer + 1)

                def halves(hi, lo, src, dup):
                    link(vec.tensor_copy(hi, dup))
                    return vec.tensor_tensor(lo, src, hi[:, :, 0, :] if len(hi.shape) == 4 else hi[:, 0:DH], ALU.subtract)

                if norm:
                    link(vec.tensor_tensor(nkn, nk[:], nk[:], ALU.mult))
                    vec.tensor_reduce(nss[:, 0:1], nkn, AX_X, ALU.add).then_inc(rsq_in, 1)
                    dve.wait_ge(rsq_out, rsq("nk", layer) + 1)
                    link(vec.tensor_scalar(nkn, nk[:], nss[:, 2:3], None, ALU.mult))
                else:
                    link(vec.tensor_copy(nkn, nk[:]))
                link(vec.tensor_tensor(nkn2, nkn, kscale[:, layer, :], ALU.mult))
                link(vec.tensor_copy(nks[:, 0, :].rearrange("p (c d) -> p c d", c=2), nkn2.unsqueeze(1).to_broadcast([P, 2, DH])))
                link(vec.tensor_tensor(nks[:, 1, 0:DH], nkn2, nks[:, 0, 0:DH], ALU.subtract))
                link(vec.tensor_copy(nks[:, 1, DH:P], nks[:, 1, 0:DH]))

                for b in range(B):
                    dve.wait_ge(kv_done, B * layer + b + 1)
                    w = slice(TB * b, TB * b + TB)
                    kv = bank[4 + b][:].rearrange("p (t c d) -> p t c d", t=TB, c=2)
                    if norm:
                        dve.wait_ge(kv_squared, B * (layer - 1) + b + 1)
                        vec.tensor_reduce(kss[:, 0, w], ksq, AX_X, ALU.add).then_inc(rsq_in, 1)
                        dve.wait_ge(rsq_out, rsq("k", layer, b) + 1)
                        link(vec.tensor_tensor(kn[:, w, :], kv[:, :, 0, :], kss[:, 2, w].unsqueeze(2).to_broadcast([P, TB, DH]),
                                               ALU.mult))
                        link(vec.tensor_tensor(kn2[:, w, :], kn[:, w, :], kscale[:, layer, :].unsqueeze(1).to_broadcast([P, TB, DH]),
                                               ALU.mult))
                    else:
                        link(vec.tensor_tensor(kn2[:, w, :], kv[:, :, 0, :], kscale[:, layer, :].unsqueeze(1).to_broadcast([P, TB, DH]),
                                               ALU.mult))
                    for c in range(2):
                        link(vec.tensor_copy(ks[:, w, c, :], kn2[:, w, :]))
                    link(vec.tensor_tensor(vd[:, w, :], kv[:, :, 1, :], nv[:].unsqueeze(1).to_broadcast([P, TB, DH]), ALU.subtract))
                    link(vec.tensor_scalar(vh[:, w, :], vd[:, w, :], VALUE_SCALE, None, ALU.mult))
                    vec.scalar_tensor_tensor(vl[:, w, :], vd[:, w, :], VALUE_SCALE, vh[:, w, :], ALU.mult, ALU.subtract
                                             ).then_inc(v_halved, 1)
                    link(vec.tensor_copy(kls[:, w, 1, 0:1], maskv[:, 0 if layer == 0 else 1, w].unsqueeze(2)))
                    vec.tensor_tensor(kls[:, w, 0, :], kn2[:, w, :], ks[:, w, 0, :], ALU.subtract).then_inc(ks_ready, 1)
                dve.nop()
                link(vec.tensor_copy(nkn, nkn2))
                vec.tensor_copy(nkn, nkn2).then_inc(ks_ready, 1)
                for g in range(2):
                    dve.wait_ge(kT_done, 5 * layer + 3 + g)
                    vec.tensor_copy(kl[:, g * 8 * P:(g + 1) * 8 * P], bank[2 + g][:].bitcast(F16)[0:DH + 1, :]).then_inc(kT_by_dve, 1)
                dve.wait_ge(kT_done, 5 * layer + 5)
                vec.tensor_copy(nkT[:], bank[4][:].bitcast(F16)[:, 0:2 * P].rearrange("p (c n) -> p c n", c=2)[:, :, 0]
                                ).then_inc(kT_by_dve, 1)

                def q_sum(it):
                    if not it or not norm:
                        return
                    dve.wait_ge(q_squared, it.count(1, 1, 1))
                    vec.tensor_reduce(qss[:, 0], qsq[:], AX_X, ALU.add).then_inc(q_summed, 1)

                def q_norm(it):
                    if not it or not norm:
                        return
                    dve.wait_ge(q_rsqrt, it.count(2, 2, 1))
                    dve.sem_inc(score_seen, 1)
                    await_(dve, q_low, it.count(1, 0))
                    dve.sem_inc(score_seen, 1)
                    vec.tensor_tensor(qn[:], psQ[:].rearrange("p (t h d) -> p t h d", t=TB, h=2),
                                      qss[:, 2].unsqueeze(3).to_broadcast([P, TB, 2, DH]), ALU.mult).then_inc(q_normed, 1)

                def null_score(it):
                    if not it:
                        return
                    dve.wait_ge(null_done, it.count(1, 1))
                    vec.tensor_reduce(sn0[:, 0], psQ[:, 0:4 * TB].rearrange("p (t h c) -> p t h c", t=TB, h=2), AX_X, ALU.add
                                      ).then_inc(null_ready, 1)
                    dve.wait_ge(null_ready, it.count(1, 1))
                    vec.tensor_scalar(sn0[:, 1], sn0[:, 0], negd, None, ALU.mult).then_inc(null_scaled, 1)
                    dve.wait_ge(null_scaled, it.count(2, 1))
                    vec.tensor_tensor(sn[it.b % 2][:], sn0[:, 1],
                                      nullb_flat[:, bass.ds(it.pair() * 2 + H * layer, 2)].unsqueeze(1).to_broadcast([P, TB, 2]),
                                      ALU.subtract).then_inc(null_scaled, 1)

                def mask_tile(it, h, t):
                    if not it:
                        return
                    if it.b == 0 and h == 0 and t == 0:
                        if layer == 0:
                            dve.wait_ge(bias_ready, it.i * 16 + 8 * it.par + 8)
                        else:
                            dve.wait_ge(bias_loaded[it.par], bias_count(layer, it.i))
                        dve.sem_inc(score_seen, 1)
                    if h == 0 and t == 0:
                        dve.wait_ge(null_scaled, it.count(2, 2))
                        dve.sem_inc(score_seen, 1)
                    dve.wait_ge(score_done, it.count(8, TB * h + t + 1))
                    dve.sem_inc(score_seen, 1)
                    n = WIDTH[t]
                    bt = bias[it.par][:, h, OFF[t]:OFF[t] + n] if layer == 0 else bias[it.par][:, h, S - n:S]
                    vec.tensor_tensor_reduce(pr[h][:, OFF[t]:OFF[t] + n], psS[(TB * h + t) % 3][:, 0:n], bt, negd,
                                             sn[it.b % 2][:, t, h:h + 1], ALU.add, ALU.min,
                                             nmax[it.b % 2][:, t, h:h + 1]).then_inc(masked, 1)

                def low_half(it, h, g):
                    if not it:
                        return
                    dve.wait_ge(prT_high, it.count(6, 3 * h + g + 1))
                    n = len(GROUPS[g]) * P
                    w = slice(4 * g * P, 4 * g * P + n)
                    vec.scalar_tensor_tensor(prl[h][:, w], psT[(3 * h + g) % 2][:, 0:n], PROB_SCALE, prh[h][:, w],
                                             ALU.mult, ALU.subtract).then_inc(prT_low, 1)

                def null_part(it):
                    if not it:
                        return
                    dve.wait_ge(masked, it.count(8, 8))
                    vec.tensor_tensor(pn[:, 0], nmax[it.b % 2][:], sn[it.b % 2][:], ALU.subtract).then_inc(null_gap, 1)

                def denominators(it):
                    if not it:
                        return
                    dve.wait_ge(null_exp, it.count(1, 1))
                    vec.tensor_tensor(pn[:, 2], rsum[it.b % 2][:], pn[:, 1], ALU.add).then_inc(den_step, 1)
                    dve.wait_ge(den_step, it.count(2, 1))
                    vec.reciprocal(pn[:, 3], pn[:, 2]).then_inc(den_step, 1)

                def o_rows(it):
                    if not it:
                        return
                    dve.wait_ge(av_done, it.count(2, 2))
                    dve.wait_ge(den_step, it.count(2, 2))
                    vec.tensor_tensor(orow[:], psO[:].rearrange("p (t h d) -> p t h d", t=TB, h=2),
                                      pn[:, 3].unsqueeze(3).to_broadcast([P, TB, 2, DH]), ALU.mult).then_inc(o_ready, 1)

                def body(before2, before, it, after, after2):
                    low_half(before, 0, 2)
                    mask_tile(it, 0, 0)
                    mask_tile(it, 0, 1)
                    mask_tile(it, 0, 2)
                    low_half(before, 1, 0)
                    o_rows(before2)
                    denominators(before)
                    q_sum(after2)
                    mask_tile(it, 0, 3)
                    mask_tile(it, 1, 0)
                    mask_tile(it, 1, 1)
                    low_half(before, 1, 1)
                    low_half(before, 1, 2)
                    mask_tile(it, 1, 2)
                    mask_tile(it, 1, 3)
                    null_part(it)
                    q_norm(after2)
                    low_half(it, 0, 0)
                    low_half(it, 0, 1)
                    null_score(after)

                positions(dve, layer, body)
                for t in range(T):
                    y = bank[t % 4][:, 0:D]
                    dve.wait_ge(proj_done, T * layer + t + 1)
                    link(vec.bn_stats(stats[:, t, :], y))
                    vec.bn_aggr(mv[:, t, :], stats[:, t, :]).then_inc(rsq_in, 1)
                    dve.wait_ge(rsq_in, rsq("out", layer, t) + 1)
                    link(vec.scalar_tensor_tensor(ytmp[:, t % 2, :], y, mv[:, t, 0:1], gout[:], ALU.subtract, ALU.mult))
                    dve.wait_ge(rsq_out, rsq("out", layer, t) + 1)
                    vec.scalar_tensor_tensor(x[:, t, :], ytmp[:, t % 2, :], rstd[:, t:t + 1], x[:, t, :], ALU.mult, ALU.add
                                             ).then_inc(proj_added, 1)


_ATTN = ("null_attn_bias", "Wq", "Wkv", "g_out")
_NORMED = ("g_norm", "q_scale", "k_scale", "w0", "b0", "g0", "w1", "b1", "g1", "w2", "b2", "Wout")
_INS = (["x", "cond_64", "fside_16xSxS_0", "mask_BxS_bk0", "mask_BxS_bf1", "L0_cond_wt", "L0_cond_wg"]
        + [f"L1_cond_{n}" for n in (*_ATTN, "g_in", "Wo")]
        + [f"L{k}_cond_{n}" for k in (2, 3) for n in (*_ATTN, *_NORMED)])


def kernel(**inputs):
    import numpy as _np
    import concourse.bacc as _bacc
    from concourse import mybir as _mybir
    from concourse.bass_utils import run_bass_kernel_spmd as _run

    nc = _bacc.Bacc("TRN2", target_bir_lowering=False, num_devices=1)
    host = {n: _np.ascontiguousarray(inputs[n]) for n in _INS}

    def experts(own, shared, axis):
        halves = _np.split(_np.asarray(inputs[shared]), 2, axis=axis)
        return _np.concatenate([_np.asarray(inputs[own]), _np.stack(halves)])

    host["gate"] = experts("L0_cond_w_gate", "L0_cond_sw_gate", 1)
    host["up"] = experts("L0_cond_w_up", "L0_cond_sw_up", 1)
    host["down"] = experts("L0_cond_w_down", "L0_cond_sw_down", 0)
    arrays, args = {}, {}
    for name, value in host.items():
        arrays[f"in_{name}_dram"] = value
        args[name] = nc.dram_tensor(f"in_{name}_dram", value.shape, _mybir.dt.from_np(value.dtype), kind="ExternalInput").ap()
    out = nc.dram_tensor("out_0_dram", (4, 512, 256), _mybir.dt.float32, kind="ExternalOutput").ap()
    build(nc, args, out)
    r = _run(nc, [arrays], core_ids=[0])
    return r.results[0]["out_0_dram"]
```

```python
from contextlib import ExitStack

import concourse.bass as bass
from concourse import mybir

F32 = mybir.dt.float32
F16 = mybir.dt.float16
U32 = mybir.dt.uint32
U8 = mybir.dt.uint8
ALU = mybir.AluOpType
ACT = mybir.ActivationFunctionType
AX_X = mybir.AxisListType.X

P = 128
B, S, D = 4, 512, 256
T = B * S // P
TB = S // P
KC = D // P
H, DH = 16, 64
PAIRS = H // 2
ITEMS = PAIRS * B
E = 8
NE = 10
M = 128
G = 64
LN_EPS = 1e-5
NEG = -1e30
MASK = 65504.0
LEAKY = 0.01

WIDTH = [(t + 1) * P for t in range(TB)]
OFF = [sum(WIDTH[:t]) for t in range(TB)]
CAUSAL = sum(WIDTH)
BLOCKS = [(t, k) for t in range(TB) for k in range(t + 1)]
GROUPS = [BLOCKS[0:4], BLOCKS[4:8], BLOCKS[8:10]]

RAW_SCALE = 8.0
PROB_SCALE = 1024.0
VALUE_SCALE = 16.0
WEIGHT_SCALE = 64.0
NORM_SCALE = 32.0


class Item:

    def __init__(self, layer, i, par, b):
        self.layer, self.i, self.par, self.b = layer, i, par, b

    def count(self, per_item, more=0, layer0=0):
        fixed = per_item * (ITEMS * (self.layer - layer0) + 4 * self.par + self.b) + more
        return self.i * (8 * per_item) + fixed

    def pair(self):
        return self.i * 2 + self.par

    def ahead(self, n):
        turn, left = divmod(4 * self.par + self.b + n, 8)
        i = self.i + turn if turn else self.i
        if isinstance(i, int) and not 0 <= i < ITEMS // 8:
            return None
        return Item(self.layer, i, left // 4, left % 4)


def await_(eng, sem, value):
    if isinstance(value, int) and value <= 0:
        return
    eng.wait_ge(sem, value)


def build(nc, a, out):
    bias_dram = nc.dram_tensor("bias_rows", (2, H, P, 640), F32, kind="Internal").ap()

    def bcast_rows(ap1d, n, offset=0):
        return bass.AP(tensor=ap1d.tensor, offset=ap1d.offset + offset, ap=[[0, P], [1, n]])

    with ExitStack() as ctx:
        def sb(name, shape, dt=F32):
            return ctx.enter_context(nc.sbuf_tensor(name, shape, dt))

        def sem(name):
            return ctx.enter_context(nc.semaphore(name))

        x = sb("x", [P, T, D])
        xT = sb("xT", [P, KC, T * P])
        outT = sb("outT", [P, PAIRS, T * P])
        ident = sb("ident", [P, P])
        ident16 = sb("ident16", [P, P], F16)
        consts = sb("consts", [P, 4])
        wq = sb("wq", [P, KC, H * DH])
        wkv = sb("wkv", [P, KC, 2 * DH])
        wo = sb("wo", [P, PAIRS, D])
        gin = sb("gin", [P, 3, KC])
        gout = sb("gout", [P, D])
        kscale = sb("kscale", [P, 3, DH])
        qscale = sb("qscale", [P, 2, DH])
        nullb = sb("nullb", [P, 3, H])
        nullb_flat = nullb[:, :, :].rearrange("p a b -> p (a b)")
        nk = sb("nk", [P, DH])
        nv = sb("nv", [P, DH])
        nvT = sb("nvT", [P, 1])
        mask8 = sb("mask8", [P, 2, T], U8)
        maskv = sb("maskv", [P, 2, T])
        stats = sb("stats", [P, T, 6])
        mv = sb("mv", [P, T, 2])
        rstd = sb("rstd", [P, T])
        rtmp = sb("rtmp", [P, T])
        kh = sb("kh", [P, T * P], F16)
        kl = sb("kl", [DH + 1, T * P], F16)
        vh = sb("vh", [P, T, DH], F16)
        vl = sb("vl", [P, T, DH], F16)
        nkT = sb("nkT", [P, 2], F16)
        bias = [sb(f"bias{n}", [P, 2, CAUSAL]) for n in range(2)]
        pr_all = sb("pr", [P, 2 * CAUSAL])
        pr = [pr_all[:, CAUSAL * n:CAUSAL * (n + 1)] for n in range(2)]
        halves = sb("halves", [P, 4, CAUSAL], F16)
        prh = [halves[:, n, :] for n in range(2)]
        prl = [halves[:, 2 + n, :] for n in range(2)]
        qraw = sb("qraw", [P, TB, 2, DH])
        qsq = sb("qsq", [P, TB, 2, DH])
        qn = sb("qn", [P, TB, 2, DH])
        qs = sb("qs", [P, TB, 2, 2, DH], F16)
        qT = [sb(f"qT{n}", [P, 2, S], F16) for n in range(2)]
        qB = [sb(f"qB{n}", [DH + 1, 2, S], F16) for n in range(2)]
        qss = sb("qss", [P, 3, TB, 2])
        sn0 = sb("nullsc", [P, 2, TB, 2])
        sn = [sb(f"sn{n}", [P, TB, 2]) for n in range(2)]
        nmax = [sb(f"nmax{n}", [P, TB, 2]) for n in range(2)]
        rsum = [sb(f"rsum{n}", [P, TB, 2]) for n in range(2)]
        pn = sb("pn", [P, 4, TB, 2])
        orow = sb("orow", [P, TB, 2, DH])
        ytmp = sb("ytmp", [P, 2, D])
        flat = halves[:, :, :].rearrange("p a b -> p (a b)").bitcast(F32)
        xn = pr_all[:, 0:4 * D].rearrange("p (t d) -> p t d", t=4)
        ks = pr_all[:, 1024:2048].bitcast(F16).rearrange("p (t c d) -> p t c d", t=T, c=2)
        kn = pr_all[:, 2048:2304].rearrange("p (t d) -> p t d", t=TB)
        vd = pr_all[:, 2304:2560].rearrange("p (t d) -> p t d", t=TB)
        kls = flat[:, 0:1024].bitcast(F16).rearrange("p (t c d) -> p t c d", t=T, c=2)
        kn2 = flat[:, 1024:1280].rearrange("p (t d) -> p t d", t=TB)
        ksq = flat[:, 1280:1536].rearrange("p (t d) -> p t d", t=TB)
        nks = flat[:, 1536:1664].bitcast(F16).rearrange("p (c d) -> p c d", c=2)
        nkn = flat[:, 1664:1728]
        nkn2 = flat[:, 1728:1792]
        kss = flat[:, 1792:1840].rearrange("p (c t) -> p c t", c=3)
        nss = flat[:, 1840:1844]
        over = outT[:, :, :].rearrange("p a b -> p (a b)")
        wload = [over[:, 768 * n:768 * n + 768] for n in range(2)]
        wgu = [w[:, 0:512].rearrange("p (w k m) -> p w k m", w=2, k=KC) for w in wload]
        wd = [w[:, 512:768] for w in wload]
        flat16 = halves[:, :, :].rearrange("p a b -> p (a b)")
        w16 = flat16[:, 0:3072].rearrange("p (n c m) -> p n c m", n=2, c=2)
        h16 = flat16[:, 3072:5120].rearrange("p (n c m) -> p n c m", n=2, c=2)
        x16 = over[:, 12032:16128].bitcast(F16).rearrange("p (c k n) -> p c k n", c=2, k=KC)
        gcopy = [over[:, 1536 + 512 * n:2048 + 512 * n] for n in range(2)]
        gleaky = [over[:, 2560 + 512 * n:3072 + 512 * n] for n in range(2)]
        hT = [over[:, 3584 + 512 * n:4096 + 512 * n] for n in range(2)]
        wtT = over[:, 4608:4624].rearrange("p (k e) -> p k e", k=KC)
        wgT = over[0:G, 4624:4632]
        condT = over[0:G, 4640:4644]
        condb = over[0:G, 4656:5168].rearrange("p (b n) -> p b n", b=B)
        lg = over[:, 5168:5296].rearrange("p (t e) -> p t e", t=T)
        sc = over[:, 5296:5424].rearrange("p (t e) -> p t e", t=T)
        top = over[:, 5424:5552].rearrange("p (t e) -> p t e", t=T)
        topi = over[:, 5552:5680].bitcast(U32).rearrange("p (t e) -> p t e", t=T)
        eq = over[:, 5680:5808].rearrange("p (t e) -> p t e", t=T)
        r1 = over[:, 5808:5936].rearrange("p (c t) -> p c t", c=8)
        idx = over[:, 5936:5968].rearrange("p (t c) -> p t c", c=2)
        cw = over[:, 5968:6128].rearrange("p (e t) -> p e t", e=NE)
        iota8 = over[:, 6128:6136]
        ce = [over[:, 6144 + 16 * n:6160 + 16 * n] for n in range(2)]
        h0 = [over[:, n:n + 1024].rearrange("p (t d) -> p t d", t=TB) for n in (6400, 1536)]
        h1 = [over[:, n:n + 1024].rearrange("p (t d) -> p t d", t=TB) for n in (7424, 2560)]
        hTT = [over[:, n:n + 1024].rearrange("p (k n) -> p k n", k=KC) for n in (8448, 3584)]
        mlp_space = (over[:, 9472:12032], pr_all)
        rows = [m[:, 0:1280].rearrange("p (c d) -> p c d", c=5) for m in mlp_space]
        w1s = [m[:, 1280:1792].rearrange("p (k d) -> p k d", k=KC) for m in mlp_space]
        w2s = [m[:, 1792:1824].rearrange("p (k d) -> p k d", k=KC) for m in mlp_space]
        b2s = [m[0:H, 1824:1825] for m in mlp_space]
        pos = over[:, 11304:11308]
        brow = [m[0:H, 1920:2560] for m in mlp_space]

        bank = [ctx.enter_context(nc.psum_tensor(f"bank{n}", [P, 512], F32)) for n in range(8)]
        psS, psT, psO, psQ, psX = bank[0:3], bank[3:5], bank[5], bank[6], bank[7]
        psX16 = psX[:].bitcast(F16)

        x_loaded = sem("x_loaded")
        gate_loaded = sem("gate_loaded")
        small_loaded = sem("small_loaded")
        mlp_loaded = [sem(f"mlp_loaded{n}") for n in range(2)]
        in_weights_loaded = sem("in_weights_loaded")
        out_weights_loaded = sem("out_weights_loaded")
        bias_scaled = sem("bias_scaled")
        bias_ready = sem("bias_ready")
        bias_rows_stored = sem("bias_rows_stored")
        stored = sem("stored")
        consts_ready = sem("consts_ready")
        dve_step = sem("dve_step")
        act_step = sem("act_step")
        pool_step = sem("pool_step")
        rsq_in = sem("rsq_in")
        rsq_out = sem("rsq_out")
        stats_ready = sem("stats_ready")
        mlp_step = sem("mlp_step")
        mlp_h = sem("mlp_h")
        mlp_turned = sem("mlp_turned")
        mlp_hT = sem("mlp_hT")
        mlp_hT_first = sem("mlp_hT_first")
        mlp_done = sem("mlp_done")
        xn_ready = sem("xn_ready")
        xT_done = sem("xT_done")
        xT_by_act = sem("xT_by_act")
        xT_by_dve = sem("xT_by_dve")
        gate_done = sem("gate_done")
        gate_max = sem("gate_max")
        gate_exp = sem("gate_exp")
        kv_done = sem("kv_done")
        v_halved = sem("v_halved")
        kv_squared = sem("kv_squared")
        ks_ready = sem("ks_ready")
        kT_done = sem("kT_done")
        kT_by_act = sem("kT_by_act")
        kT_by_dve = sem("kT_by_dve")
        proj_done = sem("proj_done")
        proj_added = sem("proj_added")
        proj_read = sem("proj_read")
        xn_turned = sem("xn_turned")
        xn_copied = sem("xn_copied")
        nks_ready = sem("nks_ready")
        x_high = sem("x_high")
        x_low = sem("x_low")
        w_scaled = sem("w_scaled")
        w_high = sem("w_high")
        w_low = sem("w_low")
        h_high = sem("h_high")
        h_low = sem("h_low")
        gu_done = sem("gu_done")
        g_copied = sem("g_copied")
        g_leaky = sem("g_leaky")
        h_ready = sem("h_ready")
        y_done = sem("y_done")
        y_added = sem("y_added")
        ce_ready = sem("ce_ready")
        q_done = sem("q_done")
        q_copied = sem("q_copied")
        q_squared = sem("q_squared")
        q_summed = sem("q_summed")
        q_rsqrt = sem("q_rsqrt")
        q_normed = sem("q_normed")
        q_high = sem("q_high")
        q_low = sem("q_low")
        qT_done = sem("qT_done")
        qT_copied = sem("qT_copied")
        qB_copied = sem("qB_copied")
        null_done = sem("null_done")
        null_scaled = sem("null_scaled")
        null_ready = sem("null_ready")
        score_done = sem("score_done")
        masked = sem("masked")
        exp_done = sem("exp_done")
        prT_done = sem("prT_done")
        prT_high = sem("prT_high")
        prT_low = sem("prT_low")
        av_done = sem("av_done")
        null_gap = sem("null_gap")
        null_exp = sem("null_exp")
        den_step = sem("den_step")
        o_ready = sem("o_ready")
        oT_done = sem("oT_done")
        oT_copied = sem("oT_copied")
        pool_seen = sem("pool_seen")
        vector_seen = sem("vector_seen")
        scalar_seen = sem("scalar_seen")
        expert_loaded = [sem(f"expert_loaded{n}") for n in range(2)]
        bias_loaded = [sem(f"bias_loaded{n}") for n in range(2)]

        block = ctx.enter_context(nc.Block())

        def positions(eng, layer, body, turn_keys=None):
            def run(item):
                body(*(item.ahead(n) for n in range(-2, 3)))

            def run_number(n):
                body(*(Item(layer, (n + m) // 8, (n + m) % 8 // 4, (n + m) % 4) if 0 <= n + m < ITEMS else None
                       for m in range(-2, 3)))

            for n in range(-2, 4):
                run_number(n)
                if n == -2 and turn_keys:
                    turn_keys(layer)
            with eng.Fori(0, ITEMS // 8 - 1) as i:
                for n in range(4, 12):
                    run(Item(layer, i, 0, 0).ahead(n))
            for n in range(ITEMS - 4, ITEMS + 2):
                run_number(n)

        LAYERS = (
            dict(n="L1_cond", norm=False, descale=1.0 / (8 * RAW_SCALE * RAW_SCALE),
                 gin="g_in", wo="Wo"),
            dict(n="L2_cond", norm=True, descale=8 / (NORM_SCALE * NORM_SCALE),
                 gin="g_norm", wo="Wout"),
            dict(n="L3_cond", norm=True, descale=8 / (NORM_SCALE * NORM_SCALE),
                 gin="g_norm", wo="Wout"),
        )

        def arg(layer, name):
            return a[f"{LAYERS[layer]['n']}_{name}"]

        N_SMALL = 16 * (3 * 2 + 2 * 2 + 6)
        N_MLP_LOADS = 16 * 8
        STEPS = range(T + 5)

        def keys_batch(t):
            return (t - 7) // 4 if t >= 7 and t % 4 == 3 and t < T + 7 else None

        def stats_tile(n, t):
            tile = t - 1 if n else t
            return tile if 0 <= tile < T else None

        RSQ = [("mlp", n, stage) for stage in range(2) for n in range(2)]
        for n in range(4):
            for t in STEPS:
                if n < 3 and stats_tile(n, t) is not None:
                    RSQ.append(("ln", n, stats_tile(n, t)))
                if n and t < T:
                    RSQ.append(("out", n - 1, t))
                if n in (1, 2) and t == 1:
                    RSQ.append(("nk", n, 0))
                if n in (1, 2) and keys_batch(t) is not None:
                    RSQ.append(("k", n, keys_batch(t)))

        def rsq(kind, layer=0, j=0):
            return RSQ.index((kind, layer, j))

        def mlp_loads(sp, n):
            for j, name in enumerate(("w0", "b0", "g0", "b1", "g1")):
                sp.dma_start(rows[n][:, j, :], bcast_rows(arg(n + 1, name), D)).then_inc(mlp_loaded[n], 16)
            sp.dma_start(w1s[n], arg(n + 1, "w1").rearrange("(k p) d -> p k d", p=P)).then_inc(mlp_loaded[n], 16)
            sp.dma_start(w2s[n], arg(n + 1, "w2").rearrange("(k p) d -> p k d", p=P)).then_inc(mlp_loaded[n], 16)
            sp.dma_start(b2s[n], arg(n + 1, "b2").rearrange("(p a) -> p a", a=1)).then_inc(mlp_loaded[n], 16)

        def load_expert(sp, e, par):
            for w, name in enumerate(("gate", "up")):
                sp.dma_start(wgu[par][:, w], a[name].rearrange("e d m -> (e d) m")[bass.ds(e * D, D)]
                             .rearrange("(k p) m -> p k m", k=KC)).then_inc(expert_loaded[par], 16)
            sp.dma_start(wd[par], a["down"].rearrange("e m d -> (e m) d")[bass.ds(e * M, M)]
                         ).then_inc(expert_loaded[par], 16)

        def load_in_weights(sp, layer):
            sp.dma_start(wkv[:], arg(layer, "Wkv").rearrange("(k p) n -> p k n", p=P)).then_inc(in_weights_loaded, 16)
            sp.dma_start(wq[:], arg(layer, "Wq").rearrange("(k p) n -> p k n", p=P)).then_inc(in_weights_loaded, 16)

        def load_out_weights(sp, layer):
            sp.dma_start(wo[:], arg(layer, LAYERS[layer]["wo"]).rearrange("(k p) n -> p k n", p=P)).then_inc(out_weights_loaded, 16)
            sp.dma_start(gout[:], bcast_rows(arg(layer, "g_out"), D)).then_inc(out_weights_loaded, 16)

        def load_bias(sp, layer, pair, par):
            if layer == 0:
                f = a["fside_16xSxS_0"].rearrange("h s n -> (h s) n")
                for h in range(2):
                    for t in range(TB):
                        sp.dma_start(bias[par][:, h, OFF[t]:OFF[t] + WIDTH[t]],
                                     f[bass.ds((pair * 2 + h) * S + t * P, P), 0:WIDTH[t]]).then_inc(bias_loaded[par], 16)
            else:
                if isinstance(pair, int) and pair == 0:
                    sp.wait_ge(bias_rows_stored, 16 * layer)
                for h in range(2):
                    src = bias_dram[layer - 1].rearrange("h p n -> (h p n)")[bass.ds((pair * 2 + h) * (P * 640) + P - 1, P * 639)]
                    sp.dma_start(bias[par][:, h, 0:S], src.rearrange("(p n) -> p n", p=P)[:, 0:S]).then_inc(bias_loaded[par], 16)

        def bias_count(layer, i):
            if layer == 0:
                return i * 128 + 128
            return i * 32 + 32 + 512 + 128 * (layer - 1)

        @block.sync
        def _(sp):
            xd = a["x"].rearrange("b (t p) d -> p (b t) d", p=P)
            mlp_loads(sp, 0)
            for n in range(4):
                sp.dma_start(x[:, 4 * n:4 * n + 4, :], xd[:, 4 * n:4 * n + 4, :]).then_inc(x_loaded, 16)
            c = a["cond_64"]
            for k in range(KC):
                sp.dma_start(wtT[:, k, :], a["L0_cond_wt"].rearrange("e (k p) -> k p e", p=P)[k],
                             allow_slow_non_contiguous=True).then_inc(gate_loaded, 16)
            sp.dma_start(wgT, a["L0_cond_wg"].rearrange("e p -> p e"),
                         allow_slow_non_contiguous=True).then_inc(gate_loaded, 16)
            sp.dma_start(condT, c.rearrange("b p -> p b"),
                         allow_slow_non_contiguous=True).then_inc(gate_loaded, 16)
            mlp_loads(sp, 1)
            for n in range(2):
                load_expert(sp, n, n)
            n = 0
            for layer in range(3):
                sp.dma_start(gin[:, layer, :], arg(layer, LAYERS[layer]["gin"]).rearrange("(k p) -> p k", p=P),
                             allow_slow_non_contiguous=True).then_inc(small_loaded, 16)
                sp.dma_start(nullb[:, layer, :], bcast_rows(arg(layer, "null_attn_bias"), H)).then_inc(small_loaded, 16)
                n += 2
                if layer:
                    sp.dma_start(kscale[:, layer, :], bcast_rows(arg(layer, "k_scale"), DH)).then_inc(small_loaded, 16)
                    sp.dma_start(qscale[:, layer - 1, :], bcast_rows(arg(layer, "q_scale"), DH)).then_inc(small_loaded, 16)
                    n += 2
            sp.dma_start(nk[:], bcast_rows(c, G)).then_inc(small_loaded, 16)
            sp.dma_start(nv[:], bcast_rows(c, G, G)).then_inc(small_loaded, 16)
            for half in range(2):
                sp.dma_start(nvT[half * DH:half * DH + DH, :], c[1:2, :].rearrange("a p -> p a"),
                             allow_slow_non_contiguous=True).then_inc(small_loaded, 16)
            for j, name in enumerate(("mask_BxS_bk0", "mask_BxS_bf1")):
                sp.dma_start(mask8[:, j, :], a[name].rearrange("b (t p) -> p (b t)", p=P),
                             allow_slow_non_contiguous=True).then_inc(small_loaded, 16)
            assert 16 * (n + 6) == N_SMALL
            load_in_weights(sp, 0)
            for par in range(2):
                load_bias(sp, 0, par, par)
            with sp.Fori(1, NE // 2) as i:
                for par in range(2):
                    sp.wait_ge(w_low, i * 2 + par - 1)
                    load_expert(sp, i * 2 + par, par)
            for layer in range(3):
                if layer:
                    sp.wait_ge(q_done, ITEMS * layer)
                    load_in_weights(sp, layer)
                    sp.wait_ge(masked, 8 * ITEMS * layer)
                    for par in range(2):
                        load_bias(sp, layer, par, par)
                    sp.wait_ge(proj_added, T * layer)
                load_out_weights(sp, layer)

                def bias_ahead(i):
                    for par in range(2):
                        sp.wait_ge(masked, i * 64 + 8 * (ITEMS * layer + 4 * par - 4))
                        load_bias(sp, layer, i * 2 + par, par)

                with sp.Fori(1, PAIRS // 2) as i:
                    bias_ahead(i)
            od = out.rearrange("b (t p) d -> p (b t) d", p=P)
            for n in range(4):
                sp.wait_ge(proj_added, 2 * T + 4 * n + 4)
                sp.dma_start(od[:, 4 * n:4 * n + 4, :], x[:, 4 * n:4 * n + 4, :]).then_inc(stored, 16)
            sp.wait_ge(stored, 64)

        @block.gpsimd
        def _(pool):
            nc.gpsimd.memset(ident[:], 0.0).then_inc(pool_step, 1)
            nc.gpsimd.memset(consts[:, 0:1], -0.5).then_inc(pool_step, 1)
            nc.gpsimd.memset(consts[:, 1:2], 1.0 / LAYERS[0]["descale"]).then_inc(pool_step, 1)
            nc.gpsimd.iota(iota8, pattern=[[1, E]], base=0, channel_multiplier=0,
                           allow_small_or_imprecise_dtypes=True).then_inc(pool_step, 1)
            nc.gpsimd.iota(pos, pattern=[[-P, TB]], base=S - 1, channel_multiplier=-1,
                           allow_small_or_imprecise_dtypes=True).then_inc(pool_step, 1)
            nc.gpsimd.memset(kscale[:, 0, :], RAW_SCALE).then_inc(pool_step, 1)
            for n in range(2):
                nc.gpsimd.memset(brow[n][:, S:640], NEG / LAYERS[1]["descale"]).then_inc(pool_step, 1)
            for n in range(2):
                pool.wait_ge(pool_step, 8 + n)
                nc.gpsimd.memset(qB[n][DH:DH + 1, :, :], MASK).then_inc(pool_step, 1)
            pool.wait_ge(pool_step, 10)
            nc.gpsimd.affine_select(out=ident[:], in_=ident[:], compare_op=ALU.not_equal, fill=1.0, base=0,
                                    pattern=[[-1, P]], channel_multiplier=1).then_inc(pool_step, 1)
            pool.wait_ge(pool_step, 11)
            nc.gpsimd.tensor_copy(ident16[:], ident[:]).then_inc(consts_ready, 1)
            steps = [11]

            def rsqrt(number, src, tmp, dst, mult=None, least=None):
                pool.wait_ge(rsq_in, number + 1)
                if mult is None:
                    nc.gpsimd.tensor_scalar(tmp, src, LN_EPS, None, ALU.add).then_inc(pool_step, 1)
                else:
                    nc.gpsimd.tensor_scalar(tmp, src, mult, least, ALU.mult, ALU.max).then_inc(pool_step, 1)
                steps[0] += 1
                pool.wait_ge(pool_step, steps[0])
                nc.gpsimd.tensor_tensor(dst, tmp, consts[:, 0:1].to_broadcast(list(tmp.shape)), ALU.pow
                                        ).then_inc(rsq_out, 1)

            for stage in range(2):
                for n in range(2):
                    w = slice(TB * n, TB * n + TB)
                    rsqrt(rsq("mlp", n, stage), mv[:, w, 1], rtmp[:, w], rstd[:, w])

            def between(n):
                for kind, layer, t in RSQ:
                    if (kind == "out" and layer == n - 1) or (kind == "ln" and layer == n):
                        rsqrt(rsq(kind, layer, t), mv[:, t, 1:2], rtmp[:, t:t + 1], rstd[:, t:t + 1])
                    elif kind == "nk" and layer == n:
                        rsqrt(rsq(kind, layer), nss[:, 0:1], nss[:, 1:2], nss[:, 2:3], 1.0, 1e-24)
                    elif kind == "k" and layer == n:
                        w = slice(TB * t, TB * t + TB)
                        rsqrt(rsq(kind, layer, t), kss[:, 0, w], kss[:, 1, w], kss[:, 2, w], 1.0, 1e-24)

            for n in range(B):
                pool.wait_ge(x_high, n + 1)
                w = slice(n * S, n * S + S)
                nc.gpsimd.tensor_tensor(x16[:, 1, :, w], xT[:, :, w], x16[:, 0, :, w], ALU.subtract).then_inc(x_low, 1)

            def weights_low(i, par):
                pool.wait_ge(w_high, i * 2 + par + 1)
                nc.gpsimd.tensor_tensor(w16[:, par, 1], wload[par], w16[:, par, 0], ALU.subtract).then_inc(w_low, 1)

            def hidden_low(i, s):
                pool.wait_ge(h_high, i * 8 + s + 1)
                nc.gpsimd.tensor_tensor(h16[:, s % 2, 1], hT[s % 2], h16[:, s % 2, 0], ALU.subtract).then_inc(h_low, 1)

            def expert_pair(i, last):
                for s in range(8):
                    hidden_low(i, s)
                    if s == 1:
                        weights_low(i, 1)
                    if s == 5 and not last:
                        weights_low(i + 1, 0)

            weights_low(0, 0)
            with pool.Fori(0, NE // 2 - 1) as i:
                expert_pair(i, False)
            expert_pair(NE // 2 - 1, True)

            def bias_part(i, par, b):
                h, tiles = b // 2, ((0, 1, 2), (3,))[b % 2]
                if b == 0:
                    pool.wait_ge(bias_loaded[par], bias_count(0, i))
                    nc.gpsimd.sem_inc(pool_seen, 1)
                w = bias[par][:, h, OFF[tiles[0]]:OFF[tiles[-1]] + WIDTH[tiles[-1]]]
                nc.gpsimd.tensor_tensor(w, w, consts[:, 1:2].to_broadcast(list(w.shape)), ALU.mult
                                        ).then_inc(bias_scaled, 1)
                pool.wait_ge(bias_scaled, i * 8 + 4 * par + b + 1)
                nc.gpsimd.sem_inc(pool_seen, 1)
                for t in tiles:
                    d = bias[par][:, h, OFF[t] + t * P:OFF[t] + t * P + P]
                    nc.gpsimd.affine_select(out=d, in_=d, compare_op=ALU.is_ge, fill=NEG, base=0,
                                            pattern=[[-1, P]], channel_multiplier=1).then_inc(bias_ready, 1)

            for part in range(4):
                bias_part(0, 0, part)
            for layer in range(3):
                norm = LAYERS[layer]["norm"]
                between(layer)

                def q_rsqrt_norm(it):
                    if not it or not norm:
                        return
                    pool.wait_ge(q_summed, it.count(1, 1, 1))
                    nc.gpsimd.sem_inc(pool_seen, 1)
                    nc.gpsimd.tensor_scalar(qss[:, 1], qss[:, 0], NORM_SCALE ** -2, 1e-24 * NORM_SCALE ** -2,
                                            ALU.mult, ALU.max).then_inc(q_rsqrt, 1)
                    pool.wait_ge(q_rsqrt, it.count(2, 1, 1))
                    nc.gpsimd.tensor_tensor(qss[:, 2], qss[:, 1], consts[:, 0:1].unsqueeze(2).to_broadcast([P, TB, 2]),
                                            ALU.pow).then_inc(q_rsqrt, 1)

                def q_squares(it):
                    if not it or not norm:
                        return
                    pool.wait_ge(q_copied, it.count(1, 1))
                    nc.gpsimd.tensor_tensor(qsq[:], qraw[:], qraw[:], ALU.mult).then_inc(q_squared, 1)

                def q_norm(it):
                    if not it or not norm:
                        return
                    pool.wait_ge(q_rsqrt, it.count(2, 2, 1))
                    nc.gpsimd.tensor_tensor(qn[:], qraw[:], qss[:, 2].unsqueeze(3).to_broadcast([P, TB, 2, DH]), ALU.mult
                                            ).then_inc(q_normed, 1)

                def q_low_half(it):
                    if not it:
                        return
                    pool.wait_ge(q_high, it.count(1, 1))
                    nc.gpsimd.tensor_tensor(qs[:, :, :, 1, :], qn[:], qs[:, :, :, 0, :], ALU.subtract).then_inc(q_low, 1)

                def qB_copy(it):
                    if not it:
                        return
                    pool.wait_ge(qT_copied, it.count(1, 1))
                    nc.gpsimd.sem_inc(pool_seen, 1)
                    nc.gpsimd.tensor_copy(qB[it.b % 2][0:DH].bitcast(U32), qT[it.b % 2][0:DH].bitcast(U32)).then_inc(qB_copied, 1)

                def body(before2, before, it, after, after2):
                    q_low_half(after)
                    q_squares(after2)
                    qB_copy(after)
                    q_rsqrt_norm(after2)
                    q_norm(after2)
                    last_pair = it and isinstance(it.i, int) and it.pair() == PAIRS - 1
                    if layer == 0 and it and it.b in (1, 2) and not last_pair:
                        for part in (0, 1) if it.b == 1 else (2, 3):
                            bias_part(it.i + it.par, 1 - it.par, part)

                positions(pool, layer, body)
            between(3)

        @block.tensor
        def _(pe):
            pe.wait_ge(consts_ready, 1)

            def transposes():
                pe.wait_ge(x_loaded, 16 * 4)
                for g in range(8):
                    if g >= 2:
                        pe.wait_ge(xT_by_act, g - 1)
                        pe.wait_ge(xT_by_dve, g - 1)
                    for c in range(KC):
                        for j in range(2):
                            ins = pe.transpose(bank[2 * (g % 2) + c][:, j * P:(j + 1) * P],
                                               x[:, 2 * g + j, c * P:(c + 1) * P], ident[:])
                    ins.then_inc(xT_done, 1)

            transposes()
            pe.wait_ge(xT_by_act, 8)
            pe.wait_ge(xT_by_dve, 8)
            pe.wait_ge(gate_loaded, 16 * 4)
            pe.wait_ge(gate_max, 1)
            for t in range(T):
                o = bank[7][:, t * E:(t + 1) * E]
                for c in range(KC):
                    pe.matmul(o, xT[:, c, t * P:(t + 1) * P], wtT[:, c, :], start=(c == 0), stop=False)
                ins = pe.matmul(o, condb[:, t // TB, :], wgT, start=False, stop=True)
            ins.then_inc(gate_done, 1)

            for stage in range(2):
                for n in range(2):
                    pe.wait_ge(mlp_h, 2 * stage + n + 1)
                    for c in range(KC):
                        for t in range(TB):
                            ins = pe.transpose(bank[4 * n + c][:, t * P:(t + 1) * P], h1[n][:, t, c * P:(c + 1) * P], ident[:])
                    ins.then_inc(mlp_turned, 1)
                for n in range(2):
                    pe.wait_ge(mlp_hT, 2 * stage + n + 1)
                    if stage == 0:
                        pe.wait_ge(gate_max, 2)
                        for t in range(TB):
                            for c in range(KC):
                                ins = pe.matmul(bank[4 * n + 2 + t // 2][:, (t % 2) * D:(t % 2 + 1) * D],
                                                hTT[n][:, c, t * P:(t + 1) * P], w1s[n][:, c, :],
                                                start=(c == 0), stop=(c == KC - 1))
                    else:
                        for c in range(KC):
                            ins = pe.matmul(bank[4 * n + 2][0:H, :], w2s[n][:, c, :], hTT[n][:, c, :],
                                            start=(c == 0), stop=(c == KC - 1))
                    ins.then_inc(mlp_done, 1)

            def gate_up(i, s):
                par, n = s // 4, s % 4
                tokens = slice(n * S, n * S + S)
                pe.wait_ge(x_low, n + 1)
                if n == 0:
                    pe.wait_ge(w_low, i * 2 + par + 1)
                await_(pe, h_ready, i * 8 + s - 1)
                for w in range(2):
                    o = bank[2 * w + s % 2][:]
                    for c in range(KC):
                        wh, wl = (w16[:, par, half, w * D + c * M:w * D + (c + 1) * M] for half in range(2))
                        pe.matmul(o, wh, x16[:, 0, c, tokens], start=(c == 0), stop=False)
                        pe.matmul(o, wh, x16[:, 1, c, tokens], start=False, stop=False)
                        ins = pe.matmul(o, wl, x16[:, 0, c, tokens], start=False, stop=(c == KC - 1))
                ins.then_inc(gu_done, 1)

            def down(i, s):
                pe.wait_ge(h_low, i * 8 + s + 1)
                wdh, wdl = (w16[:, s // 4, half, 2 * D:3 * D] for half in range(2))
                for t in range(TB):
                    o = bank[4 + 2 * (s % 2) + t // 2][:, (t % 2) * D:(t % 2 + 1) * D]
                    hh, hl = (h16[:, s % 2, half, t * P:(t + 1) * P] for half in range(2))
                    pe.matmul(o, hh, wdh, start=True, stop=False)
                    pe.matmul(o, hh, wdl, start=False, stop=False)
                    ins = pe.matmul(o, hl, wdh, start=False, stop=True)
                ins.then_inc(y_done, 1)

            pe.wait_ge(act_step, 2)
            gate_up(0, 0)
            gate_up(0, 1)

            def expert_pair(i, last):
                for s in range(8):
                    if s < 6:
                        gate_up(i, s + 2)
                    elif not last:
                        gate_up(i + 1, s - 6)
                    down(i, s)

            with pe.Fori(0, NE // 2 - 1) as i:
                expert_pair(i, False)
            expert_pair(NE // 2 - 1, True)

            def project(layer, t):
                if t == 0:
                    pe.wait_ge(oT_copied, ITEMS * (layer + 1))
                    pe.wait_ge(prT_low, 6 * ITEMS * (layer + 1))
                    pe.wait_ge(out_weights_loaded, 32 * (layer + 1))
                await_(pe, proj_read, T * layer + t - 1)
                for k in range(PAIRS):
                    ins = pe.matmul(bank[t % 2][:, 0:D], outT[:, k, t * P:(t + 1) * P], wo[:, k, :],
                                    start=(k == 0), stop=(k == PAIRS - 1))
                ins.then_inc(proj_done, 1)

            def turn_normed(layer, t):
                pe.wait_ge(xn_ready, T * layer + t + 1)
                await_(pe, xn_copied, T * layer + t - 1)
                for c in range(KC):
                    ins = pe.transpose(bank[2 + t % 2][:, c * P:(c + 1) * P], xn[:, t % 4, c * P:(c + 1) * P], ident[:])
                ins.then_inc(xn_turned, 1)

            def keys_values(layer, t):
                if t == 0:
                    pe.wait_ge(in_weights_loaded, 32 * (layer + 1))
                pe.wait_ge(xn_copied, T * layer + t + 1)
                for c in range(KC):
                    ins = pe.matmul(bank[4 + t // TB][:, (t % TB) * P:(t % TB + 1) * P], xT[:, c, t * P:(t + 1) * P],
                                    wkv[:, c, :], start=(c == 0), stop=(c == KC - 1))
                if t % TB == TB - 1:
                    ins.then_inc(kv_done, 1)

            def between(n):
                for t in STEPS:
                    if n and t < T:
                        project(n - 1, t)
                    if n < 3 and 2 <= t < T + 2:
                        turn_normed(n, t - 2)
                    if n < 3 and 3 <= t < T + 3:
                        keys_values(n, t - 3)
                if n < 3:
                    pe.wait_ge(ks_ready, B * n + 3)
                    pe.wait_ge(v_halved, B * n + 3)

            def turn_keys(n):
                await_(pe, proj_read, T * n)
                pe.wait_ge(xn_copied, T * (n + 1))
                for g in range(2):
                    pe.wait_ge(ks_ready, B * n + 2 * g + 2)
                    for half, src in enumerate((ks, kls)):
                        o16 = bank[2 * half + g][:].bitcast(F16)
                        rows_ = P if half == 0 else DH + 1
                        for j in range(8):
                            ins = pe.transpose(o16[0:rows_, j * P:(j + 1) * P],
                                               src[:, 8 * g + j, :, :].rearrange("p c d -> p (c d)")[:, 0:rows_], ident16[:])
                        ins.then_inc(kT_done, 1)
                pe.wait_ge(nks_ready, n + 1)
                pe.wait_ge(v_halved, B * (n + 1))
                for j in range(2):
                    ins = pe.transpose(bank[4][:].bitcast(F16)[:, j * P:(j + 1) * P], nks[:, j, :], ident16[:])
                ins.then_inc(kT_done, 1)
                pe.wait_ge(kT_by_act, 2 * (n + 1))
                pe.wait_ge(kT_by_dve, 3 * (n + 1))

            pe.wait_ge(y_added, T * NE)
            for layer in range(3):
                between(layer)

                def q_rows(it):
                    if not it:
                        return
                    await_(pe, null_ready, it.count(1, -1))
                    if isinstance(it.i, int) and it.ahead(-1) and not it.ahead(-2):
                        pe.wait_ge(q_copied, it.count(1, 0))
                    for t in range(TB):
                        for c in range(KC):
                            ins = pe.matmul(psQ[:, t * P:(t + 1) * P], xT[:, c, (TB * it.b + t) * P:(TB * it.b + t + 1) * P],
                                            wq[:, c, bass.ds(it.pair() * P, P)], start=(c == 0), stop=(c == KC - 1))
                    ins.then_inc(q_done, 1)

                def q_turn(it):
                    if not it:
                        return
                    pe.wait_ge(q_low, it.count(1, 1))
                    if it.ahead(-4):
                        pe.wait_ge(oT_copied, it.count(1, -3))
                    for h in range(2):
                        for t in range(TB):
                            ins = pe.transpose(psX16[:, (TB * h + t) * P:(TB * h + t + 1) * P],
                                               qs[:, t, h, :, :].rearrange("p c d -> p (c d)"), ident16[:])
                    ins.then_inc(qT_done, 1)

                def null_scores(it, after):
                    if not it:
                        return
                    pe.wait_ge(qB_copied, it.count(1, 1))
                    if after:
                        pe.wait_ge(q_copied, after.count(1, 1))
                    for t in range(TB):
                        for h in range(2):
                            o = 2 * (2 * t + h)
                            ins = pe.matmul(psQ[:, o:o + 2], qT[it.b % 2][:, h, t * P:(t + 1) * P], nkT[:],
                                            start=True, stop=True)
                    ins.then_inc(null_done, 1)

                def score(it, h, t):
                    if not it:
                        return
                    s = TB * h + t
                    await_(pe, masked, it.count(8, s - 2 if s >= 3 else (-1, 0, -2)[s]))
                    o, keys = psS[s % 3][:, 0:WIDTH[t]], slice(S * it.b, S * it.b + WIDTH[t])
                    pe.matmul(o, qT[it.b % 2][:, h, t * P:(t + 1) * P], kh[:, keys], start=True, stop=False)
                    pe.matmul(o, qB[it.b % 2][:, h, t * P:(t + 1) * P], kl[:, keys], start=False, stop=True
                              ).then_inc(score_done, 1)

                def turn(it, h, g):
                    if not it:
                        return
                    q = 3 * h + g
                    pe.wait_ge(exp_done, it.count(8, TB * h + GROUPS[g][-1][0] + 1))
                    await_(pe, prT_low, it.count(6, q - 1))
                    for j, (t, k) in enumerate(GROUPS[g]):
                        ins = pe.transpose(psT[q % 2][:, j * P:(j + 1) * P], pr[h][:, OFF[t] + k * P:OFF[t] + (k + 1) * P],
                                           ident[:])
                    ins.then_inc(prT_done, 1)

                def av(it, h):
                    if not it:
                        return
                    pe.wait_ge(prT_low, it.count(6, 3 * h + 3))
                    if h == 0:
                        await_(pe, o_ready, it.count(1, 0))
                    for t in range(TB):
                        o = psO[:, (2 * t + h) * DH:(2 * t + h + 1) * DH]
                        for k in range(t + 1):
                            j = BLOCKS.index((t, k))
                            block, values = slice(j * P, (j + 1) * P), TB * it.b + k
                            pe.matmul(o, prh[h][:, block], vh[:, values, :], start=(k == 0), stop=False)
                            pe.matmul(o, prh[h][:, block], vl[:, values, :], start=False, stop=False)
                            ins = pe.matmul(o, prl[h][:, block], vh[:, values, :], start=False, stop=(k == t))
                    ins.then_inc(av_done, 1)

                def o_turn(it):
                    if not it:
                        return
                    pe.wait_ge(o_ready, it.count(1, 1))
                    if it.ahead(3):
                        pe.wait_ge(qT_copied, it.count(1, 4))
                    else:
                        pe.wait_ge(oT_copied, it.count(1, 0))
                    for t in range(TB):
                        ins = pe.transpose(psX[:, t * P:(t + 1) * P], orow[:, t, :, :].rearrange("p h d -> p (h d)"), ident[:])
                    ins.then_inc(oT_done, 1)

                def body(before2, before, it, after, after2):
                    q_rows(after2)
                    turn(before, 1, 1)
                    score(it, 0, 3)
                    turn(before, 1, 2)
                    q_turn(after)
                    score(it, 1, 0)
                    score(it, 1, 1)
                    score(it, 1, 2)
                    av(before, 0)
                    score(it, 1, 3)
                    turn(it, 0, 0)
                    turn(it, 0, 1)
                    av(before, 1)
                    turn(it, 0, 2)
                    null_scores(after, after2)
                    score(after, 0, 0)
                    score(after, 0, 1)
                    o_turn(before2)
                    score(after, 0, 2)
                    turn(it, 1, 0)

                positions(pe, layer, body, turn_keys)

            between(3)

        @block.scalar
        def _(act):
            act.wait_ge(consts_ready, 1)

            def weights_high(i, par):
                act.wait_ge(expert_loaded[par], i * 48 + 48)
                nc.scalar.activation(w16[:, par, 0], wload[par], ACT.Copy, scale=WEIGHT_SCALE).then_inc(w_scaled, 1)
                act.wait_ge(w_scaled, i * 2 + par + 1)
                nc.scalar.activation(wload[par], wload[par], ACT.Copy, scale=WEIGHT_SCALE).then_inc(w_high, 1)

            for g in range(8):
                act.wait_ge(xT_done, g + 1)
                nc.scalar.copy(xT[:, 0, 2 * g * P:(2 * g + 2) * P], bank[2 * (g % 2)][:, 0:2 * P]).then_inc(xT_by_act, 1)
            for stage in range(2):
                for n in range(2):
                    act.wait_ge(stats_ready, 2 * stage + n + 1)
                    nc.scalar.activation(h1[n], h0[n], ACT.Silu).then_inc(mlp_h, 1)
                if stage == 0:
                    act.wait_ge(gate_max, 2)
                    nc.scalar.activation(sc, lg, ACT.Exp, scale=0.5).then_inc(gate_exp, 1)
                    act.wait_ge(xT_by_act, 8)
                    act.wait_ge(xT_by_dve, 8)
                    for b in range(B):
                        w = slice(b * S, b * S + S)
                        nc.scalar.copy(x16[:, 0, :, w], xT[:, :, w]).then_inc(x_high, 1)
                    weights_high(0, 0)
                for n in range(2):
                    act.wait_ge(mlp_turned, 2 * stage + n + 1)
                    for c in range(KC):
                        nc.scalar.copy(hTT[n][:, c, :], bank[4 * n + c][:]).then_inc((mlp_hT_first, mlp_hT)[c], 1)
            for n in range(2):
                act.wait_ge(mlp_done, 3 + n)
                nc.scalar.activation(brow[n][:, 0:S], bank[4 * n + 2][0:H, :], ACT.Identity, bias=b2s[n],
                                     scale=1 / LAYERS[1]["descale"]).then_inc(act_step, 1)
                act.wait_ge(act_step, n + 1)
                act.dma_start(bias_dram[n], brow[n].unsqueeze(1).to_broadcast([H, P, 640])).then_inc(bias_rows_stored, 16)

            def g_copy(i, s):
                act.wait_ge(gu_done, i * 8 + s + 1)
                nc.scalar.activation(gcopy[s % 2], bank[s % 2][:], ACT.Copy, scale=1 / WEIGHT_SCALE).then_inc(g_copied, 1)

            def hidden_high(i, s):
                act.wait_ge(h_ready, i * 8 + s + 1)
                nc.scalar.copy(h16[:, s % 2, 0], hT[s % 2]).then_inc(h_high, 1)

            def expert_pair(i, last):
                for s in range(8):
                    if s < 7:
                        g_copy(i, s + 1)
                    elif not last:
                        g_copy(i + 1, 0)
                    else:
                        act.wait_ge(y_done, 4 * NE - 2)
                    hidden_high(i, s)
                    if s == 1:
                        weights_high(i, 1)
                    if s == 5 and not last:
                        weights_high(i + 1, 0)

            g_copy(0, 0)
            with act.Fori(0, NE // 2 - 1) as i:
                expert_pair(i, False)
            expert_pair(NE // 2 - 1, True)

            def between(n):
                for t in STEPS:
                    b = keys_batch(t)
                    if LAYERS[n]["norm"] and b is not None:
                        act.wait_ge(kv_done, B * n + b + 1)
                        if b:
                            act.wait_ge(rsq_in, rsq("k", n, b - 1) + 1)
                        nc.scalar.activation(ksq, bank[4 + b][:].rearrange("p (t n) -> p t n", t=TB)[:, :, 0:DH],
                                             ACT.Square).then_inc(kv_squared, 1)
                    if 2 <= t < T + 2:
                        act.wait_ge(xn_turned, T * n + t - 1)
                        for c in range(KC):
                            ins = nc.scalar.activation(xT[:, c, (t - 2) * P:(t - 1) * P], bank[2 + t % 2][:, c * P:(c + 1) * P],
                                                       ACT.Copy, scale=gin[:, n, c:c + 1])
                            ins.then_inc((act_step, xn_copied)[c], 1)

            def turn_keys(n):
                for g in range(2):
                    act.wait_ge(kT_done, 5 * n + 2 * g + 1)
                    nc.scalar.copy(kh[:, g * 8 * P:(g + 1) * 8 * P], bank[g][:].bitcast(F16)).then_inc(kT_by_act, 1)

            act.wait_ge(small_loaded, N_SMALL)
            act.wait_ge(bias_rows_stored, 32)
            for layer in range(3):
                norm, negd = LAYERS[layer]["norm"], -LAYERS[layer]["descale"]
                between(layer)

                def q_copy(it):
                    if not it:
                        return
                    act.wait_ge(q_done, it.count(1, 1))
                    act.sem_inc(scalar_seen, 1)
                    if norm:
                        await_(act, q_normed, it.count(1, 0, 1))
                    else:
                        await_(act, q_low, it.count(1, 0))
                    act.sem_inc(scalar_seen, 1)
                    nc.scalar.activation((qraw if norm else qn)[:], psQ[:].rearrange("p (t h d) -> p t h d", t=TB, h=2),
                                         ACT.Copy, scale=1.0 if norm else RAW_SCALE).then_inc(q_copied, 1)

                def qT_copy(it):
                    if not it:
                        return
                    act.wait_ge(qT_done, it.count(1, 1))
                    nc.scalar.copy(qT[it.b % 2][:].rearrange("p h n -> p (h n)"), psX16).then_inc(qT_copied, 1)

                def exp(it, h, t):
                    if not it:
                        return
                    act.wait_ge(masked, it.count(8, TB * h + t + 1))
                    w = pr[h][:, OFF[t]:OFF[t] + WIDTH[t]]
                    nc.scalar.activation(w, w, ACT.Exp, bias=nmax[it.b % 2][:, t, h:h + 1], scale=-1.0,
                                         accum_out=rsum[it.b % 2][:, t, h:h + 1]).then_inc(exp_done, 1)

                def prT_copy(it, h, g):
                    if not it:
                        return
                    act.wait_ge(prT_done, it.count(6, 3 * h + g + 1))
                    n = len(GROUPS[g]) * P
                    nc.scalar.activation(prh[h][:, 4 * g * P:4 * g * P + n], psT[(3 * h + g) % 2][:, 0:n], ACT.Copy,
                                         scale=PROB_SCALE).then_inc(prT_high, 1)

                def null_weight(it):
                    if not it:
                        return
                    act.wait_ge(null_gap, it.count(1, 1))
                    await_(act, den_step, it.count(2, -1))
                    nc.scalar.activation(pn[:, 1], pn[:, 0], ACT.Exp).then_inc(null_exp, 1)

                def oT_copy(it):
                    if not it:
                        return
                    act.wait_ge(oT_done, it.count(1, 1))
                    act.sem_inc(scalar_seen, 1)
                    nc.scalar.activation(over[:, bass.ds(it.pair() * (T * P) + it.b * S, S)], psX[:], ACT.Identity,
                                         bias=nvT[:], scale=1 / (PROB_SCALE * VALUE_SCALE)).then_inc(oT_copied, 1)

                def body(before2, before, it, after, after2):
                    exp(before, 1, 3)
                    exp(it, 0, 0)
                    q_copy(after2)
                    prT_copy(before, 1, 1)
                    prT_copy(before, 1, 2)
                    qT_copy(after)
                    exp(it, 0, 1)
                    exp(it, 0, 2)
                    exp(it, 0, 3)
                    prT_copy(it, 0, 0)
                    prT_copy(it, 0, 1)
                    exp(it, 1, 0)
                    exp(it, 1, 1)
                    exp(it, 1, 2)
                    prT_copy(it, 0, 2)
                    null_weight(it)
                    oT_copy(before2)
                    prT_copy(it, 1, 0)

                positions(act, layer, body, turn_keys)

        @block.vector
        def _(dve):
            vec = nc.vector
            steps = [0]

            def link(ins):
                steps[0] += 1
                ins.then_inc(dve_step, 1)
                dve.wait_ge(dve_step, steps[0])

            def network_stats(n, stage):
                tiles = range(TB * n, TB * n + TB)
                for t in tiles:
                    link(vec.bn_stats(stats[:, t, :], h0[n][:, t % TB, :]))
                for t in tiles:
                    vec.bn_aggr(mv[:, t, :], stats[:, t, :]).then_inc(rsq_in if t == tiles[-1] else mlp_step, 1)

            def network_norm(n, stage):
                dve.wait_ge(rsq_out, rsq("mlp", n, stage) + 1)
                for t in range(TB):
                    r = TB * n + t
                    link(vec.tensor_scalar(h0[n][:, t, :], h0[n][:, t, :], mv[:, r, 0:1], rstd[:, r:r + 1],
                                           ALU.subtract, ALU.mult))
                for t in range(TB):
                    vec.tensor_tensor(h0[n][:, t, :], h0[n][:, t, :], rows[n][:, 2 + 2 * stage, :], ALU.mult
                                      ).then_inc(stats_ready if t == TB - 1 else mlp_step, 1)

            dve.wait_ge(consts_ready, 1)
            for n in range(2):
                if n == 1:
                    dve.wait_ge(gate_loaded, 16 * 4)
                    vec.tensor_copy(condb, condT.unsqueeze(2).to_broadcast([G, B, P])).then_inc(gate_max, 1)
                    for g in range(8):
                        dve.wait_ge(xT_done, g + 1)
                        vec.tensor_copy(xT[:, 1, 2 * g * P:(2 * g + 2) * P], bank[2 * (g % 2) + 1][:, 0:2 * P]).then_inc(xT_by_dve, 1)
                dve.wait_ge(mlp_loaded[n], N_MLP_LOADS)
                link(vec.tensor_scalar(b2s[n], b2s[n], 1 / LAYERS[1]["descale"], None, ALU.mult))
                for t in range(TB):
                    link(vec.scalar_tensor_tensor(h0[n][:, t, :], rows[n][:, 0, :], pos[:, t:t + 1], rows[n][:, 1, :],
                                                  ALU.mult, ALU.add))
                network_stats(n, 0)
            for n in range(2):
                network_norm(n, 0)
            dve.wait_ge(gate_done, 1)
            logits = bank[7][:, 0:T * E].rearrange("p (t e) -> p t e", t=T)
            link(vec.tensor_reduce(r1[:, 0, :], logits, AX_X, ALU.max))
            vec.tensor_tensor(lg, logits, r1[:, 0, :].unsqueeze(2).to_broadcast([P, T, E]), ALU.subtract).then_inc(gate_max, 1)
            dve.wait_ge(gate_exp, 1)
            link(vec.tensor_reduce(r1[:, 1, :], sc, AX_X, ALU.add))
            link(vec.reciprocal(r1[:, 2, :], r1[:, 1, :]))
            link(vec.tensor_tensor(sc, sc, r1[:, 2, :].unsqueeze(2).to_broadcast([P, T, E]), ALU.mult))
            for t in range(T):
                ins = vec.max(top[:, t, :], sc[:, t, :])
                if t < T - 1:
                    steps[0] += 1
                    ins.then_inc(dve_step, 1)
            link(ins)
            for t in range(T):
                link(vec.max_index(topi[:, t, :], top[:, t, :], sc[:, t, :]))
            for n in range(2):
                dve.wait_ge(mlp_done, n + 1)
                for t in range(TB):
                    link(vec.tensor_tensor(h0[n][:, t, :], bank[4 * n + 2 + t // 2][:, (t % 2) * D:(t % 2 + 1) * D],
                                           rows[n][:, 3, :], ALU.add))
                network_stats(n, 1)
            for n in range(2):
                network_norm(n, 1)

            link(vec.tensor_copy(idx, topi[:, :, 0:2]))
            link(vec.tensor_tensor(r1[:, 3, :], top[:, :, 0], top[:, :, 1], ALU.add))
            link(vec.tensor_scalar(r1[:, 4, :], r1[:, 3, :], 1e-20, None, ALU.add))
            link(vec.reciprocal(r1[:, 5, :], r1[:, 4, :]))
            cwt = cw[:, 0:E, :].rearrange("p e t -> p t e")
            for j in range(2):
                link(vec.tensor_tensor(r1[:, 6 + j, :], top[:, :, j], r1[:, 5, :], ALU.mult))
                link(vec.tensor_tensor(eq, iota8.unsqueeze(1).to_broadcast([P, T, E]),
                                       idx[:, :, j].unsqueeze(2).to_broadcast([P, T, E]), ALU.is_equal))
                w = r1[:, 6 + j, :].unsqueeze(2).to_broadcast([P, T, E])
                if j == 0:
                    link(vec.tensor_tensor(cwt, eq, w, ALU.mult))
                else:
                    link(vec.tensor_tensor(eq, eq, w, ALU.mult))
                    link(vec.tensor_tensor(cwt, cwt, eq, ALU.add))
            link(vec.memset(cw[:, E:NE, :], 1.0))
            link(vec.tensor_scalar(over[:, 5968:6128], over[:, 5968:6128], 1 / WEIGHT_SCALE, None, ALU.mult))
            vec.tensor_copy(ce[0], cw[:, 0, :]).then_inc(ce_ready, 1)

            def hidden(i, s):
                dve.wait_ge(g_copied, i * 8 + s + 1)
                vec.scalar_tensor_tensor(gleaky[s % 2], gcopy[s % 2], LEAKY, gcopy[s % 2], ALU.mult, ALU.max
                                         ).then_inc(g_leaky, 1)
                dve.wait_ge(g_leaky, i * 8 + s + 1)
                vec.scalar_tensor_tensor(hT[s % 2], bank[2 + s % 2][:], 1 / WEIGHT_SCALE, gleaky[s % 2], ALU.mult, ALU.mult
                                         ).then_inc(h_ready, 1)

            def add_out(i, s):
                dve.wait_ge(y_done, i * 8 + s + 1)
                for t in range(TB):
                    tile = TB * (s % 4) + t
                    vec.scalar_tensor_tensor(x[:, tile, :], bank[4 + 2 * (s % 2) + t // 2][:, (t % 2) * D:(t % 2 + 1) * D],
                                             ce[s // 4][:, tile:tile + 1], x[:, tile, :], ALU.mult, ALU.add
                                             ).then_inc(y_added, 1)

            def expert_pair(i, last):
                for s in range(8):
                    if s == 0:
                        vec.tensor_copy(ce[1], cw_flat[:, bass.ds(i * 2 * T + T, T)]).then_inc(ce_ready, 1)
                    if s == 4:
                        dve.wait_ge(ce_ready, i * 2 + 2)
                    if s == 0:
                        dve.wait_ge(ce_ready, i * 2 + 1)
                    if s == 4:
                        dve.wait_ge(y_added, i * 32 + 16)
                        if not last:
                            vec.tensor_copy(ce[0], cw_flat[:, bass.ds(i * 2 * T + 2 * T, T)]).then_inc(ce_ready, 1)
                    add_out(i, s)
                    if s < 6:
                        hidden(i, s + 2)
                    elif not last:
                        hidden(i + 1, s - 6)
                dve.wait_ge(y_added, i * 32 + 32)

            dve.wait_ge(small_loaded, N_SMALL)
            for j in range(2):
                link(vec.tensor_copy(maskv[:, j, :], mask8[:, j, :]))
                link(vec.tensor_scalar(maskv[:, j, :], maskv[:, j, :], 1.0, MASK, ALU.subtract, ALU.mult))
                link(vec.tensor_tensor(kscale[:, j + 1, :], kscale[:, j + 1, :], qscale[:, j, :], ALU.mult))
                link(vec.tensor_scalar(kscale[:, j + 1, :], kscale[:, j + 1, :], NORM_SCALE, None, ALU.mult))
            cw_flat = over[:, 5968:6128]
            hidden(0, 0)
            hidden(0, 1)
            with dve.Fori(0, NE // 2 - 1) as i:
                expert_pair(i, False)
            expert_pair(NE // 2 - 1, True)

            def output_stats(layer, t):
                y = bank[t % 2][:, 0:D]
                if t == 0:
                    dve.wait_ge(out_weights_loaded, 32 * (layer + 1))
                dve.wait_ge(proj_done, T * layer + t + 1)
                link(vec.bn_stats(stats[:, t, :], y))
                vec.bn_aggr(mv[:, t, :], stats[:, t, :]).then_inc(rsq_in, 1)
                dve.wait_ge(rsq_in, rsq("out", layer, t) + 1)
                vec.scalar_tensor_tensor(ytmp[:, t % 2, :], y, mv[:, t, 0:1], gout[:], ALU.subtract, ALU.mult
                                         ).then_inc(proj_read, 1)

            def add_output(layer, t):
                dve.wait_ge(proj_read, T * layer + t + 1)
                dve.wait_ge(rsq_out, rsq("out", layer, t) + 1)
                vec.scalar_tensor_tensor(x[:, t, :], ytmp[:, t % 2, :], rstd[:, t:t + 1], x[:, t, :], ALU.mult, ALU.add
                                         ).then_inc(proj_added, 1)

            def stream_stats(layer, t):
                await_(dve, proj_added, T * (layer - 1) + t + 1)
                link(vec.bn_stats(stats[:, t, :], x[:, t, :]))
                vec.bn_aggr(mv[:, t, :], stats[:, t, :]).then_inc(rsq_in, 1)

            def norm_tile(layer, t):
                dve.wait_ge(rsq_out, rsq("ln", layer, t) + 1)
                await_(dve, xn_turned, T * layer + t - 3)
                vec.tensor_scalar(xn[:, t % 4, :], x[:, t, :], mv[:, t, 0:1], rstd[:, t:t + 1], ALU.subtract, ALU.mult
                                  ).then_inc(xn_ready, 1)

            def null_key_norm():
                link(vec.tensor_tensor(nkn, nk[:], nk[:], ALU.mult))
                vec.tensor_reduce(nss[:, 0:1], nkn, AX_X, ALU.add).then_inc(rsq_in, 1)

            def null_key(layer):
                if LAYERS[layer]["norm"]:
                    dve.wait_ge(rsq_out, rsq("nk", layer) + 1)
                    link(vec.tensor_scalar(nkn, nk[:], nss[:, 2:3], None, ALU.mult))
                else:
                    link(vec.tensor_copy(nkn, nk[:]))
                link(vec.tensor_tensor(nkn2, nkn, kscale[:, layer, :], ALU.mult))
                link(vec.tensor_copy(nks[:, 0, :].rearrange("p (c d) -> p c d", c=2), nkn2.unsqueeze(1).to_broadcast([P, 2, DH])))
                link(vec.tensor_tensor(nks[:, 1, 0:DH], nkn2, nks[:, 0, 0:DH], ALU.subtract))
                vec.tensor_copy(nks[:, 1, DH:P], nks[:, 1, 0:DH]).then_inc(nks_ready, 1)

            def values(layer, b):
                dve.wait_ge(kv_done, B * layer + b + 1)
                w = slice(TB * b, TB * b + TB)
                kv = bank[4 + b][:].rearrange("p (t c d) -> p t c d", t=TB, c=2)
                if LAYERS[layer]["norm"]:
                    dve.wait_ge(kv_squared, B * (layer - 1) + b + 1)
                    vec.tensor_reduce(kss[:, 0, w], ksq, AX_X, ALU.add).then_inc(rsq_in, 1)
                link(vec.tensor_tensor(vd, kv[:, :, 1, :], nv[:].unsqueeze(1).to_broadcast([P, TB, DH]), ALU.subtract))
                link(vec.tensor_scalar(vh[:, w, :], vd, VALUE_SCALE, None, ALU.mult))
                vec.scalar_tensor_tensor(vl[:, w, :], vd, VALUE_SCALE, vh[:, w, :], ALU.mult, ALU.subtract
                                         ).then_inc(v_halved, 1)

            def keys(layer, b):
                w = slice(TB * b, TB * b + TB)
                k = bank[4 + b][:].rearrange("p (t c d) -> p t c d", t=TB, c=2)[:, :, 0, :]
                if LAYERS[layer]["norm"]:
                    dve.wait_ge(rsq_out, rsq("k", layer, b) + 1)
                    link(vec.tensor_tensor(kn, k, kss[:, 2, w].unsqueeze(2).to_broadcast([P, TB, DH]), ALU.mult))
                    k = kn
                link(vec.tensor_tensor(kn2, k, kscale[:, layer, :].unsqueeze(1).to_broadcast([P, TB, DH]), ALU.mult))
                for c in range(2):
                    link(vec.tensor_copy(ks[:, w, c, :], kn2))
                link(vec.tensor_copy(kls[:, w, 1, 0:1], maskv[:, 0 if layer == 0 else 1, w].unsqueeze(2)))
                vec.tensor_tensor(kls[:, w, 0, :], kn2, ks[:, w, 0, :], ALU.subtract).then_inc(ks_ready, 1)

            def between(n):
                for t in STEPS:
                    if n < 3 and 2 <= t < T + 2:
                        norm_tile(n, t - 2)
                    if n and 1 <= t <= T:
                        add_output(n - 1, t - 1)
                    if n < 3 and stats_tile(n, t) is not None:
                        stream_stats(n, stats_tile(n, t))
                    if n and t < T:
                        output_stats(n - 1, t)
                    if n == 3:
                        continue
                    if t == 1 and LAYERS[n]["norm"]:
                        null_key_norm()
                    if t == 3:
                        null_key(n)
                    if keys_batch(t) is not None:
                        values(n, keys_batch(t))
                    if keys_batch(t - 1) is not None:
                        keys(n, keys_batch(t - 1))

            def turn_keys(n):
                for g in range(2):
                    dve.wait_ge(kT_done, 5 * n + 2 * g + 2)
                    vec.tensor_copy(kl[:, g * 8 * P:(g + 1) * 8 * P], bank[2 + g][:].bitcast(F16)[0:DH + 1, :]).then_inc(kT_by_dve, 1)
                dve.wait_ge(kT_done, 5 * n + 5)
                vec.tensor_copy(nkT[:], bank[4][:].bitcast(F16)[:, 0:2 * P].rearrange("p (c n) -> p c n", c=2)[:, :, 0]
                                ).then_inc(kT_by_dve, 1)

            dve.wait_ge(y_added, T * NE)
            for layer in range(3):
                norm, negd = LAYERS[layer]["norm"], -LAYERS[layer]["descale"]
                between(layer)

                def q_sum(it):
                    if not it or not norm:
                        return
                    dve.wait_ge(q_squared, it.count(1, 1, 1))
                    vec.tensor_reduce(qss[:, 0], qsq[:], AX_X, ALU.add).then_inc(q_summed, 1)

                def q_high_half(it):
                    if not it:
                        return
                    if norm:
                        dve.wait_ge(q_normed, it.count(1, 1, 1))
                    else:
                        dve.wait_ge(q_copied, it.count(1, 1))
                    dve.sem_inc(vector_seen, 1)
                    await_(dve, qT_done, it.count(1, 0))
                    dve.sem_inc(vector_seen, 1)
                    vec.tensor_copy(qs[:, :, :, 0, :], qn[:]).then_inc(q_high, 1)

                def null_score(it):
                    if not it:
                        return
                    dve.wait_ge(null_done, it.count(1, 1))
                    vec.tensor_reduce(sn0[:, 0], psQ[:, 0:4 * TB].rearrange("p (t h c) -> p t h c", t=TB, h=2), AX_X, ALU.add
                                      ).then_inc(null_ready, 1)
                    dve.wait_ge(null_ready, it.count(1, 1))
                    vec.tensor_scalar(sn0[:, 1], sn0[:, 0], negd, None, ALU.mult).then_inc(null_scaled, 1)
                    dve.wait_ge(null_scaled, it.count(2, 1))
                    vec.tensor_tensor(sn[it.b % 2][:], sn0[:, 1],
                                      nullb_flat[:, bass.ds(it.pair() * 2 + H * layer, 2)].unsqueeze(1).to_broadcast([P, TB, 2]),
                                      ALU.subtract).then_inc(null_scaled, 1)

                def mask_tile(it, h, t):
                    if not it:
                        return
                    if it.b == 0 and h == 0 and t == 0:
                        if layer == 0:
                            dve.wait_ge(bias_ready, it.i * 16 + 8 * it.par + 8)
                        else:
                            dve.wait_ge(bias_loaded[it.par], bias_count(layer, it.i))
                        dve.sem_inc(vector_seen, 1)
                    if h == 1 and t != 1:
                        await_(dve, prT_done, it.count(6, {0: -2, 2: -1, 3: 0}[t]))
                        dve.sem_inc(vector_seen, 1)
                    if h == 0 and t == 0:
                        dve.wait_ge(null_scaled, it.count(2, 2))
                        dve.sem_inc(vector_seen, 1)
                    dve.wait_ge(score_done, it.count(8, TB * h + t + 1))
                    dve.sem_inc(vector_seen, 1)
                    n = WIDTH[t]
                    bt = bias[it.par][:, h, OFF[t]:OFF[t] + n] if layer == 0 else bias[it.par][:, h, S - n:S]
                    vec.tensor_tensor_reduce(pr[h][:, OFF[t]:OFF[t] + n], psS[(TB * h + t) % 3][:, 0:n], bt, negd,
                                             sn[it.b % 2][:, t, h:h + 1], ALU.add, ALU.min,
                                             nmax[it.b % 2][:, t, h:h + 1]).then_inc(masked, 1)

                def low_half(it, h, g):
                    if not it:
                        return
                    dve.wait_ge(prT_high, it.count(6, 3 * h + g + 1))
                    n = len(GROUPS[g]) * P
                    w = slice(4 * g * P, 4 * g * P + n)
                    vec.scalar_tensor_tensor(prl[h][:, w], psT[(3 * h + g) % 2][:, 0:n], PROB_SCALE, prh[h][:, w],
                                             ALU.mult, ALU.subtract).then_inc(prT_low, 1)

                def null_part(it):
                    if not it:
                        return
                    await_(dve, null_exp, it.count(1, 0))
                    dve.wait_ge(masked, it.count(8, 8))
                    vec.tensor_tensor(pn[:, 0], nmax[it.b % 2][:], sn[it.b % 2][:], ALU.subtract).then_inc(null_gap, 1)

                def denominators(it):
                    if not it:
                        return
                    dve.wait_ge(null_exp, it.count(1, 1))
                    dve.wait_ge(exp_done, it.count(8, 8))
                    vec.tensor_tensor(pn[:, 2], rsum[it.b % 2][:], pn[:, 1], ALU.add).then_inc(den_step, 1)
                    dve.wait_ge(den_step, it.count(2, 1))
                    vec.reciprocal(pn[:, 3], pn[:, 2]).then_inc(den_step, 1)

                def o_rows(it):
                    if not it:
                        return
                    dve.wait_ge(av_done, it.count(2, 2))
                    await_(dve, oT_done, it.count(1, 0))
                    dve.wait_ge(den_step, it.count(2, 2))
                    vec.tensor_tensor(orow[:], psO[:].rearrange("p (t h d) -> p t h d", t=TB, h=2),
                                      pn[:, 3].unsqueeze(3).to_broadcast([P, TB, 2, DH]), ALU.mult).then_inc(o_ready, 1)

                def body(before2, before, it, after, after2):
                    q_high_half(after)
                    mask_tile(it, 0, 1)
                    mask_tile(it, 0, 2)
                    low_half(before, 1, 0)
                    denominators(before)
                    mask_tile(it, 0, 3)
                    mask_tile(it, 1, 0)
                    mask_tile(it, 1, 1)
                    low_half(before, 1, 1)
                    low_half(before, 1, 2)
                    q_sum(after2)
                    mask_tile(it, 1, 2)
                    low_half(it, 0, 0)
                    mask_tile(it, 1, 3)
                    low_half(it, 0, 1)
                    null_part(it)
                    null_score(after)
                    mask_tile(after, 0, 0)
                    low_half(it, 0, 2)
                    o_rows(before)

                positions(dve, layer, body, turn_keys)

            between(3)


_ATTN = ("null_attn_bias", "Wq", "Wkv", "g_out")
_NORMED = ("g_norm", "q_scale", "k_scale", "w0", "b0", "g0", "w1", "b1", "g1", "w2", "b2", "Wout")
_INS = (["x", "cond_64", "fside_16xSxS_0", "mask_BxS_bk0", "mask_BxS_bf1", "L0_cond_wt", "L0_cond_wg"]
        + [f"L1_cond_{n}" for n in (*_ATTN, "g_in", "Wo")]
        + [f"L{k}_cond_{n}" for k in (2, 3) for n in (*_ATTN, *_NORMED)])


def kernel(**inputs):
    import numpy as _np
    import concourse.bacc as _bacc
    from concourse import mybir as _mybir
    from concourse.bass_utils import run_bass_kernel_spmd as _run

    nc = _bacc.Bacc("TRN2", target_bir_lowering=False, num_devices=1)
    host = {n: _np.ascontiguousarray(inputs[n]) for n in _INS}

    def experts(own, shared, axis):
        halves = _np.split(_np.asarray(inputs[shared]), 2, axis=axis)
        return _np.concatenate([_np.asarray(inputs[own]), _np.stack(halves)])

    host["gate"] = experts("L0_cond_w_gate", "L0_cond_sw_gate", 1)
    host["up"] = experts("L0_cond_w_up", "L0_cond_sw_up", 1)
    host["down"] = experts("L0_cond_w_down", "L0_cond_sw_down", 0)
    arrays, args = {}, {}
    for name, value in host.items():
        arrays[f"in_{name}_dram"] = value
        args[name] = nc.dram_tensor(f"in_{name}_dram", value.shape, _mybir.dt.from_np(value.dtype), kind="ExternalInput").ap()
    out = nc.dram_tensor("out_0_dram", (4, 512, 256), _mybir.dt.float32, kind="ExternalOutput").ap()
    build(nc, args, out)
    r = _run(nc, [arrays], core_ids=[0])
    return r.results[0]["out_0_dram"]
```
